# Optimizing a Trainium2 kernel written in Bass

```python
import numpy as np
import jax
import jax.numpy as jnp

def _softmax(x, axis=-1):
    return jax.nn.softmax(x, axis=axis)

def _gelu(x):
    return jax.nn.gelu(x, approximate=True)

def _silu(x):
    return jax.nn.silu(x)

def _sigmoid(x):
    return jax.nn.sigmoid(x)

def _layernorm(x, axis=-1, eps=1e-05):
    m = jnp.mean(x, axis=axis, keepdims=True)
    v = jnp.var(x, axis=axis, keepdims=True)
    return (x - m) / jnp.sqrt(v + eps)

def _scatter_add(tgt, idx, src, axis=0):
    return tgt.at[idx].add(src)

def _segment_sum(src, seg, n):
    return jax.ops.segment_sum(src, seg, n)
kernel_name = 'mk_audio_tower_d2_tok_audfeat1024_r4_4b438e'

def setup_inputs(seed: int=0):
    np.random.seed(seed)
    _w = jnp.asarray

    def _rec_inputs():
        import jax
        import jax.numpy as jnp
        _rk = jax.random.key(seed)
        x = -0.0002364 + 0.999977 * jax.random.normal(jax.random.fold_in(_rk, 1), (64, 202, 128), jnp.float32)
        return x
    x = _rec_inputs()

    def _L0_tok_setup():
        import jax, jax.numpy as jnp
        import numpy as np
        PATCH_SIZE = 16
        STRIDE = 8
        IN_DIM = 128
        D_MODEL = 256
        MAX_POS = 100
        key = jax.random.key(seed)
        k1, k2, k3, k4 = jax.random.split(key, 4)
        B, L, D = (64, 202, IN_DIM)
        x = jax.random.normal(k1, (B, L, D), dtype=jnp.float32)
        fan_in = IN_DIM * PATCH_SIZE
        bound = 1.0 / np.sqrt(fan_in)
        W = jax.random.uniform(k2, (fan_in, D_MODEL), dtype=jnp.float32, minval=-bound, maxval=bound)
        b = jax.random.uniform(k3, (D_MODEL,), dtype=jnp.float32, minval=-bound, maxval=bound)
        pos_embed = jax.random.normal(k4, (1, MAX_POS, D_MODEL), dtype=jnp.float32) * 0.02
        return {'x': x, 'W': W, 'b': b, 'pos_embed': pos_embed}
    _L0_tok_all = _L0_tok_setup()
    _L0_tok_in = {k: v for k, v in _L0_tok_all.items() if k in ('W', 'b', 'pos_embed')}
    del _L0_tok_all

    def _L0_attn_setup():
        import jax, jax.numpy as jnp
        import numpy as np
        DIM = 256
        SQRT_DIM = float(np.sqrt(DIM))
        key = jax.random.key(seed)
        inputs = jax.random.normal(key, (1024, 4, DIM), dtype=jnp.float32)
        return {'inputs': inputs}
    _L0_attn_all = _L0_attn_setup()
    _L0_attn_in = {k: v for k, v in _L0_attn_all.items() if k in ()}
    del _L0_attn_all

    def _L0_ffn_setup():
        import jax, jax.numpy as jnp
        import numpy as np
        DIM = 256
        DEPTH = 7
        PAR = 8
        N_NODES = 2 ** (DEPTH + 1) - 1
        WIDTH = PAR * N_NODES
        key = jax.random.key(seed)
        k1, k2, k3, k4 = jax.random.split(key, 4)
        init_k = float(np.sqrt(1.0 / DIM))
        init_k2 = float(np.sqrt(1.0 / ((DEPTH + 1) * PAR)))
        oldx = jax.random.normal(k1, (4, 512, DIM), dtype=jnp.float32)
        W_in = jax.random.uniform(k2, (WIDTH, DIM), jnp.float32, -init_k, init_k)
        b_in = jax.random.uniform(k3, (WIDTH,), jnp.float32, -init_k, init_k)
        W_out = jax.random.uniform(k4, (DIM, WIDTH), jnp.float32, -init_k2, init_k2)
        return {'oldx': oldx, 'W_in': W_in, 'b_in': b_in, 'W_out': W_out}
    _L0_ffn_all = _L0_ffn_setup()
    _L0_ffn_in = {k: v for k, v in _L0_ffn_all.items() if k in ('W_in', 'b_in', 'W_out')}
    del _L0_ffn_all

    def _L1_attn_setup():
        import jax, jax.numpy as jnp
        import numpy as np
        N_HEADS = 16
        LOCAL_WINDOW = 128
        ROPE_BASE = 10000.0

        def _rotate_half(x):
            x1 = x[..., 0::2]
            x2 = x[..., 1::2]
            return jnp.stack((-x2, x1), axis=-1).reshape(x.shape)

        def _rope_cache(T, hd, dtype):
            half = hd // 2
            inv_freq = 1.0 / ROPE_BASE ** (jnp.arange(half, dtype=dtype) / half)
            t = jnp.arange(T, dtype=dtype)
            freqs = t[:, None] * inv_freq[None, :]
            cos = jnp.repeat(jnp.cos(freqs), 2, axis=-1)
            sin = jnp.repeat(jnp.sin(freqs), 2, axis=-1)
            return (cos, sin)
        key = jax.random.key(seed)
        k1, k2, k3, k4 = jax.random.split(key, 4)
        B, T, C = (2, 512, 256)
        x = jax.random.normal(k1, (B, T, C), dtype=jnp.float32)
        Wqkv = jax.random.normal(k2, (3 * C, C), dtype=jnp.float32) * 0.02
        Wproj = jax.random.normal(k3, (C, C), dtype=jnp.float32) * 0.02
        bproj = jax.random.normal(k4, (C,), dtype=jnp.float32) * 0.02
        return {'x': x, 'Wqkv': Wqkv, 'Wproj': Wproj, 'bproj': bproj}
    _L1_attn_all = _L1_attn_setup()
    _L1_attn_in = {k: v for k, v in _L1_attn_all.items() if k in ('Wqkv', 'Wproj', 'bproj')}
    del _L1_attn_all

    def _L1_ffn_setup():
        import jax, jax.numpy as jnp
        import numpy as np
        D = 256
        HQ = 16
        HKV = 4
        G = HQ // HKV
        K = 64
        V = 64
        E = 8
        TOPK = 2
        HID = 512
        CAP_FRAC = 0.125
        EPS = 1e-06

        def _rmsnorm(x, g):
            return x * jax.lax.rsqrt(jnp.mean(x * x, axis=-1, keepdims=True) + EPS) * g

        def _rotary_tables(t, dim):
            thetas = 10000.0 ** (-np.arange(0, dim, 2, dtype=np.float32) / dim)
            ticks = np.outer(np.arange(t, dtype=np.float32), thetas)
            ticks = np.tile(ticks, (1, 2))[None, :, None, :]
            return (jnp.asarray(np.cos(ticks)), jnp.asarray(np.sin(ticks)))

        def _neg_half(x):
            x1, x2 = jnp.split(x, 2, axis=-1)
            return jnp.concatenate([-x2, x1], axis=-1)

        def _attention(x, wq, wk, wv, wo):
            b, t, _ = x.shape
            q = (x @ wq).reshape(b, t, HQ, K)
            k = (x @ wk).reshape(b, t, HKV, K)
            v = (x @ wv).reshape(b, t, HKV, V)
            cos, sin = _rotary_tables(t, K)
            q = q * cos + _neg_half(q) * sin
            k = k * cos + _neg_half(k) * sin
            qg = q.reshape(b, t, G, HKV, K)
            scores = jnp.einsum('btghk,bThk->bghtT', qg, k)
            mask = jnp.tril(jnp.ones((t, t), bool))
            scores = jnp.where(mask, scores, -jnp.inf) / np.float32(np.sqrt(K))
            p = jax.nn.softmax(scores, axis=-1)
            out = jnp.einsum('bghtT,bThv->btghv', p, v).reshape(b, t, HQ * V)
            return out @ wo

        def _moe(x, router_w, router_b, w1, w2, w3):
            b, t, d = x.shape
            n = b * t
            xf = x.reshape(n, d)
            logits = xf @ router_w + router_b
            vals, idx = jax.lax.top_k(logits, TOPK)
            scores = jax.nn.softmax(vals, axis=-1)
            cap = int(np.floor(n * CAP_FRAC))
            oh = jax.nn.one_hot(idx, E, dtype=jnp.float32)
            pos = jnp.cumsum(jnp.cumsum(oh, axis=0), axis=1).astype(jnp.int32)
            emask = oh * (pos < cap)
            tmask = jnp.sum(emask, axis=-1)
            assign = jnp.einsum('tke,e->tk', emask, jnp.arange(E, dtype=jnp.float32)).astype(jnp.int32)
            m = jnp.max(assign, axis=-1)

            def ff(w1e, w2e, w3e):
                h = jax.nn.gelu(xf @ w2e * (xf @ w1e), approximate=False)
                return h @ w3e
            y_all = jax.vmap(ff)(w1, w2, w3)
            y = y_all[m, jnp.arange(n)]
            slot = jnp.where(tmask[..., None] > 0, y[:, None, :], xf[:, None, :])
            out = jnp.einsum('tkD,tk->tD', slot, scores)
            return out.reshape(b, t, d)
        key = jax.random.key(seed)
        ks = jax.random.split(key, 10)
        w = lambda k, shape: jax.random.normal(k, shape, jnp.float32) * 0.02
        return {'x': jax.random.normal(ks[0], (4, 128, D), jnp.float32), 'g1': jnp.ones((D,), jnp.float32), 'g2': jnp.ones((D,), jnp.float32), 'wq': w(ks[1], (D, HQ * K)), 'wk': w(ks[2], (D, HKV * K)), 'wv': w(ks[3], (D, HKV * V)), 'wo': w(ks[4], (HQ * V, D)), 'router_w': w(ks[5], (D, E)), 'router_b': jnp.zeros((E,), jnp.float32), 'w1': w(ks[6], (E, D, HID)), 'w2': w(ks[7], (E, D, HID)), 'w3': w(ks[8], (E, HID, D))}
    _L1_ffn_all = _L1_ffn_setup()
    _L1_ffn_in = {k: v for k, v in _L1_ffn_all.items() if k in ('g1', 'g2', 'wq', 'wk', 'wv', 'wo', 'router_w', 'router_b', 'w1', 'w2', 'w3')}
    del _L1_ffn_all
    return {'x': x, 'L0_tok_W': _L0_tok_in['W'], 'L0_tok_b': _L0_tok_in['b'], 'L0_tok_pos_embed': _L0_tok_in['pos_embed'], 'L0_ffn_W_in': _L0_ffn_in['W_in'], 'L0_ffn_b_in': _L0_ffn_in['b_in'], 'L0_ffn_W_out': _L0_ffn_in['W_out'], 'L1_attn_Wqkv': _L1_attn_in['Wqkv'], 'L1_attn_Wproj': _L1_attn_in['Wproj'], 'L1_attn_bproj': _L1_attn_in['bproj'], 'L1_ffn_g1': _L1_ffn_in['g1'], 'L1_ffn_g2': _L1_ffn_in['g2'], 'L1_ffn_wq': _L1_ffn_in['wq'], 'L1_ffn_wk': _L1_ffn_in['wk'], 'L1_ffn_wv': _L1_ffn_in['wv'], 'L1_ffn_wo': _L1_ffn_in['wo'], 'L1_ffn_router_w': _L1_ffn_in['router_w'], 'L1_ffn_router_b': _L1_ffn_in['router_b'], 'L1_ffn_w1': _L1_ffn_in['w1'], 'L1_ffn_w2': _L1_ffn_in['w2'], 'L1_ffn_w3': _L1_ffn_in['w3']}

def reference(x, L0_tok_W, L0_tok_b, L0_tok_pos_embed, L0_ffn_W_in, L0_ffn_b_in, L0_ffn_W_out, L1_attn_Wqkv, L1_attn_Wproj, L1_attn_bproj, L1_ffn_g1, L1_ffn_g2, L1_ffn_wq, L1_ffn_wk, L1_ffn_wv, L1_ffn_wo, L1_ffn_router_w, L1_ffn_router_b, L1_ffn_w1, L1_ffn_w2, L1_ffn_w3):
    import jax
    import jax.numpy as jnp

    def _L0_tok_ref(x, W, b, pos_embed):
        import jax, jax.numpy as jnp
        import numpy as np
        PATCH_SIZE = 16
        STRIDE = 8
        IN_DIM = 128
        D_MODEL = 256
        MAX_POS = 100
        B, L, D = x.shape
        n_patches = (L - PATCH_SIZE) // STRIDE + 1
        idx = jnp.arange(n_patches)[:, None] * STRIDE + jnp.arange(PATCH_SIZE)[None, :]
        patches = x[:, idx, :].reshape(B, n_patches, PATCH_SIZE * D)
        emb = jnp.einsum('bnf,fd->bnd', patches, W) + b
        emb = emb + pos_embed[:, :n_patches, :]
        return emb

    def _L0_attn_ref(inputs):
        import jax, jax.numpy as jnp
        import numpy as np
        DIM = 256
        SQRT_DIM = float(np.sqrt(DIM))
        x = jnp.transpose(inputs, (1, 0, 2))
        scores = jnp.einsum('bsd,btd->bst', x, x) / SQRT_DIM
        attn = jax.nn.softmax(scores, axis=-1)
        out = jnp.einsum('bst,btd->bsd', attn, x)
        return jnp.transpose(out, (1, 0, 2))

    def _L0_ffn_ref(oldx, W_in, b_in, W_out):
        import jax, jax.numpy as jnp
        import numpy as np
        DIM = 256
        DEPTH = 7
        PAR = 8
        N_NODES = 2 ** (DEPTH + 1) - 1
        WIDTH = PAR * N_NODES
        x = oldx.reshape(-1, DIM)
        B = x.shape[0]
        logits = x @ W_in.T + b_in
        decisions = (logits > 0).astype(jnp.int32).reshape(B, PAR, N_NODES)
        acts = jax.nn.silu(logits).reshape(B, PAR, N_NODES)
        current = jnp.zeros((B, PAR), dtype=jnp.int32)
        dmap = jax.nn.one_hot(current, N_NODES, dtype=acts.dtype)
        for d in range(DEPTH):
            cur_platform = 2 ** d - 1
            next_platform = 2 ** (d + 1) - 1
            moves = jnp.take_along_axis(decisions, current[..., None], axis=2)[..., 0]
            current = (current - cur_platform) * 2 + moves + next_platform
            dmap = dmap + jax.nn.one_hot(current, N_NODES, dtype=acts.dtype)
        masked = acts * jax.lax.stop_gradient(dmap)
        out = masked.reshape(B, WIDTH) @ W_out.T
        return out.reshape(oldx.shape)

    def _L1_attn_ref(x, Wqkv, Wproj, bproj):
        import jax, jax.numpy as jnp
        import numpy as np
        N_HEADS = 16
        LOCAL_WINDOW = 128
        ROPE_BASE = 10000.0

        def _rotate_half(x):
            x1 = x[..., 0::2]
            x2 = x[..., 1::2]
            return jnp.stack((-x2, x1), axis=-1).reshape(x.shape)

        def _rope_cache(T, hd, dtype):
            half = hd // 2
            inv_freq = 1.0 / ROPE_BASE ** (jnp.arange(half, dtype=dtype) / half)
            t = jnp.arange(T, dtype=dtype)
            freqs = t[:, None] * inv_freq[None, :]
            cos = jnp.repeat(jnp.cos(freqs), 2, axis=-1)
            sin = jnp.repeat(jnp.sin(freqs), 2, axis=-1)
            return (cos, sin)
        B, T, C = x.shape
        H = N_HEADS
        hd = C // H
        qkv = (x @ Wqkv.T).reshape(B, T, 3, H, hd).transpose(2, 0, 3, 1, 4)
        q, k, v = (qkv[0], qkv[1], qkv[2])
        cos, sin = _rope_cache(T, hd, x.dtype)
        cos = cos[None, None]
        sin = sin[None, None]
        q = q * cos + _rotate_half(q) * sin
        k = k * cos + _rotate_half(k) * sin
        scale = 1.0 / jnp.sqrt(jnp.asarray(hd, dtype=x.dtype))
        scores = jnp.einsum('bhqd,bhkd->bhqk', q, k) * scale
        i = jnp.arange(T)[:, None]
        j = jnp.arange(T)[None, :]
        allow = (j <= i) & (jnp.abs(i - j) <= LOCAL_WINDOW)
        scores = jnp.where(allow[None, None], scores, jnp.asarray(-jnp.inf, dtype=x.dtype))
        attn = jax.nn.softmax(scores, axis=-1)
        y = jnp.einsum('bhqk,bhkd->bhqd', attn, v)
        y = y.transpose(0, 2, 1, 3).reshape(B, T, C)
        return y @ Wproj.T + bproj

    def _L1_ffn_ref(x, g1, g2, wq, wk, wv, wo, router_w, router_b, w1, w2, w3):
        import jax, jax.numpy as jnp
        import numpy as np
        D = 256
        HQ = 16
        HKV = 4
        G = HQ // HKV
        K = 64
        V = 64
        E = 8
        TOPK = 2
        HID = 512
        CAP_FRAC = 0.125
        EPS = 1e-06

        def _rmsnorm(x, g):
            return x * jax.lax.rsqrt(jnp.mean(x * x, axis=-1, keepdims=True) + EPS) * g

        def _rotary_tables(t, dim):
            thetas = 10000.0 ** (-np.arange(0, dim, 2, dtype=np.float32) / dim)
            ticks = np.outer(np.arange(t, dtype=np.float32), thetas)
            ticks = np.tile(ticks, (1, 2))[None, :, None, :]
            return (jnp.asarray(np.cos(ticks)), jnp.asarray(np.sin(ticks)))

        def _neg_half(x):
            x1, x2 = jnp.split(x, 2, axis=-1)
            return jnp.concatenate([-x2, x1], axis=-1)

        def _attention(x, wq, wk, wv, wo):
            b, t, _ = x.shape
            q = (x @ wq).reshape(b, t, HQ, K)
            k = (x @ wk).reshape(b, t, HKV, K)
            v = (x @ wv).reshape(b, t, HKV, V)
            cos, sin = _rotary_tables(t, K)
            q = q * cos + _neg_half(q) * sin
            k = k * cos + _neg_half(k) * sin
            qg = q.reshape(b, t, G, HKV, K)
            scores = jnp.einsum('btghk,bThk->bghtT', qg, k)
            mask = jnp.tril(jnp.ones((t, t), bool))
            scores = jnp.where(mask, scores, -jnp.inf) / np.float32(np.sqrt(K))
            p = jax.nn.softmax(scores, axis=-1)
            out = jnp.einsum('bghtT,bThv->btghv', p, v).reshape(b, t, HQ * V)
            return out @ wo

        def _moe(x, router_w, router_b, w1, w2, w3):
            b, t, d = x.shape
            n = b * t
            xf = x.reshape(n, d)
            logits = xf @ router_w + router_b
            vals, idx = jax.lax.top_k(logits, TOPK)
            scores = jax.nn.softmax(vals, axis=-1)
            cap = int(np.floor(n * CAP_FRAC))
            oh = jax.nn.one_hot(idx, E, dtype=jnp.float32)
            pos = jnp.cumsum(jnp.cumsum(oh, axis=0), axis=1).astype(jnp.int32)
            emask = oh * (pos < cap)
            tmask = jnp.sum(emask, axis=-1)
            assign = jnp.einsum('tke,e->tk', emask, jnp.arange(E, dtype=jnp.float32)).astype(jnp.int32)
            m = jnp.max(assign, axis=-1)

            def ff(w1e, w2e, w3e):
                h = jax.nn.gelu(xf @ w2e * (xf @ w1e), approximate=False)
                return h @ w3e
            y_all = jax.vmap(ff)(w1, w2, w3)
            y = y_all[m, jnp.arange(n)]
            slot = jnp.where(tmask[..., None] > 0, y[:, None, :], xf[:, None, :])
            out = jnp.einsum('tkD,tk->tD', slot, scores)
            return out.reshape(b, t, d)
        h = x + _attention(_rmsnorm(x, g1), wq, wk, wv, wo)
        return h + _moe(_rmsnorm(h, g2), router_w, router_b, w1, w2, w3)
    h = _L0_tok_ref(x, L0_tok_W, L0_tok_b, L0_tok_pos_embed)
    h = h + _L0_attn_ref(_layernorm(h, axis=-1))
    h = h + _L0_ffn_ref(_layernorm(h, axis=-1), L0_ffn_W_in, L0_ffn_b_in, L0_ffn_W_out)
    h = h + _L1_attn_ref(_layernorm(h, axis=-1), L1_attn_Wqkv, L1_attn_Wproj, L1_attn_bproj)
    h = h + _L1_ffn_ref(_layernorm(h, axis=-1), L1_ffn_g1, L1_ffn_g2, L1_ffn_wq, L1_ffn_wk, L1_ffn_wv, L1_ffn_wo, L1_ffn_router_w, L1_ffn_router_b, L1_ffn_w1, L1_ffn_w2, L1_ffn_w3)
    return h

_drawn_inputs = setup_inputs


def setup_inputs(seed=0):
    import zlib

    import numpy as np

    out = dict(_drawn_inputs(seed))
    spreads = {'L1_ffn_g1': (1.0, 0.6), 'L1_ffn_g2': (1.0, 0.2), 'L1_ffn_router_b': (0.0, 0.1)}
    factors = {'L1_attn_bproj': 2.956,
     'L1_ffn_wq': 4.767,
     'L1_ffn_wk': 4.789,
     'L1_ffn_w1': 8.0,
     'L1_ffn_w2': 8.0,
     'L1_ffn_w3': 8.0}
    for name, (base, spread) in spreads.items():
        noise = np.random.default_rng([zlib.crc32(name.encode()), seed]).standard_normal(out[name].shape)
        drawn = base * np.exp(spread * noise) if base else spread * noise
        out[name] = jnp.asarray(drawn.astype(out[name].dtype))
    for name, factor in factors.items():
        out[name] = (out[name] * factor).astype(out[name].dtype)
    return out
```

```python
from contextlib import ExitStack

import numpy as np

import concourse.bass as bass
from concourse import mybir
from concourse.alu_op_type import AluOpType as ALU

F32 = mybir.dt.float32
BF16 = mybir.dt.bfloat16
I32 = mybir.dt.int32
U32 = mybir.dt.uint32
ACT = mybir.ActivationFunctionType
AX = mybir.AxisListType

P = 128
BATCH, NPATCH, DIM = 64, 24, 256
SEQ, IN_DIM, PATCH, STRIDE = 202, 128, 16, 8
TOK = BATCH * NPATCH
KC = DIM // P
NTILE = TOK // P
BLK = 384
NBLK = TOK // BLK
BB = BLK // NPATCH
NQ = BB // 4
XROWS = PATCH + STRIDE
PAR, NODES, DEPTH = 8, 255, 7
NCH = 16
HEADS, HD1 = 16, 16
HKV, HD2 = 4, 64
EXPERTS, HID = 8, 512
CAP = TOK // 8
SLOTS = 2 * CAP
NSLOT = EXPERTS * SLOTS
LN_EPS, RMS_EPS = 1e-5, 1e-6
FAR = -1e30

C_IDENT = 0
C_MEAN = 128
C_BLOCKMASK = 256
C_COS1, C_SIN1, C_COS2, C_SIN2 = 384, 408, 432, 456
C_QMASK = 480
C_YMASK = 484
C_CNT = 488
C_HALF = 490
C_ONES = 491
C_IOTA = 619
C_DUMP = 627
C_EPS = 639
NCONST = 640
B_ANC0 = 0
B_ANC1 = 128
B_TRI = 256
B_ONES = 384
B_IDENT = 512
B_CAUSAL = 640
NCONSTB = 664


def _tree(node):
    out, level = [], (node + 1).bit_length() - 1
    k = node - (2 ** level - 1)
    while level:
        level, right, k = level - 1, k & 1, k >> 1
        out.append((2 ** level - 1 + k, right))
    return out


def _constants():
    c = np.zeros((P, NCONST), np.float32)
    c[:, C_IDENT:C_IDENT + P] = np.eye(P)
    c[:, C_MEAN:C_MEAN + P] = 1.0 / DIM
    blk = np.arange(P) // BATCH
    c[:, C_BLOCKMASK:C_BLOCKMASK + P] = np.where(blk[:, None] == blk[None, :], 0.0, FAR)
    t = np.arange(NPATCH, dtype=np.float32)
    f1 = (np.float32(1.0) / np.float32(10000.0) ** (np.arange(8, dtype=np.float32) / np.float32(8))).astype(np.float32)
    a1 = t[:, None] * f1[None, :]
    a1 = a1[:, np.arange(P) % 8].T
    c[:, C_COS1:C_COS1 + NPATCH], c[:, C_SIN1:C_SIN1 + NPATCH] = np.cos(a1), np.sin(a1)
    f2 = 10000.0 ** (-np.arange(0, HD2, 2, dtype=np.float32) / HD2)
    a2 = np.outer(t, f2).astype(np.float32)[:, np.arange(P) % 32].T
    c[:, C_COS2:C_COS2 + NPATCH], c[:, C_SIN2:C_SIN2 + NPATCH] = np.cos(a2), np.sin(a2)
    p = np.arange(P)
    for a in range(4):
        c[:, C_QMASK + a] = (p // 8) % 4 == a
        c[:, C_YMASK + a] = (p // 16) % 4 == a
    rights = [sum(r for _, r in _tree(n)) for n in range(31)]
    c[:120, C_CNT] = [rights[q // 8] for q in range(120)]
    c[:, C_CNT + 1] = [rights[15 + q // 8] for q in range(P)]
    c[:, C_EPS] = LN_EPS
    c[:, C_HALF] = -0.5
    c[:, C_ONES:C_ONES + P] = 1.0
    c[:, C_IOTA:C_IOTA + 8] = np.arange(8)
    c[:, C_DUMP:C_DUMP + NTILE] = NSLOT + np.arange(NTILE)[None, :] * P + p[:, None]
    b = np.zeros((P, NCONSTB), np.float32)
    for q in range(120):
        for anc, right in _tree(q // 8):
            b[anc * 8 + q % 8, B_ANC0 + q] = 1 if right else -1
    for q in range(P):
        for anc, right in _tree(15 + q // 8):
            b[anc * 8 + q % 8, B_ANC1 + q] = 1 if right else -1
    b[:, B_TRI:B_TRI + P] = p[:, None] <= p[None, :]
    b[:, B_ONES:B_ONES + P] = 1.0
    b[:, B_IDENT:B_IDENT + P] = np.eye(P)
    b[:96, B_CAUSAL:B_CAUSAL + NPATCH] = np.where(np.arange(NPATCH)[None, :] <= (np.arange(96) % NPATCH)[:, None], 0.0, FAR)
    return c, b


def _ffn_rows():
    rows = -np.ones((NCH, P), np.int64)
    q = np.arange(120)
    rows[0, :120] = (q % 8) * NODES + q // 8
    q = np.arange(P)
    for c in range(1, NCH):
        r = c.bit_length() - 1
        node = 2 ** (4 + r) - 1 + (q // 8) * 2 ** r + (c - 2 ** r)
        rows[c] = (q % 8) * NODES + node
    return rows.reshape(-1)


class Chain:

    def __init__(self, eng, sem):
        self.eng, self.sem, self.base, self.n = eng, sem, 0, 0

    def turn(self, i, per):
        self.base, self.start, self.n, self.per = self.floor() + i * per, self.floor(), 0, per

    def floor(self):
        return self.base + self.n if isinstance(self.base, int) else self.start

    def end(self, times):
        assert self.n == self.per, (self.n, self.per)
        self.base, self.n = self.start + times * self.per, 0

    def link(self, ins):
        self.n += 1
        ins.then_inc(self.sem, 1)
        self.eng.wait_ge(self.sem, self.base + self.n)


def at_least(eng, sem, value):
    if not isinstance(value, int) or value > 0:
        eng.wait_ge(sem, value)


def bc(ap, axis, count):
    new = ap.unsqueeze(axis)
    shape = list(new.shape)
    shape[axis] = count
    return new.to_broadcast(shape)


def by_batch(ap):
    return ap.rearrange("p (b n) -> p b n", n=NPATCH)


def tower(nc, io, out):
    ctx = ExitStack()
    with ctx:
        def sb(name, shape, dt=F32):
            return ctx.enter_context(nc.sbuf_tensor(name, shape, dt))

        def sem(name):
            return ctx.enter_context(nc.semaphore(name))

        const = sb("const", [P, NCONST])
        constb = sb("constb", [P, NCONSTB], BF16)
        vecs = sb("vecs", [P, 22])
        negb = sb("negb", [P, NCH])
        rbias = sb("rbias", [1, EXPERTS])
        hT = sb("hT", [P, KC, TOK])
        dT = sb("dT", [P, KC, TOK])
        rstd = sb("rstd", [P, TOK])
        xf = sb("xf", [P, NTILE, DIM])
        res = sb("res", [P, NTILE, DIM])
        logit = sb("logit", [P, NTILE, EXPERTS])
        wbig = sb("wbig", [P, 8192])
        w1q = sb("w1q", [P, KC, 768])
        w1o = sb("w1o", [P, KC, DIM])
        w2q = sb("w2q", [P, KC, 1536])
        w2o = sb("w2o", [P, 8, DIM])
        wr = sb("wr", [P, KC, EXPERTS])
        wk = sb("work", [P, 17500])
        ps = ctx.enter_context(nc.psum_tensor("ps", [P, 8, 512], F32))
        win = wbig[:, 0:4096].rearrange("p (k n) -> p k n", k=KC)
        wout = wbig[:, 4096:8192].rearrange("p (c n) -> p c n", c=NCH)

        def carve(*shapes):
            at, views = 0, []
            for s in shapes:
                n = int(np.prod(s))
                v = wk[:, at:at + n]
                if len(s) > 1:
                    names = "abcd"[:len(s)]
                    v = v.rearrange(f"p ({' '.join(names)}) -> p {' '.join(names)}",
                                    **{k: d for k, d in zip(names, s)})
                views.append(v)
                at += n
            assert at <= 17500, at
            return views

        constb32 = dT[:, 1, 0:NCONSTB]
        ident = const[:, C_IDENT:C_IDENT + P]
        meanw = const[:, C_MEAN:C_MEAN + P]

        (wtok, xring, posb, brow, hA, xnA, xnTA, smA, eA, etA, h2A, statA, mvA, varA, rsA, nbA, sumA, rinvA, idleA) = carve(
            (PATCH, DIM), (2, XROWS * BATCH), (NTILE, DIM), (DIM,), (2, DIM), (2, DIM), (KC, P), (P,), (P,), (P,),
            (DIM,), (6,), (2,), (1,), (1,), (1,), (1,), (1,), (1,))
        sqL, stdL, riL = carve((KC, BLK), (BLK,), (BLK,))
        (xB, actB, accB, maskBf) = carve((KC, BLK), (4, BLK), (4, BLK), (NCH, BLK // 2))
        maskB = maskBf.bitcast(BF16)
        (xC, qC, kC, tC, qrawC, pC, smC, ptC, vC, yC, mxC, suC, riC) = carve(
            (KC, BB, 32), (2, 4 * BLK), (2, BLK), (2, 4, BLK), (2, BLK), (4, BB, 32), (2, BB, NPATCH), (4, 4 * 96), (NQ, DIM),
            (2, 4, BLK), (4, BB), (4, BB), (4, BB))

        def q_of(half, a):
            return qC[:, half, :].rearrange("p (b a n) -> p b a n", b=BB, a=4)[:, :, a, :]

        (xfF, rF, sqF, stdF, top8, idx8f, e12, oh, pq, em, cumS, t96, tm, asg, mG, actG, rankG, slotf, wy, wx,
         slotS, slotG, xsH, xtH, aH, prodH, gH, ysH, ohm) = carve(
            (KC, BLK), (KC, BLK), (KC, BLK), (BLK,), (NTILE, 8), (NTILE, 8), (2, NTILE), (2, NTILE, 8 // 2), (2, NTILE),
            (2, NTILE, 8), (2, NTILE, 8), (2, NTILE, 8), (2, NTILE), (2, NTILE), (NTILE,), (NTILE,), (NTILE,), (2, NTILE),
            (2, NTILE), (2, NTILE), (NTILE,), (NTILE,), (2, 3, DIM), (KC, SLOTS), (2, SLOTS), (2, SLOTS), (4, SLOTS),
            (2, 3, DIM), (NTILE, 8 // 2))
        ohB = oh.rearrange("p k t e -> p (k t e)").bitcast(BF16).rearrange("p (k t e) -> p k t e", k=2, t=NTILE)
        ohmB = ohm.rearrange("p t e -> p (t e)").bitcast(BF16).rearrange("p (t e) -> p t e", t=NTILE)
        idx8 = idx8f.bitcast(U32)
        slotS, slotG = slotS.bitcast(I32), slotG.bitcast(I32)
        ygH = dT[:].rearrange("p k t -> p (k t)").rearrange("p (t f) -> p t f", f=DIM)
        xs_d = nc.dram_tensor("xs", [NSLOT + TOK, DIM], F32).ap()
        ys_d = nc.dram_tensor("ys", [NSLOT, DIM], F32).ap()
        wexp = [wbig[:, q * 3072:(q + 1) * 3072] for q in range(2)]
        w1e = [w[:, 0:1024].rearrange("p (k n) -> p k n", k=KC) for w in wexp]
        w2e = [w[:, 1024:2048].rearrange("p (k n) -> p k n", k=KC) for w in wexp]
        w3e = [w[:, 2048:3072].rearrange("p (k n) -> p k n", k=4) for w in wexp]

        vd, ad, gd = sem("dve_step"), sem("act_step"), sem("pool_step")
        const_in, wtok_in, win_in, w1_in, w2_in = (sem(n) for n in ("const_in", "wtok_in", "wffn_in", "watt1_in", "watt2_in"))
        pos_in, constb_ready = sem("pos_in"), sem("constb_ready")
        x_in = [sem("x_in0"), sem("x_in1")]
        posb_ready, tok_ps, hA_ready, var_ready, rstdA_ready, xn_ready = (
            sem(n) for n in ("posb_ready", "tok_ps", "hA_ready", "var_ready", "rstdA_ready", "xn_ready"))
        xnT_ps, xnT_ready, sA_ps, smA_ready, eA_ready, eA_ps, etA_ready, pvA_ps, h2_ready, h2_ps, hT_ready = (
            sem(n) for n in ("xnT_ps", "xnT_ready", "sA_ps", "smA_ready", "eA_ready", "eA_ps", "etA_ready", "pvA_ps",
                             "h2_ready", "h2_ps", "hT_ready"))

        LN = {k: {n: sem(f"ln{k}_{n}") for n in ("mean_ps", "d_ready", "sq_ready", "var_ps", "std_ready", "done",
                                                "ms_ready", "rms_ready")}
              for k in "BCE"}
        FB = {n: sem(f"ffn_{n}") for n in ("x_ready", "l_ps", "dec_ready", "v_ps", "a_ready", "act_ready", "o_ps", "h_ready")}
        AT = {k: {n: sem(f"att{k}_{n}") for n in ("x_ready", "v_ps", "v_ready", "proj_ps", "t_ready", "qk_pool", "qk_ready",
                                                 "s_ps", "sub_ready", "e_ready", "p_ready", "pt_ps", "pt_ready",
                                                 "y_ps", "y_ready", "o_ps", "h_ready")}
              for k in "CE"}

        MO = {n: sem(f"moe_{n}") for n in ("r_ready", "std_ready", "xf_ready", "r_ps", "lg_ready", "diff_ready", "oh_ready",
                                          "cum_ps", "ohm_ready", "ex_ready", "rank_ps", "slot_ready", "a_ready",
                                          "prod_ready", "y_ps", "ys_ready", "yg_in", "out_ready", "sq_ready", "ms_ps",
                                          "xfT_ps", "xf_out", "xt_ps", "xt_ready", "up_ps", "g_ready", "scattered")}
        MO["ys_out"] = [sem("moe_ys_out0"), sem("moe_ys_out1")]
        MO["xs_in"] = [sem("moe_xs_in0"), sem("moe_xs_in1")]
        MO["we_in"] = [sem("moe_we_in0"), sem("moe_we_in1")]
        zero_ready, zero_out, out_done = sem("zero_ready"), sem("zero_out"), sem("out_done")

        block = ctx.enter_context(nc.Block())

        @block.sync
        def _(sp):
            sp.dma_start(const[:], io["const"]).then_inc(const_in, 16)
            sp.dma_start(constb32, io["constb"]).then_inc(const_in, 16)
            sp.dma_start(vecs[:], io["vecs"]).then_inc(const_in, 16)
            sp.dma_start(rbias[:], io["rb"]).then_inc(const_in, 16)
            sp.dma_start(wtok, io["wtok"]).then_inc(wtok_in, 16)

            def load_x(t, q):
                at_least(sp, tok_ps, t - 1)
                sp.dma_start(xring[:, q, :], io["x"][bass.ds(t, 1)].rearrange("t p n -> (t p) n")).then_inc(x_in[q], 16)

            load_x(0, 0)
            load_x(1, 1)
            with sp.Fori(1, NTILE // 2) as j:
                for q in range(2):
                    load_x(2 * j + q, q)

            def load_expert(e, q):
                sp.dma_start(wexp[q], io["wexp"][bass.ds(e, 1)].rearrange("e p n -> (e p) n")).then_inc(MO["we_in"][q], 16)

            def load_slots(e, q):
                sp.dma_start(xsH[:, q], xs_d[bass.ds(e * SLOTS, SLOTS), :].rearrange("(s p) f -> p s f", p=P)).then_inc(MO["xs_in"][q], 16)

            sp.wait_ge(FB["h_ready"], NBLK)
            for q in range(2):
                load_expert(q, q)
            sp.wait_ge(MO["scattered"], 16 * NTILE)
            for q in range(2):
                load_slots(q, q)
            with sp.Fori(1, EXPERTS // 2) as g:
                for q in range(2):
                    sp.wait_ge(MO["y_ps"], 6 * g - 6 + 3 * q + 3)
                    load_expert(2 * g + q, q)
                    load_slots(2 * g + q, q)
            for t in range(NTILE):
                sp.wait_ge(MO["out_ready"], t + 1)
                sp.dma_start(out[t * P:(t + 1) * P, :], res[:, t, :]).then_inc(out_done, 16)
            sp.wait_ge(out_done, 16 * NTILE)

        @block.gpsimd
        def _(pool):
            pool.dma_start(posb[0:64, :, :], io["pos"][0:NPATCH:2, :].unsqueeze(0).to_broadcast([64, NTILE, DIM])).then_inc(pos_in, 16)
            pool.dma_start(posb[64:128, :, :], io["pos"][1:NPATCH:2, :].unsqueeze(0).to_broadcast([64, NTILE, DIM])).then_inc(pos_in, 16)
            pool.dma_start(brow, io["btok"].to_broadcast([P, DIM])).then_inc(pos_in, 16)
            for dst, name in ((win, "win"), (wout, "wout")):
                pool.dma_start(dst, io[name]).then_inc(win_in, 16)
            for dst, name in ((w1q, "w1q"), (w1o, "w1o")):
                pool.dma_start(dst[:], io[name]).then_inc(w1_in, 16)
            for dst, name in ((w2q, "w2q"), (w2o, "w2o"), (wr, "wr")):
                pool.dma_start(dst[:], io[name]).then_inc(w2_in, 16)
            pool.wait_ge(const_in, 64)
            ch = Chain(pool, gd)
            nc.gpsimd.memset(dT[:, 0, 0:DIM], 0.0).then_inc(zero_ready, 1)
            pool.wait_ge(zero_ready, 1)
            pool.dma_start(xs_d[0:NSLOT, :].rearrange("(r p) f -> p r f", p=P), bc(dT[:, 0, 0:DIM], 1, NSLOT // P)).then_inc(zero_out, 16)

            def rstd_a(i):
                pool.wait_ge(var_ready, i + 1)
                ch.link(nc.gpsimd.tensor_tensor(varA, mvA[:, 1:2], const[:, C_EPS:C_EPS + 1], ALU.add))
                nc.gpsimd.tensor_tensor(rsA, varA, const[:, C_HALF:C_HALF + 1], ALU.pow).then_inc(rstdA_ready, 1)

            for i in (0, 1):
                rstd_a(i)
            with pool.Fori(2, NTILE) as i:
                ch.turn(i - 2, 1)
                rstd_a(i)
            ch.end(NTILE - 2)
            for kind in "CE":
                S = AT[kind]
                pairs = 2 if kind == "C" else 5
                with pool.Fori(0, NBLK) as i:
                    for p in range(pairs):
                        pool.wait_ge(S["t_ready"], i * pairs + p + 1)
                        last = p == pairs - 1
                        for half, (op, a, b) in enumerate(((ALU.subtract, 0, 1), (ALU.add, 2, 3))):
                            dst = by_batch(kC[:, half, :]) if last else by_batch(qrawC[:, half, :]) if kind == "C" else q_of(half, p)
                            ins = nc.gpsimd.tensor_tensor(dst, by_batch(tC[:, p % 2, a, :]), by_batch(tC[:, p % 2, b, :]), op)
                        ins.then_inc(S["qk_pool"], 1)
            pool.wait_ge(MO["slot_ready"], 1)
            pool.wait_ge(MO["xf_out"], NBLK)
            pool.wait_ge(zero_out, 16)
            for t in range(NTILE):
                pool.indirect_dma_start(xs_d, bass.IndirectOffsetOnAxis(ap=slotS[:, t:t + 1], axis=0), xf[:, t, :], None).then_inc(MO["scattered"], 16)
            with pool.Fori(0, EXPERTS // 2) as g:
                for q in range(2):
                    pool.wait_ge(MO["ys_ready"], 6 * g + 3 * q + 3)
                    pool.dma_start(ys_d[bass.ds((2 * g + q) * SLOTS, SLOTS), :].rearrange("(s p) f -> p s f", p=P), ysH[:, q]).then_inc(MO["ys_out"][q], 16)
            for q in range(2):
                pool.wait_ge(MO["ys_out"][q], 16 * (EXPERTS // 2))
            for t in range(NTILE):
                pool.indirect_dma_start(ygH[:, t, :], None, ys_d, bass.IndirectOffsetOnAxis(ap=slotG[:, t:t + 1], axis=0)).then_inc(MO["yg_in"], 16)

        @block.vector
        def _(dve):
            v = nc.vector
            ch = Chain(dve, vd)
            dve.wait_ge(const_in, 64)
            ch.link(v.tensor_scalar(negb[:], vecs[:, 0:NCH], -1.0, None, ALU.mult))
            v.tensor_copy(constb[:], constb32).then_inc(constb_ready, 1)
            dve.wait_ge(pos_in, 48)
            v.tensor_tensor(posb, posb, bc(brow, 1, NTILE), ALU.add).then_inc(posb_ready, 1)
            dve.wait_ge(posb_ready, 1)

            def embed(i, q):
                dve.wait_ge(tok_ps, i + 1)
                v.tensor_tensor(hA[:, q, :], ps[:, q, 0:DIM], posb[:, bass.ds(i, 1), :].rearrange("p t f -> p (t f)"),
                                ALU.add).then_inc(hA_ready, 1)
                dve.wait_ge(hA_ready, i + 1)
                ch.link(v.bn_stats(statA, hA[:, q, :]))
                v.memset(idleA, 0.0)
                v.bn_aggr(mvA, statA).then_inc(var_ready, 1)
                dve.wait_ge(rstdA_ready, i + 1)
                v.tensor_scalar(xnA[:, q, :], hA[:, q, :], mvA[:, 0:1], rsA, ALU.subtract, ALU.mult).then_inc(xn_ready, 1)

            def soft_a(i):
                dve.wait_ge(sA_ps, i + 1)
                ch.link(v.scalar_tensor_tensor(smA, ps[:, 3, 0:P], 1.0 / 16, const[:, C_BLOCKMASK:C_BLOCKMASK + P],
                                               ALU.mult, ALU.add))
                v.tensor_reduce(nbA, smA, AX.X, ALU.max, negate=True).then_inc(smA_ready, 1)

            def out_a(i, q):
                dve.wait_ge(pvA_ps, i + 1)
                ch.link(v.reciprocal(rinvA, sumA))
                v.scalar_tensor_tensor(h2A, ps[:, 5, 0:DIM], rinvA, hA[:, q, :], ALU.mult, ALU.add).then_inc(h2_ready, 1)

            embed(0, 0)
            PER_A = 3

            def tile_a(i, q, last=False):
                soft_a(i)
                if not last:
                    embed(i + 1, 1 - q)
                out_a(i, q)

            for i in (0, 1):
                tile_a(i, i)
            with dve.Fori(1, NTILE // 2 - 1) as j:
                ch.turn(j - 1, 2 * PER_A)
                for q in range(2):
                    tile_a(2 * j + q, q)
            ch.end(NTILE // 2 - 2)
            for i in (NTILE - 2, NTILE - 1):
                tile_a(i, i % 2, last=i == NTILE - 1)

            def norm(kind):
                S = LN[kind]
                with dve.Fori(0, NBLK) as i:
                    cols = bass.ds(i * BLK, BLK)
                    ch.turn(i, 6 if kind == "E" else 0)
                    dve.wait_ge(S["mean_ps"], i + 1)
                    v.tensor_tensor(dT[:, :, cols], hT[:, :, cols], bc(ps[:, 0, 0:BLK], 1, KC), ALU.subtract).then_inc(S["d_ready"], 1)
                    dve.wait_ge(S["std_ready"], i + 1)
                    if kind != "E":
                        v.reciprocal(rstd[:, cols], stdL).then_inc(S["done"], 1)
                    else:
                        ch.link(v.reciprocal(riL, stdL))
                        ch.link(v.tensor_tensor(dT[:, :, cols], dT[:, :, cols], bc(riL, 1, KC), ALU.mult))
                        ch.link(v.tensor_tensor(sqL[:, 0, :], ps[:, 1, 0:BLK], riL, ALU.mult))
                        ch.link(v.tensor_tensor(sqL[:, 1, :], sqL[:, 0, :], riL, ALU.mult))
                        v.tensor_scalar(sqL[:, 0, :], sqL[:, 1, :], RMS_EPS, None, ALU.add).then_inc(S["ms_ready"], 1)
                        dve.wait_ge(S["rms_ready"], i + 1)
                        ch.link(v.reciprocal(riL, stdL))
                        ch.link(v.tensor_copy(rstd[:, cols], riL))
                ch.end(NBLK)

            dve.wait_ge(hT_ready, NTILE)
            dve.wait_ge(zero_out, 16)
            norm("B")
            dve.wait_ge(LN["B"]["done"], NBLK)
            with dve.Fori(0, NBLK) as i:
                cols = bass.ds(i * BLK, BLK)
                ch.turn(i, 8)
                v.tensor_tensor(xB, dT[:, :, cols], bc(rstd[:, cols], 1, KC), ALU.mult).then_inc(FB["x_ready"], 1)
                for c in range(NCH):
                    l_ps = ps[:, c % 4, 0:BLK]
                    dve.wait_ge(FB["l_ps"], i * NCH + c + 1)
                    if c == 0:
                        v.tensor_scalar(maskB[:, 0, :], l_ps, negb[:, 0:1], None, ALU.is_gt).then_inc(FB["dec_ready"], 1)
                        dve.wait_ge(FB["v_ps"], i + 1)
                        ch.link(v.tensor_scalar(maskB[:, 1, :], ps[:, 7, 0:BLK], const[:, C_CNT + 1:C_CNT + 2], None,
                                                ALU.is_equal))
                        dve.wait_ge(FB["a_ready"], i * NCH + c + 1)
                        v.scalar_tensor_tensor(accB[:, 0, :], ps[:, 6, 0:BLK], const[:, C_CNT:C_CNT + 1], actB[:, 0, :],
                                               ALU.is_equal, ALU.mult).then_inc(FB["act_ready"], 1)
                        continue
                    if c < 8:
                        v.scalar_tensor_tensor(maskB[:, 2 * c + 1, :], l_ps, negb[:, c:c + 1], maskB[:, c, :],
                                               ALU.is_gt, ALU.mult).then_inc(FB["dec_ready"], 1)
                        dve.wait_ge(FB["dec_ready"], 8 * i + c + 1)
                        ch.link(v.tensor_tensor(maskB[:, 2 * c, :], maskB[:, c, :], maskB[:, 2 * c + 1, :], ALU.subtract))
                    dve.wait_ge(FB["a_ready"], i * NCH + c + 1)
                    v.tensor_tensor(accB[:, c % 4, :], actB[:, c % 4, :], maskB[:, c, :], ALU.mult).then_inc(FB["act_ready"], 1)
                dve.wait_ge(FB["o_ps"], i + 1)
                v.tensor_tensor(hT[:, :, cols], hT[:, :, cols], ps[:, 4:6, 0:BLK], ALU.add).then_inc(FB["h_ready"], 1)
            ch.end(NBLK)

            def attention(kind):
                S = AT[kind]
                pairs = 2 if kind == "C" else 5
                cos0, sin0 = (C_COS1, C_SIN1) if kind == "C" else (C_COS2, C_SIN2)
                cos = bc(const[:, cos0:cos0 + NPATCH], 1, BB)
                sin = bc(const[:, sin0:sin0 + NPATCH], 1, BB)
                ch.link(v.memset(pC, 0.0))
                ch.link(v.memset(xC, 0.0))
                with dve.Fori(0, NBLK) as i:
                    cols = bass.ds(i * BLK, BLK)
                    ch.turn(i, 18 if kind == "C" else 12)
                    if kind == "C":
                        for c in range(KC):
                            ins = v.tensor_tensor(xC[:, c, :, 0:NPATCH], by_batch(dT[:, c, cols]), by_batch(rstd[:, cols]), ALU.mult)
                        ins.then_inc(S["x_ready"], 1)
                    else:
                        for c in range(KC):
                            ins = v.scalar_tensor_tensor(xC[:, c, :, 0:NPATCH], by_batch(dT[:, c, cols]), vecs[:, 16 + c:17 + c], by_batch(rstd[:, cols]),
                                                         ALU.mult, ALU.mult)
                        ins.then_inc(S["x_ready"], 1)
                    for p in range(pairs):
                        dve.wait_ge(S["proj_ps"], i * pairs + p + 1)
                        if p >= 2:
                            dve.wait_ge(S["qk_pool"], i * pairs + p - 1)
                        first, second = (ps[:, 2 * (p % 2) + h, 0:BLK].rearrange("p (b n) -> p b n", n=NPATCH) for h in range(2))
                        for k, (src, tab) in enumerate(((first, cos), (second, sin), (second, cos), (first, sin))):
                            ins = v.tensor_tensor(tC[:, p % 2, k, :].rearrange("p (b n) -> p b n", n=NPATCH), src, tab, ALU.mult)
                        ins.then_inc(S["t_ready"], 1)
                    if kind == "C":
                        dve.wait_ge(S["qk_pool"], i * pairs + 1)
                        for half in range(2):
                            for a in range(4):
                                ins = v.tensor_scalar(q_of(half, a), by_batch(qrawC[:, half, :]), const[:, C_QMASK + a:C_QMASK + a + 1],
                                                      None, ALU.mult)
                        ins.then_inc(S["qk_ready"], 1)

                    def spread(g):
                        dve.wait_ge(S["s_ps"], 4 * i + g + 1)
                        s_ps = ps[0:96, 4 + g, :].rearrange("p (b n) -> p b n", n=32)[:, :, 0:NPATCH]
                        ch.link(v.tensor_reduce(mxC[0:96, g, :], s_ps, AX.X, ALU.max))
                        v.tensor_tensor(smC[0:96, g % 2], s_ps, bc(mxC[0:96, g, :], 2, NPATCH), ALU.subtract).then_inc(S["sub_ready"], 1)

                    def weigh(g):
                        dve.wait_ge(S["e_ready"], 4 * i + g + 1)
                        p_g = pC[0:96, g, :, 0:NPATCH]
                        ch.link(v.tensor_reduce(suC[0:96, g, :], p_g, AX.X, ALU.add))
                        ch.link(v.reciprocal(riC[0:96, g, :], suC[0:96, g, :]))
                        v.tensor_tensor(p_g, p_g, bc(riC[0:96, g, :], 2, NPATCH), ALU.mult).then_inc(S["p_ready"], 1)

                    for g in range(4):
                        spread(g)
                        if g:
                            weigh(g - 1)
                    weigh(3)
                    if kind == "C":
                        for hp in range(2):
                            dve.wait_ge(S["y_ps"], 2 * i + hp + 1)
                            bank = 4 if hp == 0 else 0
                            y = yC[:, hp, 0, :].rearrange("p (j n) -> p j n", j=4)
                            for a in range(4):
                                src = ps[:, bank:bank + 4, a * 96:(a + 1) * 96]
                                m = const[:, C_YMASK + a:C_YMASK + a + 1]
                                if a == 0:
                                    ins = v.tensor_scalar(y, src, m, None, ALU.mult)
                                else:
                                    ins = v.scalar_tensor_tensor(y, src, m, y, ALU.mult, ALU.add)
                                if a == 3:
                                    ins.then_inc(S["y_ready"], 1)
                                elif hp == 0:
                                    ch.link(ins)
                                else:
                                    ch.link(ins)
                    dve.wait_ge(S["o_ps"], i + 1)
                    if kind == "C":
                        for c in range(KC):
                            ins = v.scalar_tensor_tensor(hT[:, c, cols], ps[:, 4 + c, 0:BLK], vecs[:, 20 + c:21 + c], hT[:, c, cols],
                                                         ALU.add, ALU.add)
                        ins.then_inc(S["h_ready"], 1)
                    else:
                        v.tensor_tensor(dT[:, :, cols], dT[:, :, cols], ps[:, 4:6, 0:BLK], ALU.add).then_inc(S["h_ready"], 1)
                ch.end(NBLK)

            dve.wait_ge(FB["h_ready"], NBLK)
            norm("C")
            dve.wait_ge(LN["C"]["done"], NBLK)
            attention("C")
            dve.wait_ge(AT["C"]["h_ready"], NBLK)
            norm("E")
            attention("E")
            dve.wait_ge(AT["E"]["h_ready"], NBLK)

            with dve.Fori(0, NBLK) as i:
                cols = bass.ds(i * BLK, BLK)
                ch.turn(i, 1)
                v.tensor_tensor(rF, hT[:, :, cols], dT[:, :, cols], ALU.add).then_inc(MO["r_ready"], 1)
                dve.wait_ge(MO["std_ready"], i + 1)
                ch.link(v.reciprocal(rstd[:, 0:BLK], stdF))
                for c in range(KC):
                    ins = v.scalar_tensor_tensor(xfF[:, c, :], dT[:, c, cols], vecs[:, 18 + c:19 + c], rstd[:, 0:BLK],
                                                 ALU.mult, ALU.mult)
                ins.then_inc(MO["xf_ready"], 1)
                dve.wait_ge(MO["r_ps"], i + 1)
                v.tensor_copy(res[:, bass.ds(3 * i, 2), :], ps[:, 5, :].rearrange("p (t f) -> p t f", f=DIM))
                v.tensor_copy(res[:, bass.ds(3 * i + 2, 1), :], ps[:, 6, 0:DIM].rearrange("p (t f) -> p t f", f=DIM))
                v.tensor_copy(logit[:, bass.ds(3 * i, 3), :], ps[:, 2, 0:24].rearrange("p (t e) -> p t e", e=8)).then_inc(MO["lg_ready"], 1)
            ch.end(NBLK)
            dve.wait_ge(MO["lg_ready"], NBLK)

            for t in range(NTILE):
                ins = v.max(top8[:, t, :], logit[:, t, :])
            ch.link(ins)
            for t in range(NTILE):
                ins = v.max_index(idx8[:, t, :], top8[:, t, :], logit[:, t, :])
            v.tensor_tensor(pq[:, 1, :], top8[:, :, 1], top8[:, :, 0], ALU.subtract).then_inc(MO["diff_ready"], 1)
            dve.wait_ge(MO["diff_ready"], 1)
            ch.link(v.tensor_copy(e12, idx8[:, :, 0:2].rearrange("p t k -> p k t")))
            iota = const[:, C_IOTA:C_IOTA + 8]
            iota_t = bc(iota, 1, NTILE)
            for k in range(2):
                ins = v.tensor_tensor(ohB[:, k], iota_t, bc(e12[:, k, :], 2, 8), ALU.is_equal)
            ins.then_inc(MO["oh_ready"], 1)
            dve.wait_ge(MO["cum_ps"], 1)
            cum = ps[:, 0, 0:192].rearrange("p (k t e) -> p k t e", k=2, t=NTILE)
            ch.link(v.tensor_copy(cumS[:, 0], cum[:, 0]))
            ch.link(v.tensor_tensor(cumS[:, 1], cum[:, 1], cumS[:, 0], ALU.add))
            for k in range(2):
                ch.link(v.scalar_tensor_tensor(em[:, k], cumS[:, k], float(CAP), ohB[:, k], ALU.is_lt, ALU.mult))
                ch.link(v.tensor_reduce(tm[:, k, :], em[:, k], AX.X, ALU.add))
                ch.link(v.tensor_tensor(t96[:, k], em[:, k], iota_t, ALU.mult))
                ch.link(v.tensor_reduce(asg[:, k, :], t96[:, k], AX.X, ALU.add))
            ch.link(v.tensor_tensor(mG, asg[:, 0, :], asg[:, 1, :], ALU.max))
            ch.link(v.tensor_tensor(actG, tm[:, 0, :], tm[:, 1, :], ALU.max))
            ch.link(v.tensor_tensor(t96[:, 0], iota_t, bc(mG, 2, 8), ALU.is_equal))
            v.tensor_tensor(ohmB, t96[:, 0], bc(actG, 2, 8), ALU.mult).then_inc(MO["ohm_ready"], 1)
            dve.wait_ge(MO["ex_ready"], 1)
            ch.link(v.tensor_scalar(rankG, pq[:, 1, :], 1.0, None, ALU.add))
            ch.link(v.reciprocal(pq[:, 0, :], rankG))
            ch.link(v.tensor_tensor(pq[:, 1, :], pq[:, 1, :], pq[:, 0, :], ALU.mult))
            ch.link(v.tensor_tensor(wy, tm, pq, ALU.mult))
            ch.link(v.tensor_tensor(wx, pq, wy, ALU.subtract))
            ch.link(v.tensor_tensor(wy[:, 0, :], wy[:, 0, :], wy[:, 1, :], ALU.add))
            ch.link(v.tensor_tensor(wx[:, 0, :], wx[:, 0, :], wx[:, 1, :], ALU.add))
            dve.wait_ge(MO["rank_ps"], 1)
            ch.link(v.tensor_tensor(t96[:, 1], ps[:, 1, 0:96].rearrange("p (t e) -> p t e", e=8), ohmB, ALU.mult))
            ch.link(v.tensor_reduce(rankG, t96[:, 1], AX.X, ALU.add))
            ch.link(v.scalar_tensor_tensor(slotf[:, 0, :], mG, float(SLOTS), rankG, ALU.mult, ALU.add))
            ch.link(v.tensor_scalar(slotf[:, 1, :], slotf[:, 0, :], -1.0, None, ALU.add))
            ch.link(v.tensor_tensor(slotf[:, 0, :], slotf[:, 1, :], const[:, C_DUMP:C_DUMP + NTILE], ALU.subtract))
            ch.link(v.tensor_tensor(slotf[:, 0, :], slotf[:, 0, :], actG, ALU.mult))
            ch.link(v.tensor_tensor(slotf[:, 0, :], slotf[:, 0, :], const[:, C_DUMP:C_DUMP + NTILE], ALU.add))
            ch.link(v.tensor_tensor(slotf[:, 1, :], slotf[:, 1, :], actG, ALU.mult))
            v.tensor_copy(slotS, slotf[:, 0, :])
            v.tensor_copy(slotG, slotf[:, 1, :]).then_inc(MO["slot_ready"], 1)

            def expert(g, q):
                for j in range(4):
                    n = (2 * g + q) * 4 + j + 1
                    dve.wait_ge(MO["a_ready"], n)
                    v.tensor_tensor(prodH[:, j % 2, :], aH[:, j % 2, :], ps[:, 3 + 2 * (j % 2), 0:SLOTS], ALU.mult).then_inc(MO["prod_ready"], 1)
                at_least(dve, MO["ys_out"][q], 16 * g)
                for s in range(3):
                    dve.wait_ge(MO["y_ps"], (2 * g + q) * 3 + s + 1)
                    v.tensor_copy(ysH[:, q, s, :], ps[:, 6 + s % 2, 0:DIM]).then_inc(MO["ys_ready"], 1)

            for q in range(2):
                expert(0, q)
            with dve.Fori(1, EXPERTS // 2) as g:
                for q in range(2):
                    expert(g, q)

            for t in range(NTILE):
                dve.wait_ge(MO["yg_in"], 16 * NTILE)
                ch.link(v.scalar_tensor_tensor(res[:, t, :], ygH[:, t, :], wy[:, 0, t:t + 1], res[:, t, :], ALU.mult, ALU.add))
                v.scalar_tensor_tensor(res[:, t, :], xf[:, t, :], wx[:, 0, t:t + 1], res[:, t, :],
                                       ALU.mult, ALU.add).then_inc(MO["out_ready"], 1)

        @block.scalar
        def _(act):
            a_ = nc.scalar

            def place_h(i):
                act.wait_ge(h2_ps, i + 1)
                dst = hT[:].rearrange("p c (b n) -> p c n b", n=NPATCH)[:, :, bass.ds(2 * i, 2), :]
                a_.activation(dst, ps[:, 6, 0:DIM].rearrange("p (c n b) -> p c n b", c=KC, n=2), ACT.Copy).then_inc(hT_ready, 1)

            def tile_a(i, first=False):
                if not first:
                    place_h(i - 1)
                act.wait_ge(xnT_ps, i + 1)
                a_.activation(xnTA, ps[:, 2, 0:DIM].rearrange("p (c t) -> p c t", c=KC), ACT.Copy).then_inc(xnT_ready, 1)
                act.wait_ge(smA_ready, i + 1)
                a_.activation(eA, smA, ACT.Exp, bias=nbA, accum_out=sumA).then_inc(eA_ready, 1)
                act.wait_ge(eA_ps, i + 1)
                a_.activation(etA, ps[:, 4, 0:P], ACT.Copy).then_inc(etA_ready, 1)

            tile_a(0, first=True)
            with act.Fori(1, NTILE) as i:
                tile_a(i)
            place_h(NTILE - 1)

            def norm(kind):
                S = LN[kind]
                with act.Fori(0, NBLK) as i:
                    cols = bass.ds(i * BLK, BLK)
                    act.wait_ge(S["d_ready"], i + 1)
                    a_.activation(sqL, dT[:, :, cols], ACT.Square).then_inc(S["sq_ready"], 1)
                    act.wait_ge(S["var_ps"], i + 1)
                    a_.activation(stdL, ps[:, 1, 0:BLK], ACT.Sqrt, bias=LN_EPS).then_inc(S["std_ready"], 1)
                    if kind == "E":
                        act.wait_ge(S["ms_ready"], i + 1)
                        a_.activation(stdL, sqL[:, 0, :], ACT.Sqrt).then_inc(S["rms_ready"], 1)

            norm("B")
            with act.Fori(0, NBLK) as i:
                for c in range(NCH):
                    act.wait_ge(FB["l_ps"], i * NCH + c + 1)
                    if c < 8:
                        act.wait_ge(FB["dec_ready"], 8 * i + c + 1)
                    a_.activation(actB[:, c % 4, :], ps[:, c % 4, 0:BLK], ACT.Silu, bias=vecs[:, c:c + 1]).then_inc(FB["a_ready"], 1)

            def attention(kind):
                S = AT[kind]
                scale = 0.25 if kind == "C" else 0.125
                with act.Fori(0, NBLK) as i:
                    act.wait_ge(S["v_ps"], i + 1)
                    a_.activation(vC, ps[:, 6:8, :].rearrange("p k (q f) -> p (k q) f", f=DIM), ACT.Copy).then_inc(S["v_ready"], 1)
                    for g in range(4):
                        act.wait_ge(S["sub_ready"], 4 * i + g + 1)
                        a_.activation(pC[0:96, g, :, 0:NPATCH], smC[0:96, g % 2], ACT.Exp, scale=scale).then_inc(S["e_ready"], 1)
                    for g in range(4):
                        act.wait_ge(S["pt_ps"], 4 * i + g + 1)
                        a_.activation(ptC[:, g, :], ps[:, g, 0:BLK], ACT.Copy).then_inc(S["pt_ready"], 1)
                    if kind == "E":
                        for hp in range(2):
                            act.wait_ge(S["y_ps"], 2 * i + hp + 1)
                            bank = 4 if hp == 0 else 0
                            for a in range(4):
                                ins = a_.activation(yC[:, hp, a, :].rearrange("p (j n) -> p j n", j=4),
                                                    ps[:, bank:bank + 4, a * 96:(a + 1) * 96], ACT.Copy)
                            ins.then_inc(S["y_ready"], 1)

            norm("C")
            attention("C")
            norm("E")
            attention("E")
            with act.Fori(0, NBLK) as i:
                cols = bass.ds(i * BLK, BLK)
                act.wait_ge(AT["E"]["h_ready"], NBLK)
                a_.activation(sqF, dT[:, :, cols], ACT.Square).then_inc(MO["sq_ready"], 1)
                act.wait_ge(MO["ms_ps"], i + 1)
                a_.activation(stdF, ps[:, 0, 0:BLK], ACT.Sqrt, bias=RMS_EPS).then_inc(MO["std_ready"], 1)
                act.wait_ge(MO["xfT_ps"], i + 1)
                a_.activation(xf[:, bass.ds(3 * i, 2), :], ps[:, 3, :].rearrange("p (t f) -> p t f", f=DIM), ACT.Copy)
                a_.activation(xf[:, bass.ds(3 * i + 2, 1), :], ps[:, 4, 0:DIM].rearrange("p (t f) -> p t f", f=DIM),
                              ACT.Copy).then_inc(MO["xf_out"], 1)
            act.wait_ge(MO["diff_ready"], 1)
            a_.activation(pq[:, 1, :], pq[:, 1, :], ACT.Exp).then_inc(MO["ex_ready"], 1)
            with act.Fori(0, EXPERTS // 2) as g:
                for q in range(2):
                    e = 2 * g + q
                    act.wait_ge(MO["xt_ps"], e + 1)
                    xt = xtH.rearrange("p c (s t) -> p s c t", t=P)
                    a_.activation(xt[:, 0:2], ps[:, 0, :].rearrange("p (s c t) -> p s c t", c=KC, t=P), ACT.Copy)
                    a_.activation(xt[:, 2], ps[:, 1, 0:DIM].rearrange("p (c t) -> p c t", t=P), ACT.Copy).then_inc(MO["xt_ready"], 1)

                    def gelu(j):
                        act.wait_ge(MO["prod_ready"], e * 4 + j + 1)
                        a_.activation(gH[:, j, :], prodH[:, j % 2, :], ACT.Gelu).then_inc(MO["g_ready"], 1)

                    for j in range(4):
                        act.wait_ge(MO["up_ps"], e * 4 + j + 1)
                        a_.activation(aH[:, j % 2, :], ps[:, 2 + 2 * (j % 2), 0:SLOTS], ACT.Copy).then_inc(MO["a_ready"], 1)
                        if j:
                            gelu(j - 1)
                    gelu(3)

        @block.tensor
        def _(pe):
            mm, tr = nc.tensor.matmul, nc.tensor.transpose
            pe.wait_ge(const_in, 64)
            pe.wait_ge(wtok_in, 16)

            def embed(q, first, last):
                x = xring[:, q, :].rearrange("p (r l) -> p r l", r=STRIDE)
                for r in range(first, last):
                    at = r // STRIDE * BATCH
                    ins = mm(ps[:, q, 0:DIM], x[:, r % STRIDE, at:at + P], wtok[:, r, :], start=r == 0, stop=r == PATCH - 1)
                if last == PATCH:
                    ins.then_inc(tok_ps, 1)

            def transpose_h():
                for c in range(KC):
                    ins = tr(ps[:, 6, c * P:(c + 1) * P], h2A[:, c * P:(c + 1) * P], ident)
                ins.then_inc(h2_ps, 1)

            def tile_a(i, q, j=0, first=False, last=False):
                if not last:
                    pe.wait_ge(x_in[1 - q], 16 * (j + q + 1))
                    at_least(pe, hA_ready, i)
                    embed(1 - q, 0, 5)
                if not first:
                    pe.wait_ge(h2_ready, i)
                    transpose_h()
                pe.wait_ge(xn_ready, i + 1)
                for c in range(KC):
                    ins = tr(ps[:, 2, c * P:(c + 1) * P], xnA[:, q, c * P:(c + 1) * P], ident)
                ins.then_inc(xnT_ps, 1)
                if not last:
                    embed(1 - q, 5, 8)
                pe.wait_ge(xnT_ready, i + 1)
                for c in range(KC):
                    ins = mm(ps[:, 3, 0:P], xnTA[:, c, :], xnTA[:, c, :], start=c == 0, stop=c == KC - 1)
                ins.then_inc(sA_ps, 1)
                if not last:
                    embed(1 - q, 8, 12)
                pe.wait_ge(eA_ready, i + 1)
                tr(ps[:, 4, 0:P], eA, ident).then_inc(eA_ps, 1)
                if not last:
                    embed(1 - q, 12, 16)
                pe.wait_ge(etA_ready, i + 1)
                mm(ps[:, 5, 0:DIM], etA, xnA[:, q, :], start=True, stop=True).then_inc(pvA_ps, 1)

            pe.wait_ge(x_in[0], 16)
            embed(0, 0, PATCH)
            tile_a(0, 0, j=0, first=True)
            tile_a(1, 1, j=0)
            with pe.Fori(1, NTILE // 2 - 1) as j:
                for q in range(2):
                    tile_a(2 * j + q, q, j=j)
            tile_a(NTILE - 2, 0, j=NTILE // 2 - 1)
            tile_a(NTILE - 1, 1, j=NTILE // 2 - 1, last=True)
            pe.wait_ge(h2_ready, NTILE)
            transpose_h()

            def norm(kind, source, count):
                S = LN[kind]
                pe.wait_ge(source, count)
                with pe.Fori(0, NBLK) as i:
                    for c in range(KC):
                        ins = mm(ps[:, 0, 0:BLK], meanw, hT[:, c, bass.ds(i * BLK, BLK)], start=c == 0, stop=c == KC - 1)
                    ins.then_inc(S["mean_ps"], 1)
                    pe.wait_ge(S["sq_ready"], i + 1)
                    for c in range(KC):
                        ins = mm(ps[:, 1, 0:BLK], meanw, sqL[:, c, :], start=c == 0, stop=c == KC - 1)
                    ins.then_inc(S["var_ps"], 1)

            pe.wait_ge(constb_ready, 1)
            norm("B", hT_ready, NTILE)
            pe.wait_ge(win_in, 32)
            with pe.Fori(0, NBLK) as i:
                pe.wait_ge(FB["x_ready"], i + 1)

                def down(c):
                    pe.wait_ge(FB["act_ready"], i * NCH + c + 1)
                    for o in range(KC):
                        ins = mm(ps[:, 4 + o, 0:BLK], wout[:, c, o * P:(o + 1) * P], accB[:, c % 4, :], start=c == 0, stop=c == NCH - 1)
                    return ins

                for c in range(NCH):
                    if c >= 4:
                        pe.wait_ge(FB["act_ready"], i * NCH + c - 3)
                    for k in range(KC):
                        ins = mm(ps[:, c % 4, 0:BLK], win[:, k, c * P:(c + 1) * P], xB[:, k, :], start=k == 0, stop=k == KC - 1)
                    ins.then_inc(FB["l_ps"], 1)
                    if c == 1:
                        pe.wait_ge(FB["dec_ready"], 8 * i + 1)
                        mm(ps[:, 6, 0:BLK], constb[:, B_ANC0:B_ANC0 + P], maskB[:, 0, :], start=True, stop=True)
                        mm(ps[:, 7, 0:BLK], constb[:, B_ANC1:B_ANC1 + P], maskB[:, 0, :], start=True, stop=True).then_inc(FB["v_ps"], 1)
                    if c >= 2:
                        down(c - 2)
                down(NCH - 2)
                down(NCH - 1).then_inc(FB["o_ps"], 1)

            def attention(kind):
                S = AT[kind]
                pairs = 2 if kind == "C" else 5
                w, voff = (w1q, 512) if kind == "C" else (w2q, 1280)
                wo, nout = (w1o, 1) if kind == "C" else (w2o, 4)
                pe.wait_ge(w1_in if kind == "C" else w2_in, 32 if kind == "C" else 48)
                with pe.Fori(0, NBLK) as i:
                    pe.wait_ge(S["x_ready"], i + 1)
                    for p in range(pairs):
                        if p >= 2:
                            pe.wait_ge(S["t_ready"], i * pairs + p - 1)
                        for half in range(2):
                            col = (2 * p + half) * P
                            for k in range(KC):
                                ins = mm(ps[:, 2 * (p % 2) + half, 0:BLK], w[:, k, col:col + P], xC[:, k, :, 0:NPATCH],
                                         start=k == 0, stop=k == KC - 1)
                        ins.then_inc(S["proj_ps"], 1)
                        if p == 1:
                            for n in range(NQ):
                                for k in range(KC):
                                    x = xC[:, k, 4 * n:4 * n + 4, :].rearrange("p b n -> p (b n)")
                                    ins = mm(ps[:, 6 + n // 2, (n % 2) * DIM:(n % 2 + 1) * DIM], x, w[:, k, voff:voff + DIM],
                                             start=k == 0, stop=k == KC - 1)
                            ins.then_inc(S["v_ps"], 1)
                    pe.wait_ge(S["v_ready"], i + 1)
                    pe.wait_ge(S["qk_pool"], (i + 1) * pairs)
                    if kind == "C":
                        pe.wait_ge(S["qk_ready"], i + 1)
                    for g in range(4):
                        rows = slice(32 * g, 32 * g + 32)
                        s_ps = ps[0:96, 4 + g, :].rearrange("p (b n) -> p b n", n=32)
                        mm(s_ps[:, :, 0:NPATCH], constb[0:96, B_IDENT:B_IDENT + 96],
                           bc(constb[0:96, B_CAUSAL:B_CAUSAL + NPATCH], 1, BB), start=True, stop=False, skip_group_check=True)
                        for b in range(BB):
                            for half in range(2):
                                ins = mm(s_ps[:, b, 0:NPATCH], qC[rows, half, b * 96:(b + 1) * 96],
                                         kC[rows, half, b * NPATCH:(b + 1) * NPATCH], start=False,
                                         stop=b == BB - 1 and half == 1, skip_group_check=True)
                        ins.then_inc(S["s_ps"], 1)
                    for g in range(4):
                        pe.wait_ge(S["p_ready"], 4 * i + g + 1)
                        for n in range(NQ):
                            ins = tr(ps[:, g, n * 96:(n + 1) * 96],
                                     pC[0:96, g, 4 * n:4 * n + 4, :].rearrange("p b n -> p (b n)"), ident[0:96, 0:96])
                        ins.then_inc(S["pt_ps"], 1)
                    for hp in range(2):
                        pe.wait_ge(S["pt_ready"], 4 * i + (2 if hp == 0 else 4))
                        for n in range(NQ):
                            for s in range(2):
                                g = 2 * hp + s
                                for j in range(4):
                                    rows = slice(32 * j, 32 * j + 32)
                                    dst = ps[64 * s:64 * s + 64, (4 if hp == 0 else 0) + j, 0:BLK].rearrange(
                                        "p (a n q) -> p a n q", a=4, n=NQ)[:, :, n, :]
                                    ins = mm(dst, vC[rows, n, 64 * g:64 * g + 64], ptC[rows, g, n * 96:(n + 1) * 96],
                                             start=True, stop=True)
                        ins.then_inc(S["y_ps"], 1)
                    pe.wait_ge(S["y_ready"], 2 * i + 2)
                    for o in range(KC):
                        for m in range(2 * nout):
                            hp, a = m // nout, m % nout
                            y = yC[:, hp, a, :].rearrange("p (j n q) -> p n j q", j=4, n=NQ)
                            ins = mm(ps[:, 4 + o, 0:BLK], wo[:, m, o * P:(o + 1) * P], y, start=m == 0, stop=m == 2 * nout - 1)
                    ins.then_inc(S["o_ps"], 1)

            norm("C", FB["h_ready"], NBLK)
            attention("C")
            norm("E", AT["C"]["h_ready"], NBLK)
            attention("E")
            with pe.Fori(0, NBLK) as i:
                pe.wait_ge(MO["sq_ready"], i + 1)
                for c in range(KC):
                    ins = mm(ps[:, 0, 0:BLK], meanw, sqF[:, c, :], start=c == 0, stop=c == KC - 1)
                ins.then_inc(MO["ms_ps"], 1)
                pe.wait_ge(MO["xf_ready"], i + 1)
                for t in range(3):
                    for c in range(KC):
                        ins = tr(ps[:, 3 + t // 2, (t % 2) * DIM + c * P:(t % 2) * DIM + (c + 1) * P], xfF[:, c, t * P:(t + 1) * P], ident)
                ins.then_inc(MO["xfT_ps"], 1)
                for t in range(3):
                    for c in range(KC):
                        mm(ps[:, 2, t * 8:t * 8 + 8], xfF[:, c, t * P:(t + 1) * P], wr[:, c, :], start=c == 0, stop=False)
                    mm(ps[:, 2, t * 8:t * 8 + 8], const[0:1, C_ONES:C_ONES + P], rbias[:], start=False, stop=True)
                for t in range(3):
                    for c in range(KC):
                        ins = tr(ps[:, 5 + t // 2, (t % 2) * DIM + c * P:(t % 2) * DIM + (c + 1) * P], rF[:, c, t * P:(t + 1) * P], ident)
                ins.then_inc(MO["r_ps"], 1)

            def count(dst, pick, k):
                mm(dst, constb[:, B_TRI:B_TRI + P], pick, start=True, stop=False, skip_group_check=True)
                for t in range(NTILE - 1):
                    rest = NTILE - 1 - t
                    if k:
                        for kk in range(2):
                            ins = mm(dst[:, kk, t + 1:, :], constb[:, B_ONES:B_ONES + P], bc(pick[:, kk, t, :], 1, rest), start=False,
                                     stop=t == NTILE - 2 and kk == 1, skip_group_check=True)
                    else:
                        ins = mm(dst[:, t + 1:, :], constb[:, B_ONES:B_ONES + P], bc(pick[:, t, :], 1, rest), start=False,
                                 stop=t == NTILE - 2, skip_group_check=True)
                return ins

            pe.wait_ge(MO["oh_ready"], 1)
            count(ps[:, 0, 0:192].rearrange("p (k t e) -> p k t e", k=2, t=NTILE), ohB, True).then_inc(MO["cum_ps"], 1)
            pe.wait_ge(MO["ohm_ready"], 1)
            count(ps[:, 1, 0:96].rearrange("p (t e) -> p t e", t=NTILE), ohmB, False).then_inc(MO["rank_ps"], 1)
            pe.wait_ge(MO["slot_ready"], 1)

            with pe.Fori(0, EXPERTS // 2) as g:
                for q in range(2):
                    e = 2 * g + q
                    pe.wait_ge(MO["xs_in"][q], 16 * g + 16)
                    for s in range(3):
                        for c in range(KC):
                            ins = tr(ps[:, s // 2, (s % 2) * DIM + c * P:(s % 2) * DIM + (c + 1) * P], xsH[:, q, s, c * P:(c + 1) * P], ident)
                    ins.then_inc(MO["xt_ps"], 1)
                    pe.wait_ge(MO["we_in"][q], 16 * g + 16)
                    pe.wait_ge(MO["xt_ready"], e + 1)
                    for j in range(4):
                        if j >= 2:
                            pe.wait_ge(MO["prod_ready"], e * 4 + j - 1)
                        for m, w in enumerate((w2e[q], w1e[q])):
                            for k in range(KC):
                                ins = mm(ps[:, 2 + 2 * (j % 2) + m, 0:SLOTS], w[:, k, j * P:(j + 1) * P], xtH[:, k, :],
                                         start=k == 0, stop=k == KC - 1)
                        ins.then_inc(MO["up_ps"], 1)
                    for s in range(3):
                        pe.wait_ge(MO["g_ready"], e * 4 + 4)
                        if s == 2:
                            pe.wait_ge(MO["ys_ready"], e * 3 + 1)
                        for j in range(4):
                            ins = mm(ps[:, 6 + s % 2, 0:DIM], gH[:, j, s * P:(s + 1) * P], w3e[q][:, j, :], start=j == 0, stop=j == 3)
                        ins.then_inc(MO["y_ps"], 1)


def kernel(**inputs):
    import concourse.bacc as bacc
    from concourse.bass_utils import run_bass_kernel_spmd

    arrays = _layout(inputs)
    nc = bacc.Bacc("TRN2", target_bir_lowering=False, num_devices=1)
    io = {n: nc.dram_tensor(f"in_{n}", a.shape, mybir.dt.from_np(a.dtype), kind="ExternalInput").ap() for n, a in arrays.items()}
    out = nc.dram_tensor("out", [TOK, DIM], F32, kind="ExternalOutput").ap()
    tower(nc, io, out)
    r = run_bass_kernel_spmd(nc, [{f"in_{n}": a for n, a in arrays.items()}], core_ids=[0])
    return r.results[0]["out"].reshape(BATCH, NPATCH, DIM)


def _layout(inputs):
    g = {k: np.asarray(a) for k, a in inputs.items()}
    cols = lambda w: np.ascontiguousarray(w.reshape(-1, P, w.shape[1]).transpose(1, 0, 2))
    c, cb = _constants()
    rows = _ffn_rows()
    pad = lambda a: np.concatenate([a, np.zeros((1,) + a.shape[1:], a.dtype)])
    win = pad(g["L0_ffn_W_in"])[rows]
    wout = pad(np.ascontiguousarray(g["L0_ffn_W_out"].T))[rows]
    bin_ = pad(g["L0_ffn_b_in"])[rows].reshape(NCH, P).T
    two = lambda a: a.reshape(KC, P).T
    vecs = np.ascontiguousarray(np.concatenate([bin_, two(g["L1_ffn_g1"]), two(g["L1_ffn_g2"]), two(g["L1_attn_bproj"])], 1))
    r1 = np.arange(HEADS)[:, None] * HD1 + 2 * np.arange(8)[None, :]
    even, odd = r1.reshape(-1), r1.reshape(-1) + 1
    wqkv = g["L1_attn_Wqkv"].T
    w1q = np.concatenate([wqkv[:, even], wqkv[:, odd], wqkv[:, DIM + even], wqkv[:, DIM + odd], wqkv[:, 2 * DIM:]], 1)
    half = lambda h, s: (np.asarray(h)[:, None] * HD2 + 32 * s + np.arange(32)[None, :]).reshape(-1)
    wq, wk_, wv = g["L1_ffn_wq"], g["L1_ffn_wk"], g["L1_ffn_wv"]
    parts = []
    for q in range(4):
        heads = [4 * q + h for h in range(HKV)]
        parts += [wq[:, half(heads, 0)], wq[:, half(heads, 1)]]
    parts += [wk_[:, half(range(HKV), 0)], wk_[:, half(range(HKV), 1)], wv]
    wo = g["L1_ffn_wo"].reshape(4, 2, 2, HD2, DIM).transpose(1, 0, 2, 3, 4).reshape(8, P, DIM)
    ex = lambda w: w.reshape(EXPERTS, -1, P, w.shape[2]).transpose(0, 2, 1, 3).reshape(EXPERTS, P, -1)
    wexp = np.concatenate([ex(g["L1_ffn_w1"]), ex(g["L1_ffn_w2"]), ex(g["L1_ffn_w3"])], 2)
    xt = g["x"].transpose(2, 1, 0)[:, :8 * (NPATCH + 1)].reshape(IN_DIM, NPATCH + 1, 8, BATCH)
    return {
        "const": c, "constb": cb, "vecs": vecs, "rb": g["L1_ffn_router_b"].reshape(1, EXPERTS),
        "x": np.stack([xt[:, 2 * t:2 * t + 3].transpose(0, 2, 1, 3).reshape(IN_DIM, -1) for t in range(NTILE)]),
        "wtok": cols(g["L0_tok_W"]), "btok": g["L0_tok_b"].reshape(1, DIM),
        "pos": np.ascontiguousarray(g["L0_tok_pos_embed"][0, :NPATCH]),
        "win": cols(np.ascontiguousarray(win.T)), "wout": cols(wout),
        "w1q": cols(w1q), "w1o": cols(np.ascontiguousarray(g["L1_attn_Wproj"].T)),
        "w2q": cols(np.concatenate(parts, 1)), "w2o": np.ascontiguousarray(wo.transpose(1, 0, 2)),
        "wr": cols(g["L1_ffn_router_w"]), "wexp": np.ascontiguousarray(wexp),
    }
```

```python
from contextlib import ExitStack

import numpy as np

import concourse.bass as bass
from concourse import mybir
from concourse.alu_op_type import AluOpType as ALU

F32 = mybir.dt.float32
BF16 = mybir.dt.bfloat16
I32 = mybir.dt.int32
U32 = mybir.dt.uint32
ACT = mybir.ActivationFunctionType
AX = mybir.AxisListType

P = 128
BATCH, NPATCH, DIM = 64, 24, 256
SEQ, IN_DIM, PATCH, STRIDE = 202, 128, 16, 8
TOK = BATCH * NPATCH
KC = DIM // P
NTILE = TOK // P
BLK = 384
NBLK = TOK // BLK
BB = BLK // NPATCH
NQ = BB // 4
XROWS = PATCH + STRIDE
PAR, NODES, DEPTH = 8, 255, 7
NCH = 16
HEADS, HD1 = 16, 16
HKV, HD2 = 4, 64
EXPERTS, HID = 8, 512
CAP = TOK // 8
SLOTS = 2 * CAP
NSLOT = EXPERTS * SLOTS
LN_EPS, RMS_EPS = 1e-5, 1e-6
FAR = -1e30

C_IDENT = 0
C_MEAN = 128
C_BLOCKMASK = 256
C_COS1, C_SIN1, C_COS2, C_SIN2 = 384, 408, 432, 456
C_AMASK = 480
C_GMASK = 484
C_CNT = 488
C_HALF = 490
C_ONES = 491
C_IOTA = 619
C_DUMP = 627
C_EPS = 639
NCONST = 640
B_ANC0 = 0
B_ANC1 = 128
B_TRI = 256
B_ONES = 384
B_IDENT = 512
B_CAUSAL = 640
NCONSTB = 672


def _tree(node):
    out, level = [], (node + 1).bit_length() - 1
    k = node - (2 ** level - 1)
    while level:
        level, right, k = level - 1, k & 1, k >> 1
        out.append((2 ** level - 1 + k, right))
    return out


def _constants():
    c = np.zeros((P, NCONST), np.float32)
    c[:, C_IDENT:C_IDENT + P] = np.eye(P)
    c[:, C_MEAN:C_MEAN + P] = 1.0 / DIM
    blk = np.arange(P) // BATCH
    c[:, C_BLOCKMASK:C_BLOCKMASK + P] = np.where(blk[:, None] == blk[None, :], 0.0, FAR)
    t = np.arange(NPATCH, dtype=np.float32)
    f1 = (np.float32(1.0) / np.float32(10000.0) ** (np.arange(8, dtype=np.float32) / np.float32(8))).astype(np.float32)
    a1 = t[:, None] * f1[None, :]
    a1 = a1[:, np.arange(P) % 8].T
    c[:, C_COS1:C_COS1 + NPATCH], c[:, C_SIN1:C_SIN1 + NPATCH] = np.cos(a1), np.sin(a1)
    f2 = 10000.0 ** (-np.arange(0, HD2, 2, dtype=np.float32) / HD2)
    a2 = np.outer(t, f2).astype(np.float32)[:, np.arange(P) % 32].T
    c[:, C_COS2:C_COS2 + NPATCH], c[:, C_SIN2:C_SIN2 + NPATCH] = np.cos(a2), np.sin(a2)
    p = np.arange(P)
    for a in range(4):
        c[:, C_AMASK + a] = (p // 8) % 4 == a
        c[:, C_GMASK + a] = p // 32 == a
    rights = [sum(r for _, r in _tree(n)) for n in range(31)]
    c[:120, C_CNT] = [rights[q // 8] for q in range(120)]
    c[:, C_CNT + 1] = [rights[15 + q // 8] for q in range(P)]
    c[:, C_EPS] = LN_EPS
    c[:, C_HALF] = -0.5
    c[:, C_ONES:C_ONES + P] = 1.0
    c[:, C_IOTA:C_IOTA + 8] = np.arange(8)
    c[:, C_DUMP:C_DUMP + NTILE] = NSLOT + np.arange(NTILE)[None, :] * P + p[:, None]
    b = np.zeros((P, NCONSTB), np.float32)
    for q in range(120):
        for anc, right in _tree(q // 8):
            b[anc * 8 + q % 8, B_ANC0 + q] = 1 if right else -1
    for q in range(P):
        for anc, right in _tree(15 + q // 8):
            b[anc * 8 + q % 8, B_ANC1 + q] = 1 if right else -1
    b[:, B_TRI:B_TRI + P] = p[:, None] <= p[None, :]
    b[:, B_ONES:B_ONES + P] = 1.0
    b[:, B_IDENT:B_IDENT + P] = np.eye(P)
    key, query = (p % 32)[:, None], np.arange(32)[None, :]
    b[:, B_CAUSAL:B_CAUSAL + 32] = np.where((key < NPATCH) & (key <= query), 0.0, FAR)
    return c, b


def _ffn_rows():
    rows = -np.ones((NCH, P), np.int64)
    q = np.arange(120)
    rows[0, :120] = (q % 8) * NODES + q // 8
    q = np.arange(P)
    for c in range(1, NCH):
        r = c.bit_length() - 1
        node = 2 ** (4 + r) - 1 + (q // 8) * 2 ** r + (c - 2 ** r)
        rows[c] = (q % 8) * NODES + node
    return rows.reshape(-1)


class Chain:

    def __init__(self, eng, sem):
        self.eng, self.sem, self.base, self.n = eng, sem, 0, 0

    def turn(self, i, per):
        self.base, self.start, self.n, self.per = self.floor() + i * per, self.floor(), 0, per

    def floor(self):
        return self.base + self.n if isinstance(self.base, int) else self.start

    def end(self, times):
        assert self.n == self.per, (self.n, self.per)
        self.base, self.n = self.start + times * self.per, 0

    def link(self, ins):
        self.n += 1
        ins.then_inc(self.sem, 1)
        self.eng.wait_ge(self.sem, self.base + self.n)


def order(pairs):
    steps = [("rope", 0), ("sum", 0), ("weigh", 0), ("sum", 1), ("weigh", 1), ("rope", 1), ("sum", 2), ("weigh", 2),
             ("sum", 3), ("weigh", 3), ("rope", 2), ("turn", 0), ("turn", 1), ("rope", 3), ("turn", 2), ("turn", 3),
             ("rope", 4)]
    return [s for s in steps if s[0] != "rope" or s[1] < pairs]


def at_least(eng, sem, value):
    if not isinstance(value, int) or value > 0:
        eng.wait_ge(sem, value)


def bc(ap, axis, count):
    new = ap.unsqueeze(axis)
    shape = list(new.shape)
    shape[axis] = count
    return new.to_broadcast(shape)


def by_batch(ap):
    return ap.rearrange("p (b n) -> p b n", n=NPATCH)


def tower(nc, io, out):
    ctx = ExitStack()
    with ctx:
        def sb(name, shape, dt=F32):
            return ctx.enter_context(nc.sbuf_tensor(name, shape, dt))

        def sem(name):
            return ctx.enter_context(nc.semaphore(name))

        const = sb("const", [P, NCONST])
        constb = sb("constb", [P, NCONSTB], BF16)
        vecs = sb("vecs", [P, 22])
        negb = sb("negb", [P, NCH])
        rbias = sb("rbias", [1, EXPERTS])
        hT = sb("hT", [P, KC, TOK])
        dT = sb("dT", [P, KC, TOK])
        rstd = sb("rstd", [P, TOK])
        xf = sb("xf", [P, NTILE, DIM])
        res = sb("res", [P, NTILE, DIM])
        logit = sb("logit", [P, NTILE, EXPERTS])
        wbig = sb("wbig", [P, 8192])
        w1q = sb("w1q", [P, KC, 768])
        w1o = sb("w1o", [P, KC, DIM])
        w2q = sb("w2q", [P, KC, 1536])
        w2o = sb("w2o", [P, 8, DIM])
        wr = sb("wr", [P, KC, EXPERTS])
        nrm = sb("nrm", [P, 5, BLK])
        wk = sb("work", [P, 16080])
        ps = ctx.enter_context(nc.psum_tensor("ps", [P, 8, 512], F32))
        win = wbig[:, 0:4096].rearrange("p (k n) -> p k n", k=KC)
        wout = wbig[:, 4096:8192].rearrange("p (c n) -> p c n", c=NCH)

        def carve(*shapes):
            at, views = 0, []
            for s in shapes:
                n = int(np.prod(s))
                v = wk[:, at:at + n]
                if len(s) > 1:
                    names = "abcd"[:len(s)]
                    v = v.rearrange(f"p ({' '.join(names)}) -> p {' '.join(names)}",
                                    **{k: d for k, d in zip(names, s)})
                views.append(v)
                at += n
            assert at <= 16080, at
            return views

        constb32 = dT[:, 1, 0:NCONSTB]
        ident = const[:, C_IDENT:C_IDENT + P]
        meanw = const[:, C_MEAN:C_MEAN + P]

        (wtok, xring, posb, brow, hA, xnA, xnTA, smA, eA, etA, h2A, statA, mvA, varA, rsA, nbA, sumA, rinvA, idleA) = carve(
            (PATCH, DIM), (2, XROWS * BATCH), (NTILE, DIM), (DIM,), (2, DIM), (2, DIM), (KC, P), (P,), (P,), (P,),
            (DIM,), (6,), (2,), (1,), (1,), (1,), (1,), (1,), (1,))
        sqL, stdL, riL, varL = nrm[:, 0:2], nrm[:, 2], nrm[:, 3], nrm[:, 4]
        (xB, actB, accB, maskBf) = carve((KC, BLK), (4, BLK), (4, BLK), (NCH, BLK // 2))
        maskB = maskBf.bitcast(BF16)
        (xC, qC, kC, tC, rawC, yC, mxC, suC, riC, idleC) = carve(
            (KC, BB, 32), (2, 4 * BLK), (2, 4 * BB * 32), (2, 4, BLK), (4, BLK), (2, 4, BLK), (4, 16), (4, 16), (4, 16), (1,))
        vC = wbig[:, 0:4096].rearrange("p (b f) -> p b f", b=BB)
        pC = wbig[:, 4096:6144].rearrange("p (n s k) -> p n s k", n=NQ, k=32)
        sC = wbig[:, 6144:8192].rearrange("p (n s k) -> p n s k", n=NQ, k=32)

        def q_of(half, g):
            return qC[:, half, :].rearrange("p (b a n) -> p b a n", b=BB, a=4)[:, :, g, :]

        def k_of(half, a):
            return kC[:, half, :].rearrange("p (b a n) -> p b a n", b=BB, a=4)[:, :, a, 0:NPATCH]

        xfF, rF = (w1q[:].rearrange("p k n -> p (k n)")[:, i * 768:(i + 1) * 768].rearrange("p (k t) -> p k t", k=KC) for i in range(2))
        (top8, idx8f, e12, oh, pq, em, cumS, t96, tm, asg, mG, actG, rankG, slotf, wy, wx,
         slotS, slotG, xsH, xtH, aH, prodH, gH, ysH, ohm) = carve(
            (NTILE, 8), (NTILE, 8), (2, NTILE), (2, NTILE, 8 // 2), (2, NTILE),
            (2, NTILE, 8), (2, NTILE, 8), (2, NTILE, 8), (2, NTILE), (2, NTILE), (NTILE,), (NTILE,), (NTILE,), (2, NTILE),
            (2, NTILE), (2, NTILE), (NTILE,), (NTILE,), (2, 3, DIM), (KC, SLOTS), (2, SLOTS), (2, SLOTS), (4, SLOTS),
            (2, 3, DIM), (NTILE, 8 // 2))
        ohB = oh.rearrange("p k t e -> p (k t e)").bitcast(BF16).rearrange("p (k t e) -> p k t e", k=2, t=NTILE)
        ohmB = ohm.rearrange("p t e -> p (t e)").bitcast(BF16).rearrange("p (t e) -> p t e", t=NTILE)
        idx8 = idx8f.bitcast(U32)
        slotS, slotG = slotS.bitcast(I32), slotG.bitcast(I32)
        ygH = dT[:].rearrange("p k t -> p (k t)").rearrange("p (t f) -> p t f", f=DIM)
        xs_d = nc.dram_tensor("xs", [NSLOT + TOK, DIM], F32).ap()
        ys_d = nc.dram_tensor("ys", [NSLOT, DIM], F32).ap()
        wexp = [wbig[:, q * 3072:(q + 1) * 3072] for q in range(2)]
        w1e = [w[:, 0:1024].rearrange("p (k n) -> p k n", k=KC) for w in wexp]
        w2e = [w[:, 1024:2048].rearrange("p (k n) -> p k n", k=KC) for w in wexp]
        w3e = [w[:, 2048:3072].rearrange("p (k n) -> p k n", k=4) for w in wexp]

        vd, ad, gd = sem("dve_step"), sem("act_step"), sem("pool_step")
        const_in, wtok_in, win_in, w1_in, w2_in = (sem(n) for n in ("const_in", "wtok_in", "wffn_in", "watt1_in", "watt2_in"))
        pos_in, constb_ready = sem("pos_in"), sem("constb_ready")
        x_in = [sem("x_in0"), sem("x_in1")]
        posb_ready, tok_ps, hA_ready, var_ready, rstdA_ready, xn_ready = (
            sem(n) for n in ("posb_ready", "tok_ps", "hA_ready", "var_ready", "rstdA_ready", "xn_ready"))
        xnT_ps, xnT_ready, sA_ps, smA_ready, eA_ready, eA_ps, etA_ready, pvA_ps, h2_ready, h2_ps, hT_ready = (
            sem(n) for n in ("xnT_ps", "xnT_ready", "sA_ps", "smA_ready", "eA_ready", "eA_ps", "etA_ready", "pvA_ps",
                             "h2_ready", "h2_ps", "hT_ready"))

        LN = {k: {n: sem(f"ln{k}_{n}") for n in ("mean_ps", "d_ready", "sq_ready", "var_ps", "std_ready", "done",
                                                "ri_ready", "ms_ready", "rms_ready")}
              for k in "BCE"}
        FB = {n: sem(f"ffn_{n}") for n in ("x_ready", "l_ps", "dec_ready", "v_ps", "a_ready", "act_ready", "o_ps", "h_ready")}
        AT = {k: {n: sem(f"att{k}_{n}") for n in ("x_ready", "proj_ps", "t_ready", "qk_pool", "kx_ready", "qx_ready", "v_ps",
                                                 "v_ready", "s_ps", "st_ready", "sub_ready", "e_ready", "ri_ready",
                                                 "p_ready", "pt_ready", "y_ps", "y_ready", "o_ps", "h_ready", "zero_ready")}
              for k in "CE"}
        MO = {n: sem(f"moe_{n}") for n in ("r_ready", "std_ready", "xf_ready", "r_ps", "lg_ready", "diff_ready", "oh_ready",
                                          "cum_ps", "ohm_ready", "ex_ready", "rank_ps", "slot_ready", "a_ready",
                                          "prod_ready", "y_ps", "ys_ready", "yg_in", "out_ready", "sq_ready", "ms_ps",
                                          "lg_ps", "xf_out", "xt_ps", "xt_ready", "up_ps", "g_ready", "scattered")}
        MO["ys_out"] = [sem("moe_ys_out0"), sem("moe_ys_out1")]
        MO["xs_in"] = [sem("moe_xs_in0"), sem("moe_xs_in1")]
        MO["we_in"] = [sem("moe_we_in0"), sem("moe_we_in1")]
        zero_ready, zero_out, out_done = sem("zero_ready"), sem("zero_out"), sem("out_done")

        block = ctx.enter_context(nc.Block())

        @block.sync
        def _(sp):
            sp.dma_start(const[:], io["const"]).then_inc(const_in, 16)
            sp.dma_start(constb32, io["constb"]).then_inc(const_in, 16)
            sp.dma_start(vecs[:], io["vecs"]).then_inc(const_in, 16)
            sp.dma_start(rbias[:], io["rb"]).then_inc(const_in, 16)
            sp.dma_start(wtok, io["wtok"]).then_inc(wtok_in, 16)

            def load_x(t, q):
                at_least(sp, tok_ps, t - 1)
                sp.dma_start(xring[:, q, :], io["x"][bass.ds(t, 1)].rearrange("t p n -> (t p) n")).then_inc(x_in[q], 16)

            load_x(0, 0)
            load_x(1, 1)
            with sp.Fori(1, NTILE // 2) as j:
                for q in range(2):
                    load_x(2 * j + q, q)

            def load_expert(e, q):
                sp.dma_start(wexp[q], io["wexp"][bass.ds(e, 1)].rearrange("e p n -> (e p) n")).then_inc(MO["we_in"][q], 16)

            def load_slots(e, q):
                sp.dma_start(xsH[:, q], xs_d[bass.ds(e * SLOTS, SLOTS), :].rearrange("(s p) f -> p s f", p=P)).then_inc(MO["xs_in"][q], 16)

            sp.wait_ge(AT["E"]["h_ready"], NBLK)
            for q in range(2):
                load_expert(q, q)
            sp.wait_ge(MO["scattered"], 16 * NTILE)
            for q in range(2):
                load_slots(q, q)
            with sp.Fori(1, EXPERTS // 2) as g:
                for q in range(2):
                    sp.wait_ge(MO["y_ps"], 6 * g - 6 + 3 * q + 3)
                    load_expert(2 * g + q, q)
                    load_slots(2 * g + q, q)
            for t in range(NTILE):
                sp.wait_ge(MO["out_ready"], t + 1)
                sp.dma_start(out[t * P:(t + 1) * P, :], res[:, t, :]).then_inc(out_done, 16)
            sp.wait_ge(out_done, 16 * NTILE)

        @block.gpsimd
        def _(pool):
            pool.dma_start(posb[0:64, :, :], io["pos"][0:NPATCH:2, :].unsqueeze(0).to_broadcast([64, NTILE, DIM])).then_inc(pos_in, 16)
            pool.dma_start(posb[64:128, :, :], io["pos"][1:NPATCH:2, :].unsqueeze(0).to_broadcast([64, NTILE, DIM])).then_inc(pos_in, 16)
            pool.dma_start(brow, io["btok"].to_broadcast([P, DIM])).then_inc(pos_in, 16)
            for dst, name in ((win, "win"), (wout, "wout")):
                pool.dma_start(dst, io[name]).then_inc(win_in, 16)
            for dst, name in ((w1q, "w1q"), (w1o, "w1o")):
                pool.dma_start(dst[:], io[name]).then_inc(w1_in, 16)
            for dst, name in ((w2q, "w2q"), (w2o, "w2o"), (wr, "wr")):
                pool.dma_start(dst[:], io[name]).then_inc(w2_in, 16)
            pool.wait_ge(const_in, 64)
            ch = Chain(pool, gd)
            nc.gpsimd.memset(dT[:, 0, 0:DIM], 0.0).then_inc(zero_ready, 1)
            pool.wait_ge(zero_ready, 1)
            pool.dma_start(xs_d[0:NSLOT, :].rearrange("(r p) f -> p r f", p=P), bc(dT[:, 0, 0:DIM], 1, NSLOT // P)).then_inc(zero_out, 16)

            def rstd_a(i):
                pool.wait_ge(var_ready, i + 1)
                ch.link(nc.gpsimd.tensor_tensor(varA, mvA[:, 1:2], const[:, C_EPS:C_EPS + 1], ALU.add))
                nc.gpsimd.tensor_tensor(rsA, varA, const[:, C_HALF:C_HALF + 1], ALU.pow).then_inc(rstdA_ready, 1)

            for i in (0, 1):
                rstd_a(i)
            with pool.Fori(2, NTILE) as i:
                ch.turn(i - 2, 1)
                rstd_a(i)
            ch.end(NTILE - 2)


            def attention(kind, nk):
                S = AT[kind]
                pairs = 2 if kind == "C" else 5

                def rope(i, p):
                    pool.wait_ge(S["t_ready"], i * pairs + p + 1)
                    for half, (op, a, b) in enumerate(((ALU.subtract, 0, 1), (ALU.add, 2, 3))):
                        if kind == "C":
                            dst = by_batch(rawC[:, 2 * p + half, :])
                        else:
                            dst = by_batch(rawC[:, 2 + half, :]) if p == pairs - 1 else q_of(half, p)
                        ins = nc.gpsimd.tensor_tensor(dst, by_batch(tC[:, p % 2, a, :]), by_batch(tC[:, p % 2, b, :]), op)
                    ins.then_inc(S["qk_pool"], 1)

                def weigh(i, n):
                    pool.wait_ge(S["ri_ready"], 4 * i + n + 1)
                    nc.gpsimd.tensor_tensor(pC[:, n, :, 0:NPATCH], pC[:, n, :, 0:NPATCH], bc(riC[:, n, :], 2, NPATCH),
                                            ALU.mult).then_inc(S["p_ready"], 1)

                def body(i, nxt):
                    for step in order(pairs):
                        if step[0] == "rope" and nxt:
                            rope(i + 1, step[1])
                        if step[0] == "weigh":
                            weigh(i, step[1])
                    if nk == "E":
                        scale_rms(i - 1)

                def scale_rms(m):
                    if isinstance(m, int) and m < 0:
                        return
                    S = LN["E"]
                    pool.wait_ge(S["ri_ready"], m + 1)
                    ch.link(nc.gpsimd.tensor_tensor(varL, varL, riL, ALU.mult))
                    nc.gpsimd.tensor_tensor(varL, varL, riL, ALU.mult).then_inc(S["ms_ready"], 1)

                if kind == "C":
                    pool.wait_ge(FB["h_ready"], NBLK)
                    nc.gpsimd.memset(kC, 0.0)
                    nc.gpsimd.memset(pC, 0.0)
                else:
                    pool.wait_ge(AT["C"]["h_ready"], NBLK)
                nc.gpsimd.memset(vC, 0.0).then_inc(S["zero_ready"], 1)
                for p in range(pairs):
                    rope(0, p)
                    if p == 0 and kind == "E":
                        scale_rms(3)
                body(0, True)
                with pool.Fori(1, NBLK - 1) as i:
                    ch.turn(i - 1, 1 if nk == "E" else 0)
                    body(i, True)
                ch.end(NBLK - 2)
                body(NBLK - 1, False)

            attention("C", "E")
            attention("E", None)
            pool.wait_ge(MO["slot_ready"], 1)
            pool.wait_ge(MO["xf_out"], NBLK)
            pool.wait_ge(zero_out, 16)
            for t in range(NTILE):
                pool.indirect_dma_start(xs_d, bass.IndirectOffsetOnAxis(ap=slotS[:, t:t + 1], axis=0), xf[:, t, :], None).then_inc(MO["scattered"], 16)
            with pool.Fori(0, EXPERTS // 2) as g:
                for q in range(2):
                    pool.wait_ge(MO["ys_ready"], 6 * g + 3 * q + 3)
                    pool.dma_start(ys_d[bass.ds((2 * g + q) * SLOTS, SLOTS), :].rearrange("(s p) f -> p s f", p=P), ysH[:, q]).then_inc(MO["ys_out"][q], 16)
            for q in range(2):
                pool.wait_ge(MO["ys_out"][q], 16 * (EXPERTS // 2))
            for t in range(NTILE):
                pool.indirect_dma_start(ygH[:, t, :], None, ys_d, bass.IndirectOffsetOnAxis(ap=slotG[:, t:t + 1], axis=0)).then_inc(MO["yg_in"], 16)

        @block.vector
        def _(dve):
            v = nc.vector
            ch = Chain(dve, vd)
            dve.wait_ge(const_in, 64)
            ch.link(v.tensor_scalar(negb[:], vecs[:, 0:NCH], -1.0, None, ALU.mult))
            v.tensor_copy(constb[:], constb32).then_inc(constb_ready, 1)
            dve.wait_ge(pos_in, 48)
            v.tensor_tensor(posb, posb, bc(brow, 1, NTILE), ALU.add).then_inc(posb_ready, 1)
            dve.wait_ge(posb_ready, 1)

            def embed(i, q):
                dve.wait_ge(tok_ps, i + 1)
                v.tensor_tensor(hA[:, q, :], ps[:, q, 0:DIM], posb[:, bass.ds(i, 1), :].rearrange("p t f -> p (t f)"),
                                ALU.add).then_inc(hA_ready, 1)
                dve.wait_ge(hA_ready, i + 1)
                ch.link(v.bn_stats(statA, hA[:, q, :]))
                v.memset(idleA, 0.0)
                v.bn_aggr(mvA, statA).then_inc(var_ready, 1)
                dve.wait_ge(rstdA_ready, i + 1)
                v.tensor_scalar(xnA[:, q, :], hA[:, q, :], mvA[:, 0:1], rsA, ALU.subtract, ALU.mult).then_inc(xn_ready, 1)

            def soft_a(i):
                dve.wait_ge(sA_ps, i + 1)
                ch.link(v.scalar_tensor_tensor(smA, ps[:, 3, 0:P], 1.0 / 16, const[:, C_BLOCKMASK:C_BLOCKMASK + P],
                                               ALU.mult, ALU.add))
                v.tensor_reduce(nbA, smA, AX.X, ALU.max, negate=True).then_inc(smA_ready, 1)

            def out_a(i, q):
                dve.wait_ge(pvA_ps, i + 1)
                ch.link(v.reciprocal(rinvA, sumA))
                v.scalar_tensor_tensor(h2A, ps[:, 5, 0:DIM], rinvA, hA[:, q, :], ALU.mult, ALU.add).then_inc(h2_ready, 1)

            embed(0, 0)
            PER_A = 3

            def tile_a(i, q, last=False):
                soft_a(i)
                if not last:
                    embed(i + 1, 1 - q)
                out_a(i, q)

            for i in (0, 1):
                tile_a(i, i)
            with dve.Fori(1, NTILE // 2 - 1) as j:
                ch.turn(j - 1, 2 * PER_A)
                for q in range(2):
                    tile_a(2 * j + q, q)
            ch.end(NTILE // 2 - 2)
            for i in (NTILE - 2, NTILE - 1):
                tile_a(i, i % 2, last=i == NTILE - 1)

            def center(kind, m, bank):
                S, cols = LN[kind], bass.ds(m * BLK, BLK)
                dve.wait_ge(S["mean_ps"], m + 1)
                v.tensor_tensor(dT[:, :, cols], hT[:, :, cols], bc(ps[:, bank, 0:BLK], 1, KC),
                                ALU.subtract).then_inc(S["d_ready"], 1)

            def invert(kind, m):
                S, cols = LN[kind], bass.ds(m * BLK, BLK)
                dve.wait_ge(S["std_ready"], m + 1)
                if kind == "E":
                    v.reciprocal(riL, stdL).then_inc(S["ri_ready"], 1)
                    dve.wait_ge(S["ri_ready"], m + 1)
                    v.tensor_tensor(dT[:, :, cols], dT[:, :, cols], bc(riL, 1, KC), ALU.mult)
                    dve.wait_ge(S["rms_ready"], m + 1)
                v.memset(idleC, 0.0)
                v.reciprocal(rstd[:, cols], stdL).then_inc(S["done"], 1)

            dve.wait_ge(hT_ready, NTILE)
            dve.wait_ge(zero_out, 16)
            center("B", 0, 6)
            invert("B", 0)

            def feed(i):
                cols = bass.ds(i * BLK, BLK)
                static = isinstance(i, int)
                dve.wait_ge(LN["B"]["done"], i + 1)
                v.tensor_tensor(xB, dT[:, :, cols], bc(rstd[:, cols], 1, KC), ALU.mult).then_inc(FB["x_ready"], 1)
                for c in range(NCH):
                    l_ps = ps[:, c % 4, 0:BLK]
                    if c < 8:
                        dve.wait_ge(FB["l_ps"], i * NCH + c + 1)
                    if c == 0:
                        v.tensor_scalar(maskB[:, 0, :], l_ps, negb[:, 0:1], None, ALU.is_gt).then_inc(FB["dec_ready"], 1)
                        dve.wait_ge(FB["v_ps"], i + 1)
                        ch.link(v.tensor_scalar(maskB[:, 1, :], ps[:, 7, 0:BLK], const[:, C_CNT + 1:C_CNT + 2], None,
                                                ALU.is_equal))
                        dve.wait_ge(FB["a_ready"], i * NCH + c + 1)
                        v.scalar_tensor_tensor(accB[:, 0, :], ps[:, 6, 0:BLK], const[:, C_CNT:C_CNT + 1], actB[:, 0, :],
                                               ALU.is_equal, ALU.mult).then_inc(FB["act_ready"], 1)
                        continue
                    if c < 8:
                        v.scalar_tensor_tensor(maskB[:, 2 * c + 1, :], l_ps, negb[:, c:c + 1], maskB[:, c, :],
                                               ALU.is_gt, ALU.mult).then_inc(FB["dec_ready"], 1)
                        dve.wait_ge(FB["dec_ready"], 8 * i + c + 1)
                        ch.link(v.tensor_tensor(maskB[:, 2 * c, :], maskB[:, c, :], maskB[:, 2 * c + 1, :], ALU.subtract))
                    dve.wait_ge(FB["a_ready"], i * NCH + c + 1)
                    v.tensor_tensor(accB[:, c % 4, :], actB[:, c % 4, :], maskB[:, c, :], ALU.mult).then_inc(FB["act_ready"], 1)
                    if not static or i < NBLK - 1:
                        if c == 5:
                            center("B", i + 1, 6)
                        if c == 9:
                            invert("B", i + 1)
                    if not static or i > 0:
                        if c == 10:
                            center("C", i - 1, 6)
                        if c == 14:
                            invert("C", i - 1)
                dve.wait_ge(FB["o_ps"], i + 1)
                v.tensor_tensor(hT[:, :, cols], hT[:, :, cols], ps[:, 4:6, 0:BLK], ALU.add).then_inc(FB["h_ready"], 1)

            feed(0)
            with dve.Fori(1, NBLK - 1) as i:
                ch.turn(i - 1, 8)
                feed(i)
            ch.end(NBLK - 2)
            feed(NBLK - 1)

            def attention(kind, nk):
                S = AT[kind]
                pairs = 2 if kind == "C" else 5
                cos0, sin0 = (C_COS1, C_SIN1) if kind == "C" else (C_COS2, C_SIN2)
                cos = bc(const[:, cos0:cos0 + NPATCH], 1, BB)
                sin = bc(const[:, sin0:sin0 + NPATCH], 1, BB)

                def scaled_x(i):
                    cols = bass.ds(i * BLK, BLK)
                    dve.wait_ge(LN[kind]["done"], i + 1)
                    at_least(dve, S["v_ps"], i)
                    for c in range(KC):
                        dst = xC[:, c, :, 0:NPATCH]
                        if kind == "C":
                            ins = v.tensor_tensor(dst, by_batch(dT[:, c, cols]), by_batch(rstd[:, cols]), ALU.mult)
                        else:
                            ins = v.scalar_tensor_tensor(dst, by_batch(dT[:, c, cols]), vecs[:, 16 + c:17 + c],
                                                         by_batch(rstd[:, cols]), ALU.mult, ALU.mult)
                    ins.then_inc(S["x_ready"], 1)

                def rope(i, p):
                    dve.wait_ge(S["proj_ps"], i * pairs + p + 1)
                    at_least(dve, S["qk_pool"], i * pairs + p - 1)
                    bank = 2 * ((p + 1) % 2)
                    first, second = (by_batch(ps[:, bank + h, 0:BLK]) for h in range(2))
                    for k, (src, tab) in enumerate(((first, cos), (second, sin), (second, cos), (first, sin))):
                        ins = v.tensor_tensor(by_batch(tC[:, p % 2, k, :]), src, tab, ALU.mult)
                    ins.then_inc(S["t_ready"], 1)

                def spread_k(i):
                    dve.wait_ge(S["qk_pool"], (i + 1) * pairs)
                    col = C_AMASK if kind == "C" else C_GMASK
                    for half in range(2):
                        for a in range(4):
                            ins = v.tensor_scalar(k_of(half, a), by_batch(rawC[:, 2 + half, :]), const[:, col + a:col + a + 1],
                                                  None, ALU.mult)
                    ins.then_inc(S["kx_ready"], 1)

                def scores(i, n):
                    dve.wait_ge(S["s_ps"], 4 * i + n + 1)
                    v.transpose(sC[:, n].rearrange("p s k -> p (s k)"), ps[:, 4 + n, :]).then_inc(S["st_ready"], 1)
                    dve.wait_ge(S["st_ready"], 4 * i + n + 1)
                    s_n = sC[:, n, :, 0:NPATCH]
                    ch.link(v.tensor_reduce(mxC[:, n, :], s_n, AX.X, ALU.max))
                    v.tensor_tensor(s_n, s_n, bc(mxC[:, n, :], 2, NPATCH), ALU.subtract).then_inc(S["sub_ready"], 1)

                def total(i, n):
                    dve.wait_ge(S["e_ready"], 4 * i + n + 1)
                    ch.link(v.tensor_reduce(suC[:, n, :], pC[:, n, :, 0:NPATCH], AX.X, ALU.add))
                    v.reciprocal(riC[:, n, :], suC[:, n, :]).then_inc(S["ri_ready"], 1)

                def turn_back(i, n):
                    dve.wait_ge(S["p_ready"], 4 * i + n + 1)
                    v.transpose(sC[:, n].rearrange("p s k -> p (s k)"), pC[:, n].rearrange("p s k -> p (s k)")).then_inc(S["pt_ready"], 1)

                def body(i, nxt):
                    static = isinstance(i, int)
                    cols = bass.ds(i * BLK, BLK)
                    if nxt:
                        scaled_x(i + 1)
                    for n in range(NQ):
                        scores(i, n)
                    more = nk == "E" and (not static or i > 0)
                    if more:
                        center("E", i - 1, 0)
                    if kind == "E" and (not static or i > 0):
                        moe_input(i - 1)
                    for what, n in order(pairs):
                        if what == "rope" and nxt:
                            rope(i + 1, n)
                        elif what == "sum":
                            total(i, n)
                        elif what == "turn":
                            turn_back(i, n)
                    if nxt:
                        spread_k(i + 1)
                    if more:
                        invert("E", i - 1)
                    if kind == "E" and (not static or i > 0):
                        moe_logits(i - 1)
                    dve.wait_ge(S["o_ps"], i + 1)
                    if kind == "C":
                        for c in range(KC):
                            ins = v.scalar_tensor_tensor(hT[:, c, cols], ps[:, 2 + c, 0:BLK], vecs[:, 20 + c:21 + c], hT[:, c, cols],
                                                         ALU.add, ALU.add)
                        ins.then_inc(S["h_ready"], 1)
                    else:
                        v.tensor_tensor(dT[:, :, cols], dT[:, :, cols], ps[:, 2:4, 0:BLK], ALU.add).then_inc(S["h_ready"], 1)

                if kind == "C":
                    ch.link(v.memset(xC, 0.0))
                scaled_x(0)
                center(kind, 3, 0)
                rope(0, 0)
                for p in range(1, pairs):
                    if p == 1:
                        invert(kind, 3)
                    rope(0, p)
                dve.wait_ge(S["zero_ready"], 1)
                spread_k(0)
                body(0, True)
                with dve.Fori(1, NBLK - 1) as i:
                    ch.turn(i - 1, 8 + (1 if kind == "E" else 0))
                    body(i, True)
                ch.end(NBLK - 2)
                body(NBLK - 1, False)

            def moe_input(m):
                cols = bass.ds(m * BLK, BLK)
                dve.wait_ge(AT["E"]["h_ready"], m + 1)
                v.tensor_tensor(rF, hT[:, :, cols], dT[:, :, cols], ALU.add)
                dve.wait_ge(MO["std_ready"], m + 1)
                ch.link(v.reciprocal(riL, stdL))
                for c in range(KC):
                    ins = v.scalar_tensor_tensor(xfF[:, c, :], dT[:, c, cols], vecs[:, 18 + c:19 + c], riL, ALU.mult, ALU.mult)
                ins.then_inc(MO["xf_ready"], 1)

            def moe_logits(m):
                dve.wait_ge(MO["lg_ps"], m + 1)
                v.tensor_copy(logit[:, bass.ds(3 * m, 3), :], ps[:, 3, DIM:DIM + 24].rearrange("p (t e) -> p t e", e=8)).then_inc(MO["lg_ready"], 1)
                dve.wait_ge(MO["r_ps"], m + 1)
                v.tensor_copy(res[:, bass.ds(3 * m, 2), :], ps[:, 2, :].rearrange("p (t f) -> p t f", f=DIM))
                v.tensor_copy(res[:, bass.ds(3 * m + 2, 1), :], ps[:, 3, 0:DIM].rearrange("p (t f) -> p t f", f=DIM)).then_inc(MO["r_ready"], 1)

            attention("C", "E")
            attention("E", None)
            moe_input(3)
            moe_logits(3)
            dve.wait_ge(MO["lg_ready"], NBLK)

            for t in range(NTILE):
                ins = v.max(top8[:, t, :], logit[:, t, :])
            ch.link(ins)
            for t in range(NTILE):
                ins = v.max_index(idx8[:, t, :], top8[:, t, :], logit[:, t, :])
            v.tensor_tensor(pq[:, 1, :], top8[:, :, 1], top8[:, :, 0], ALU.subtract).then_inc(MO["diff_ready"], 1)
            dve.wait_ge(MO["diff_ready"], 1)
            ch.link(v.tensor_copy(e12, idx8[:, :, 0:2].rearrange("p t k -> p k t")))
            iota = const[:, C_IOTA:C_IOTA + 8]
            iota_t = bc(iota, 1, NTILE)
            for k in range(2):
                ins = v.tensor_tensor(ohB[:, k], iota_t, bc(e12[:, k, :], 2, 8), ALU.is_equal)
            ins.then_inc(MO["oh_ready"], 1)
            dve.wait_ge(MO["cum_ps"], 1)
            cum = ps[:, 0, 0:192].rearrange("p (k t e) -> p k t e", k=2, t=NTILE)
            ch.link(v.tensor_copy(cumS[:, 0], cum[:, 0]))
            ch.link(v.tensor_tensor(cumS[:, 1], cum[:, 1], cumS[:, 0], ALU.add))
            for k in range(2):
                ch.link(v.scalar_tensor_tensor(em[:, k], cumS[:, k], float(CAP), ohB[:, k], ALU.is_lt, ALU.mult))
                ch.link(v.tensor_reduce(tm[:, k, :], em[:, k], AX.X, ALU.add))
                ch.link(v.tensor_tensor(t96[:, k], em[:, k], iota_t, ALU.mult))
                ch.link(v.tensor_reduce(asg[:, k, :], t96[:, k], AX.X, ALU.add))
            ch.link(v.tensor_tensor(mG, asg[:, 0, :], asg[:, 1, :], ALU.max))
            ch.link(v.tensor_tensor(actG, tm[:, 0, :], tm[:, 1, :], ALU.max))
            ch.link(v.tensor_tensor(t96[:, 0], iota_t, bc(mG, 2, 8), ALU.is_equal))
            v.tensor_tensor(ohmB, t96[:, 0], bc(actG, 2, 8), ALU.mult).then_inc(MO["ohm_ready"], 1)
            dve.wait_ge(MO["ex_ready"], 1)
            ch.link(v.tensor_scalar(rankG, pq[:, 1, :], 1.0, None, ALU.add))
            ch.link(v.reciprocal(pq[:, 0, :], rankG))
            ch.link(v.tensor_tensor(pq[:, 1, :], pq[:, 1, :], pq[:, 0, :], ALU.mult))
            ch.link(v.tensor_tensor(wy, tm, pq, ALU.mult))
            ch.link(v.tensor_tensor(wx, pq, wy, ALU.subtract))
            ch.link(v.tensor_tensor(wy[:, 0, :], wy[:, 0, :], wy[:, 1, :], ALU.add))
            ch.link(v.tensor_tensor(wx[:, 0, :], wx[:, 0, :], wx[:, 1, :], ALU.add))
            dve.wait_ge(MO["rank_ps"], 1)
            ch.link(v.tensor_tensor(t96[:, 1], ps[:, 1, 0:96].rearrange("p (t e) -> p t e", e=8), ohmB, ALU.mult))
            ch.link(v.tensor_reduce(rankG, t96[:, 1], AX.X, ALU.add))
            ch.link(v.scalar_tensor_tensor(slotf[:, 0, :], mG, float(SLOTS), rankG, ALU.mult, ALU.add))
            ch.link(v.tensor_scalar(slotf[:, 1, :], slotf[:, 0, :], -1.0, None, ALU.add))
            ch.link(v.tensor_tensor(slotf[:, 0, :], slotf[:, 1, :], const[:, C_DUMP:C_DUMP + NTILE], ALU.subtract))
            ch.link(v.tensor_tensor(slotf[:, 0, :], slotf[:, 0, :], actG, ALU.mult))
            ch.link(v.tensor_tensor(slotf[:, 0, :], slotf[:, 0, :], const[:, C_DUMP:C_DUMP + NTILE], ALU.add))
            ch.link(v.tensor_tensor(slotf[:, 1, :], slotf[:, 1, :], actG, ALU.mult))
            v.tensor_copy(slotS, slotf[:, 0, :])
            v.tensor_copy(slotG, slotf[:, 1, :]).then_inc(MO["slot_ready"], 1)

            def expert(g, q):
                for j in range(4):
                    n = (2 * g + q) * 4 + j + 1
                    dve.wait_ge(MO["a_ready"], n)
                    v.tensor_tensor(prodH[:, j % 2, :], aH[:, j % 2, :], ps[:, 3 + 2 * (j % 2), 0:SLOTS], ALU.mult).then_inc(MO["prod_ready"], 1)
                at_least(dve, MO["ys_out"][q], 16 * g)
                for s in range(3):
                    dve.wait_ge(MO["y_ps"], (2 * g + q) * 3 + s + 1)
                    v.tensor_copy(ysH[:, q, s, :], ps[:, 6 + s % 2, 0:DIM]).then_inc(MO["ys_ready"], 1)

            for q in range(2):
                expert(0, q)
            with dve.Fori(1, EXPERTS // 2) as g:
                for q in range(2):
                    expert(g, q)

            for t in range(NTILE):
                dve.wait_ge(MO["yg_in"], 16 * NTILE)
                ch.link(v.scalar_tensor_tensor(res[:, t, :], ygH[:, t, :], wy[:, 0, t:t + 1], res[:, t, :], ALU.mult, ALU.add))
                v.scalar_tensor_tensor(res[:, t, :], xf[:, t, :], wx[:, 0, t:t + 1], res[:, t, :],
                                       ALU.mult, ALU.add).then_inc(MO["out_ready"], 1)

        @block.scalar
        def _(act):
            a_ = nc.scalar

            def place_h(i):
                act.wait_ge(h2_ps, i + 1)
                dst = hT[:].rearrange("p c (b n) -> p c n b", n=NPATCH)[:, :, bass.ds(2 * i, 2), :]
                a_.activation(dst, ps[:, 6, 0:DIM].rearrange("p (c n b) -> p c n b", c=KC, n=2), ACT.Copy).then_inc(hT_ready, 1)

            def tile_a(i, first=False):
                if not first:
                    place_h(i - 1)
                act.wait_ge(xnT_ps, i + 1)
                a_.activation(xnTA, ps[:, 2, 0:DIM].rearrange("p (c t) -> p c t", c=KC), ACT.Copy).then_inc(xnT_ready, 1)
                act.wait_ge(smA_ready, i + 1)
                a_.activation(eA, smA, ACT.Exp, bias=nbA, accum_out=sumA).then_inc(eA_ready, 1)
                act.wait_ge(eA_ps, i + 1)
                a_.activation(etA, ps[:, 4, 0:P], ACT.Copy).then_inc(etA_ready, 1)

            tile_a(0, first=True)
            with act.Fori(1, NTILE) as i:
                tile_a(i)
            place_h(NTILE - 1)

            def square(kind, m):
                act.wait_ge(LN[kind]["d_ready"], m + 1)
                a_.activation(sqL, dT[:, :, bass.ds(m * BLK, BLK)], ACT.Square).then_inc(LN[kind]["sq_ready"], 1)

            def root(kind, m, bank):
                S = LN[kind]
                act.wait_ge(S["var_ps"], m + 1)
                if kind == "E":
                    a_.activation(varL, ps[:, bank, 0:BLK], ACT.Copy)
                a_.activation(stdL, ps[:, bank, 0:BLK], ACT.Sqrt, bias=LN_EPS).then_inc(S["std_ready"], 1)
                if kind == "E":
                    act.wait_ge(S["ms_ready"], m + 1)
                    a_.activation(stdL, varL, ACT.Sqrt, bias=RMS_EPS).then_inc(S["rms_ready"], 1)

            square("B", 0)
            root("B", 0, 7)

            def feed(i):
                static = isinstance(i, int)
                for c in range(NCH):
                    act.wait_ge(FB["l_ps"], i * NCH + c + 1)
                    if c < 8:
                        act.wait_ge(FB["dec_ready"], 8 * i + c + 1)
                    a_.activation(actB[:, c % 4, :], ps[:, c % 4, 0:BLK], ACT.Silu, bias=vecs[:, c:c + 1]).then_inc(FB["a_ready"], 1)
                    if not static or i < NBLK - 1:
                        if c == 6:
                            square("B", i + 1)
                        if c == 8:
                            root("B", i + 1, 7)
                    if not static or i > 0:
                        if c == 11:
                            square("C", i - 1)
                        if c == 13:
                            root("C", i - 1, 7)

            feed(0)
            with act.Fori(1, NBLK - 1) as i:
                feed(i)
            feed(NBLK - 1)

            def attention(kind, nk):
                S = AT[kind]
                pairs = 2 if kind == "C" else 5
                scale = 0.25 if kind == "C" else 0.125

                def values(i):
                    act.wait_ge(S["v_ps"], i + 1)
                    for b in range(4):
                        src = ps[32 * b:32 * b + 32, 0:2, :].rearrange("p k (n f) -> p (k n) f", f=DIM)
                        for h in range(4):
                            dst = vC[32 * h:32 * h + 32].rearrange("p (n b) f -> p n b f", b=4)[:, :, b, :]
                            if kind == "C":
                                ins = a_.activation(dst.rearrange("p n (g a d) -> p n g a d", g=4, a=4)[:, :, :, h, :],
                                                    src.rearrange("p n (g a d) -> p n g a d", g=4, a=4)[:, :, :, h, :], ACT.Copy)
                            else:
                                ins = a_.activation(dst[:, :, 64 * h:64 * h + 64], src[:, :, 64 * h:64 * h + 64], ACT.Copy)
                    ins.then_inc(S["v_ready"], 1)

                def spread_q(i):
                    act.wait_ge(S["qk_pool"], i * pairs + 1)
                    for half in range(2):
                        for g in range(4):
                            ins = a_.activation(q_of(half, g), by_batch(rawC[:, half, :]), ACT.Copy, scale=const[:, C_GMASK + g:C_GMASK + g + 1])
                    ins.then_inc(S["qx_ready"], 1)

                def output(i, np_):
                    act.wait_ge(S["y_ps"], 2 * i + np_ + 1)
                    for hp in range(2):
                        for u in range(2):
                            if kind == "C":
                                g = 2 * hp + u
                                for n in range(2):
                                    rows = slice(64 * u, 64 * u + 64)
                                    src = ps[rows, 4 + 2 * n + hp, 0:BLK].rearrange("p (b g q) -> p b g q", b=4, g=4)[:, :, g, :]
                                    t0 = (2 * np_ + n) * 96
                                    ins = a_.activation(by_batch(yC[rows, hp, 0, t0:t0 + 96]), src, ACT.Copy)
                            else:
                                t0 = (2 * np_ + u) * 96
                                src = ps[:, 4 + 2 * u + hp, 0:BLK].rearrange("p (b g q) -> p b g q", b=4, g=4)
                                dst = yC[:, hp, :, t0:t0 + 96].rearrange("p g (b q) -> p b g q", b=4)
                                ins = a_.activation(dst, src, ACT.Copy)
                    ins.then_inc(S["y_ready"], 1)

                def body(i, nxt):
                    static = isinstance(i, int)
                    for n in range(NQ):
                        act.wait_ge(S["sub_ready"], 4 * i + n + 1)
                        a_.activation(pC[:, n, :, 0:NPATCH], sC[:, n, :, 0:NPATCH], ACT.Exp, scale=scale).then_inc(S["e_ready"], 1)
                        if kind == "E" and n == 0 and (not static or i > 0):
                            moe_square(i - 1)
                    if kind == "E" and (not static or i > 0):
                        moe_root(i - 1)
                    if nk == "E" and (not static or i > 0):
                        square("E", i - 1)
                    if nxt and kind == "C":
                        spread_q(i + 1)
                    output(i, 0)
                    if nk == "E" and (not static or i > 0):
                        root("E", i - 1, 2)
                    if kind == "E" and (not static or i > 0):
                        moe_rows(i - 1)
                    output(i, 1)
                    if nxt:
                        values(i + 1)

                square(kind, 3)
                root(kind, 3, 1)
                if kind == "C":
                    spread_q(0)
                act.wait_ge(S["zero_ready"], 1)
                values(0)
                body(0, True)
                with act.Fori(1, NBLK - 1) as i:
                    body(i, True)
                body(NBLK - 1, False)

            def moe_square(m):
                act.wait_ge(AT["E"]["h_ready"], m + 1)
                a_.activation(sqL, dT[:, :, bass.ds(m * BLK, BLK)], ACT.Square).then_inc(MO["sq_ready"], 1)

            def moe_root(m):
                act.wait_ge(MO["ms_ps"], m + 1)
                a_.activation(stdL, ps[:, 0, 0:BLK], ACT.Sqrt, bias=RMS_EPS).then_inc(MO["std_ready"], 1)

            def moe_rows(m):
                act.wait_ge(MO["lg_ps"], m + 1)
                a_.activation(xf[:, bass.ds(3 * m, 2), :], ps[:, 2, :].rearrange("p (t f) -> p t f", f=DIM), ACT.Copy)
                act.wait_ge(MO["lg_ready"], m + 1)
                a_.activation(xf[:, bass.ds(3 * m + 2, 1), :], ps[:, 3, 0:DIM].rearrange("p (t f) -> p t f", f=DIM),
                              ACT.Copy).then_inc(MO["xf_out"], 1)

            attention("C", "E")
            attention("E", None)
            moe_square(3)
            moe_root(3)
            moe_rows(3)
            act.wait_ge(MO["diff_ready"], 1)
            a_.activation(pq[:, 1, :], pq[:, 1, :], ACT.Exp).then_inc(MO["ex_ready"], 1)
            with act.Fori(0, EXPERTS // 2) as g:
                for q in range(2):
                    e = 2 * g + q
                    act.wait_ge(MO["xt_ps"], e + 1)
                    xt = xtH.rearrange("p c (s t) -> p s c t", t=P)
                    a_.activation(xt[:, 0:2], ps[:, 0, :].rearrange("p (s c t) -> p s c t", c=KC, t=P), ACT.Copy)
                    a_.activation(xt[:, 2], ps[:, 1, 0:DIM].rearrange("p (c t) -> p c t", t=P), ACT.Copy).then_inc(MO["xt_ready"], 1)

                    def gelu(j):
                        act.wait_ge(MO["prod_ready"], e * 4 + j + 1)
                        a_.activation(gH[:, j, :], prodH[:, j % 2, :], ACT.Gelu).then_inc(MO["g_ready"], 1)

                    for j in range(4):
                        act.wait_ge(MO["up_ps"], e * 4 + j + 1)
                        a_.activation(aH[:, j % 2, :], ps[:, 2 + 2 * (j % 2), 0:SLOTS], ACT.Copy).then_inc(MO["a_ready"], 1)
                        if j:
                            gelu(j - 1)
                    gelu(3)

        @block.tensor
        def _(pe):
            mm, tr = nc.tensor.matmul, nc.tensor.transpose
            pe.wait_ge(const_in, 64)
            pe.wait_ge(wtok_in, 16)

            def embed(q, first, last):
                x = xring[:, q, :].rearrange("p (r l) -> p r l", r=STRIDE)
                for r in range(first, last):
                    at = r // STRIDE * BATCH
                    ins = mm(ps[:, q, 0:DIM], x[:, r % STRIDE, at:at + P], wtok[:, r, :], start=r == 0, stop=r == PATCH - 1)
                if last == PATCH:
                    ins.then_inc(tok_ps, 1)

            def transpose_h():
                for c in range(KC):
                    ins = tr(ps[:, 6, c * P:(c + 1) * P], h2A[:, c * P:(c + 1) * P], ident)
                ins.then_inc(h2_ps, 1)

            def tile_a(i, q, j=0, first=False, last=False):
                if not last:
                    pe.wait_ge(x_in[1 - q], 16 * (j + q + 1))
                    at_least(pe, hA_ready, i)
                    embed(1 - q, 0, 5)
                if not first:
                    pe.wait_ge(h2_ready, i)
                    transpose_h()
                pe.wait_ge(xn_ready, i + 1)
                for c in range(KC):
                    ins = tr(ps[:, 2, c * P:(c + 1) * P], xnA[:, q, c * P:(c + 1) * P], ident)
                ins.then_inc(xnT_ps, 1)
                if not last:
                    embed(1 - q, 5, 8)
                pe.wait_ge(xnT_ready, i + 1)
                for c in range(KC):
                    ins = mm(ps[:, 3, 0:P], xnTA[:, c, :], xnTA[:, c, :], start=c == 0, stop=c == KC - 1)
                ins.then_inc(sA_ps, 1)
                if not last:
                    embed(1 - q, 8, 12)
                pe.wait_ge(eA_ready, i + 1)
                tr(ps[:, 4, 0:P], eA, ident).then_inc(eA_ps, 1)
                if not last:
                    embed(1 - q, 12, 16)
                pe.wait_ge(etA_ready, i + 1)
                mm(ps[:, 5, 0:DIM], etA, xnA[:, q, :], start=True, stop=True).then_inc(pvA_ps, 1)

            pe.wait_ge(x_in[0], 16)
            embed(0, 0, PATCH)
            tile_a(0, 0, j=0, first=True)
            tile_a(1, 1, j=0)
            with pe.Fori(1, NTILE // 2 - 1) as j:
                for q in range(2):
                    tile_a(2 * j + q, q, j=j)
            tile_a(NTILE - 2, 0, j=NTILE // 2 - 1)
            tile_a(NTILE - 1, 1, j=NTILE // 2 - 1, last=True)
            pe.wait_ge(h2_ready, NTILE)
            transpose_h()

            def mean(kind, m, bank):
                for c in range(KC):
                    ins = mm(ps[:, bank, 0:BLK], meanw, hT[:, c, bass.ds(m * BLK, BLK)], start=c == 0, stop=c == KC - 1)
                ins.then_inc(LN[kind]["mean_ps"], 1)

            def variance(kind, m, bank):
                pe.wait_ge(LN[kind]["sq_ready"], m + 1)
                for c in range(KC):
                    ins = mm(ps[:, bank, 0:BLK], meanw, sqL[:, c, :], start=c == 0, stop=c == KC - 1)
                ins.then_inc(LN[kind]["var_ps"], 1)

            pe.wait_ge(constb_ready, 1)
            pe.wait_ge(hT_ready, NTILE)
            mean("B", 0, 6)
            variance("B", 0, 7)
            pe.wait_ge(win_in, 32)

            def feed(i):
                static = isinstance(i, int)
                pe.wait_ge(FB["x_ready"], i + 1)

                def down(c):
                    pe.wait_ge(FB["act_ready"], i * NCH + c + 1)
                    for o in range(KC):
                        ins = mm(ps[:, 4 + o, 0:BLK], wout[:, c, o * P:(o + 1) * P], accB[:, c % 4, :], start=c == 0, stop=c == NCH - 1)
                    return ins

                for c in range(NCH):
                    if c >= 4:
                        pe.wait_ge(FB["act_ready"], i * NCH + c - 3)
                    for k in range(KC):
                        ins = mm(ps[:, c % 4, 0:BLK], win[:, k, c * P:(c + 1) * P], xB[:, k, :], start=k == 0, stop=k == KC - 1)
                    ins.then_inc(FB["l_ps"], 1)
                    if c == 1:
                        pe.wait_ge(FB["dec_ready"], 8 * i + 1)
                        mm(ps[:, 6, 0:BLK], constb[:, B_ANC0:B_ANC0 + P], maskB[:, 0, :], start=True, stop=True)
                        mm(ps[:, 7, 0:BLK], constb[:, B_ANC1:B_ANC1 + P], maskB[:, 0, :], start=True, stop=True).then_inc(FB["v_ps"], 1)
                    if c >= 3:
                        down(c - 3)
                    if not static or i < NBLK - 1:
                        if c == 5:
                            mean("B", i + 1, 6)
                        if c == 8:
                            variance("B", i + 1, 7)
                    if not static or i > 0:
                        if c == 10:
                            pe.wait_ge(FB["h_ready"], i)
                            mean("C", i - 1, 6)
                        if c == 13:
                            variance("C", i - 1, 7)
                for c in range(NCH - 3, NCH):
                    last = down(c)
                last.then_inc(FB["o_ps"], 1)

            feed(0)
            with pe.Fori(1, NBLK - 1) as i:
                feed(i)
            feed(NBLK - 1)

            def attention(kind, nk):
                S = AT[kind]
                pairs = 2 if kind == "C" else 5
                w, voff = (w1q, 512) if kind == "C" else (w2q, 1280)
                wo, nout = (w1o, 1) if kind == "C" else (w2o, 4)
                pe.wait_ge(w1_in if kind == "C" else w2_in, 32 if kind == "C" else 48)

                def project(i, p):
                    if p == 0:
                        pe.wait_ge(S["x_ready"], i + 1)
                        at_least(pe, S["h_ready"], i - 1)
                    at_least(pe, S["v_ready"], i)
                    at_least(pe, S["t_ready"], i * pairs + p - 1)
                    for half in range(2):
                        col = (2 * p + half) * P
                        for k in range(KC):
                            ins = mm(ps[:, 2 * ((p + 1) % 2) + half, 0:BLK], w[:, k, col:col + P], xC[:, k, :, 0:NPATCH],
                                     start=k == 0, stop=k == KC - 1)
                    ins.then_inc(S["proj_ps"], 1)

                def values(i):
                    pe.wait_ge(S["t_ready"], (i + 1) * pairs)
                    for n in range(NQ):
                        for k in range(KC):
                            ins = mm(ps[:, n // 2, (n % 2) * DIM:(n % 2 + 1) * DIM], xC[:, k, 4 * n:4 * n + 4, :].rearrange("p b n -> p (b n)"),
                                     w[:, k, voff:voff + DIM], start=k == 0, stop=k == KC - 1)
                    ins.then_inc(S["v_ps"], 1)

                def scores(i):
                    pe.wait_ge(S["kx_ready"], i + 1)
                    if kind == "C":
                        pe.wait_ge(S["qx_ready"], i + 1)
                    for n in range(NQ):
                        mm(ps[:, 4 + n, :], constb[:, B_IDENT:B_IDENT + P], bc(constb[:, B_CAUSAL:B_CAUSAL + 32], 1, 16),
                           start=True, stop=False, skip_group_check=True)
                        for b in range(4 * n, 4 * n + 4):
                            dst = ps[:, 4 + n, (b % 4) * P:(b % 4 + 1) * P].rearrange("p (g q) -> p g q", g=4)[:, :, 0:NPATCH]
                            for half in range(2):
                                ins = mm(dst, kC[:, half, b * P:(b + 1) * P], qC[:, half, b * 96:(b + 1) * 96],
                                         start=False, stop=b % 4 == 3 and half == 1, skip_group_check=True)
                        ins.then_inc(S["s_ps"], 1)

                def output(i, np_):
                    if np_ == 0:
                        pe.wait_ge(S["v_ready"], i + 1)
                        pe.wait_ge(S["st_ready"], 4 * i + 4)
                    else:
                        pe.wait_ge(S["y_ready"], 2 * i + 1)
                    for n in range(2):
                        q = 2 * np_ + n
                        pe.wait_ge(S["pt_ready"], 4 * i + q + 1)
                        for hp in range(2):
                            for b in range(4):
                                src = sC[:, q].rearrange("p (b g) q -> p b g q", b=4)[:, b, :, 0:NPATCH]
                                ins = mm(ps[:, 4 + 2 * n + hp, b * 96:(b + 1) * 96], vC[:, 4 * q + b, hp * P:(hp + 1) * P], src,
                                         start=True, stop=True)
                    ins.then_inc(S["y_ps"], 1)

                def body(i, nxt):
                    static = isinstance(i, int)
                    more = nk == "E" and (not static or i > 0)
                    moe = kind == "E" and (not static or i > 0)
                    scores(i)
                    if more or moe:
                        at_least(pe, S["v_ready"], i + 1)
                        pe.wait_ge(S["h_ready"], i)
                    if more:
                        mean("E", i - 1, 0)
                    if moe:
                        moe_square(i - 1)
                    if nxt:
                        for p in range(pairs):
                            if p == 1 and more:
                                pe.wait_ge(LN["E"]["d_ready"], i)
                            if p == 1 and moe:
                                pe.wait_ge(MO["std_ready"], i)
                            project(i + 1, p)
                    output(i, 0)
                    if nxt:
                        pe.wait_ge(S["t_ready"], (i + 2) * pairs)
                    if more:
                        at_least(pe, S["h_ready"], i)
                        variance("E", i - 1, 2)
                    if moe:
                        moe_rows(i - 1)
                    if nxt:
                        values(i + 1)
                    output(i, 1)
                    if moe:
                        moe_rest(i - 1)
                    pe.wait_ge(S["y_ready"], 2 * i + 2)
                    if more:
                        pe.wait_ge(LN["E"]["std_ready"], i)
                    for o in range(KC):
                        for m in range(2 * nout):
                            ins = mm(ps[:, 2 + o, 0:BLK], wo[:, m, o * P:(o + 1) * P], yC[:, m // nout, m % nout, :],
                                     start=m == 0, stop=m == 2 * nout - 1)
                    ins.then_inc(S["o_ps"], 1)

                source = FB if kind == "C" else AT["C"]
                pe.wait_ge(source["h_ready"], NBLK)
                mean(kind, 3, 0)
                project(0, 0)
                variance(kind, 3, 1)
                for p in range(1, pairs):
                    pe.wait_ge(LN[kind]["std_ready"], 4)
                    project(0, p)
                values(0)
                body(0, True)
                with pe.Fori(1, NBLK - 1) as i:
                    body(i, True)
                body(NBLK - 1, False)

            def moe_square(m):
                pe.wait_ge(MO["sq_ready"], m + 1)
                for c in range(KC):
                    ins = mm(ps[:, 0, 0:BLK], meanw, sqL[:, c, :], start=c == 0, stop=c == KC - 1)
                ins.then_inc(MO["ms_ps"], 1)

            def moe_rows(m):
                pe.wait_ge(MO["xf_ready"], m + 1)
                for t in range(3):
                    for c in range(KC):
                        tr(ps[:, 2 + t // 2, (t % 2) * DIM + c * P:(t % 2) * DIM + (c + 1) * P], xfF[:, c, t * P:(t + 1) * P], ident)
                for t in range(3):
                    dst = ps[:, 3, DIM + t * 8:DIM + t * 8 + 8]
                    for c in range(KC):
                        mm(dst, xfF[:, c, t * P:(t + 1) * P], wr[:, c, :], start=c == 0, stop=False)
                    ins = mm(dst, const[0:1, C_ONES:C_ONES + P], rbias[:], start=False, stop=True)
                ins.then_inc(MO["lg_ps"], 1)

            def moe_rest(m):
                pe.wait_ge(MO["xf_out"], m + 1)
                for t in range(3):
                    for c in range(KC):
                        ins = tr(ps[:, 2 + t // 2, (t % 2) * DIM + c * P:(t % 2) * DIM + (c + 1) * P], rF[:, c, t * P:(t + 1) * P], ident)
                ins.then_inc(MO["r_ps"], 1)
                pe.wait_ge(MO["r_ready"], m + 1)

            attention("C", "E")
            attention("E", None)
            moe_square(3)
            moe_rows(3)
            moe_rest(3)

            def count(dst, pick, k):
                mm(dst, constb[:, B_TRI:B_TRI + P], pick, start=True, stop=False, skip_group_check=True)
                for t in range(NTILE - 1):
                    rest = NTILE - 1 - t
                    if k:
                        for kk in range(2):
                            ins = mm(dst[:, kk, t + 1:, :], constb[:, B_ONES:B_ONES + P], bc(pick[:, kk, t, :], 1, rest), start=False,
                                     stop=t == NTILE - 2 and kk == 1, skip_group_check=True)
                    else:
                        ins = mm(dst[:, t + 1:, :], constb[:, B_ONES:B_ONES + P], bc(pick[:, t, :], 1, rest), start=False,
                                 stop=t == NTILE - 2, skip_group_check=True)
                return ins

            pe.wait_ge(MO["oh_ready"], 1)
            count(ps[:, 0, 0:192].rearrange("p (k t e) -> p k t e", k=2, t=NTILE), ohB, True).then_inc(MO["cum_ps"], 1)
            pe.wait_ge(MO["ohm_ready"], 1)
            count(ps[:, 1, 0:96].rearrange("p (t e) -> p t e", t=NTILE), ohmB, False).then_inc(MO["rank_ps"], 1)
            pe.wait_ge(MO["slot_ready"], 1)

            with pe.Fori(0, EXPERTS // 2) as g:
                for q in range(2):
                    e = 2 * g + q
                    pe.wait_ge(MO["xs_in"][q], 16 * g + 16)
                    for s in range(3):
                        for c in range(KC):
                            ins = tr(ps[:, s // 2, (s % 2) * DIM + c * P:(s % 2) * DIM + (c + 1) * P], xsH[:, q, s, c * P:(c + 1) * P], ident)
                    ins.then_inc(MO["xt_ps"], 1)
                    pe.wait_ge(MO["we_in"][q], 16 * g + 16)
                    pe.wait_ge(MO["xt_ready"], e + 1)
                    for j in range(4):
                        if j >= 2:
                            pe.wait_ge(MO["prod_ready"], e * 4 + j - 1)
                        for m, w in enumerate((w2e[q], w1e[q])):
                            for k in range(KC):
                                ins = mm(ps[:, 2 + 2 * (j % 2) + m, 0:SLOTS], w[:, k, j * P:(j + 1) * P], xtH[:, k, :],
                                         start=k == 0, stop=k == KC - 1)
                        ins.then_inc(MO["up_ps"], 1)
                    for s in range(3):
                        pe.wait_ge(MO["g_ready"], e * 4 + 4)
                        if s == 2:
                            pe.wait_ge(MO["ys_ready"], e * 3 + 1)
                        for j in range(4):
                            ins = mm(ps[:, 6 + s % 2, 0:DIM], gH[:, j, s * P:(s + 1) * P], w3e[q][:, j, :], start=j == 0, stop=j == 3)
                        ins.then_inc(MO["y_ps"], 1)


def kernel(**inputs):
    import concourse.bacc as bacc
    from concourse.bass_utils import run_bass_kernel_spmd

    arrays = _layout(inputs)
    nc = bacc.Bacc("TRN2", target_bir_lowering=False, num_devices=1)
    io = {n: nc.dram_tensor(f"in_{n}", a.shape, mybir.dt.from_np(a.dtype), kind="ExternalInput").ap() for n, a in arrays.items()}
    out = nc.dram_tensor("out", [TOK, DIM], F32, kind="ExternalOutput").ap()
    tower(nc, io, out)
    r = run_bass_kernel_spmd(nc, [{f"in_{n}": a for n, a in arrays.items()}], core_ids=[0])
    return r.results[0]["out"].reshape(BATCH, NPATCH, DIM)


def _layout(inputs):
    g = {k: np.asarray(a) for k, a in inputs.items()}
    cols = lambda w: np.ascontiguousarray(w.reshape(-1, P, w.shape[1]).transpose(1, 0, 2))
    c, cb = _constants()
    rows = _ffn_rows()
    pad = lambda a: np.concatenate([a, np.zeros((1,) + a.shape[1:], a.dtype)])
    win = pad(g["L0_ffn_W_in"])[rows]
    wout = pad(np.ascontiguousarray(g["L0_ffn_W_out"].T))[rows]
    bin_ = pad(g["L0_ffn_b_in"])[rows].reshape(NCH, P).T
    two = lambda a: a.reshape(KC, P).T
    vecs = np.ascontiguousarray(np.concatenate([bin_, two(g["L1_ffn_g1"]), two(g["L1_ffn_g2"]), two(g["L1_attn_bproj"])], 1))
    r1 = np.arange(HEADS)[:, None] * HD1 + 2 * np.arange(8)[None, :]
    even, odd = r1.reshape(-1), r1.reshape(-1) + 1
    wqkv = g["L1_attn_Wqkv"].T
    w1q = np.concatenate([wqkv[:, even], wqkv[:, odd], wqkv[:, DIM + even], wqkv[:, DIM + odd], wqkv[:, 2 * DIM:]], 1)
    half = lambda h, s: (np.asarray(h)[:, None] * HD2 + 32 * s + np.arange(32)[None, :]).reshape(-1)
    wq, wk_, wv = g["L1_ffn_wq"], g["L1_ffn_wk"], g["L1_ffn_wv"]
    parts = []
    for q in range(4):
        heads = [4 * q + h for h in range(HKV)]
        parts += [wq[:, half(heads, 0)], wq[:, half(heads, 1)]]
    parts += [wk_[:, half(range(HKV), 0)], wk_[:, half(range(HKV), 1)], wv]
    wo = g["L1_ffn_wo"].reshape(4, 2, 2, HD2, DIM).transpose(1, 0, 2, 3, 4).reshape(8, P, DIM)
    ex = lambda w: w.reshape(EXPERTS, -1, P, w.shape[2]).transpose(0, 2, 1, 3).reshape(EXPERTS, P, -1)
    wexp = np.concatenate([ex(g["L1_ffn_w1"]), ex(g["L1_ffn_w2"]), ex(g["L1_ffn_w3"])], 2)
    xt = g["x"].transpose(2, 1, 0)[:, :8 * (NPATCH + 1)].reshape(IN_DIM, NPATCH + 1, 8, BATCH)
    return {
        "const": c, "constb": cb, "vecs": vecs, "rb": g["L1_ffn_router_b"].reshape(1, EXPERTS),
        "x": np.stack([xt[:, 2 * t:2 * t + 3].transpose(0, 2, 1, 3).reshape(IN_DIM, -1) for t in range(NTILE)]),
        "wtok": cols(g["L0_tok_W"]), "btok": g["L0_tok_b"].reshape(1, DIM),
        "pos": np.ascontiguousarray(g["L0_tok_pos_embed"][0, :NPATCH]),
        "win": cols(np.ascontiguousarray(win.T)), "wout": cols(wout),
        "w1q": cols(w1q), "w1o": cols(np.ascontiguousarray(g["L1_attn_Wproj"].T)),
        "w2q": cols(np.concatenate(parts, 1)), "w2o": np.ascontiguousarray(wo.transpose(1, 0, 2)),
        "wr": cols(g["L1_ffn_router_w"]), "wexp": np.ascontiguousarray(wexp),
    }
```

```python
from contextlib import ExitStack

import numpy as np

import concourse.bass as bass
from concourse import mybir
from concourse.alu_op_type import AluOpType as ALU

F32 = mybir.dt.float32
F32R = mybir.dt.float32r
BF16 = mybir.dt.bfloat16
I32 = mybir.dt.int32
U32 = mybir.dt.uint32
ACT = mybir.ActivationFunctionType
AX = mybir.AxisListType

P = 128
BATCH, NPATCH, DIM = 64, 24, 256
IN_DIM, PATCH, STRIDE = 128, 16, 8
TOK = BATCH * NPATCH
KC = DIM // P
NTILE = TOK // P
BLK = 384
NBLK = TOK // BLK
BB = BLK // NPATCH
NQ = BB // 4
XROWS = PATCH + STRIDE
NODES = 255
NCH = 16
HEADS, HD1 = 16, 16
HKV, HD2 = 4, 64
EXPERTS = 8
CAP = TOK // 8
SLOTS = 2 * CAP
NSLOT = EXPERTS * SLOTS
ID, WEIGHT, REST, ROW = DIM, DIM + 1, DIM + 2, 2 * DIM + 2
OUT_ROWS = TOK + NSLOT
LN_EPS, RMS_EPS = 1e-5, 1e-6
FAR = -1e30

C_IDENT = 0
C_MEAN = 128
C_BLOCKMASK = 256
C_COS1, C_SIN1, C_COS2, C_SIN2 = 384, 408, 432, 456
C_AMASK = 480
C_GMASK = 484
C_CNT = 488
C_HALF = 490
C_ONES = 491
C_IOTA = 619
C_DUMP = 627
C_EPS = 639
C_EMPTY = 640
NCONST = 640 + NSLOT // P
B_ANC0 = 0
B_ANC1 = 128
B_TRI = 256
B_ONES = 384
B_IDENT = 512
B_CAUSAL = 640
NCONSTB = 672


def _tree(node):
    out, level = [], (node + 1).bit_length() - 1
    k = node - (2 ** level - 1)
    while level:
        level, right, k = level - 1, k & 1, k >> 1
        out.append((2 ** level - 1 + k, right))
    return out


def _constants():
    c = np.zeros((P, NCONST), np.float32)
    c[:, C_IDENT:C_IDENT + P] = np.eye(P)
    c[:, C_MEAN:C_MEAN + P] = 1.0 / DIM
    blk = np.arange(P) // BATCH
    c[:, C_BLOCKMASK:C_BLOCKMASK + P] = np.where(blk[:, None] == blk[None, :], 0.0, FAR)
    t = np.arange(NPATCH, dtype=np.float32)
    f1 = (np.float32(1.0) / np.float32(10000.0) ** (np.arange(8, dtype=np.float32) / np.float32(8))).astype(np.float32)
    a1 = t[:, None] * f1[None, :]
    a1 = a1[:, np.arange(P) % 8].T
    c[:, C_COS1:C_COS1 + NPATCH], c[:, C_SIN1:C_SIN1 + NPATCH] = np.cos(a1), np.sin(a1)
    f2 = 10000.0 ** (-np.arange(0, HD2, 2, dtype=np.float32) / HD2)
    a2 = np.outer(t, f2).astype(np.float32)[:, np.arange(P) % 32].T
    c[:, C_COS2:C_COS2 + NPATCH], c[:, C_SIN2:C_SIN2 + NPATCH] = np.cos(a2), np.sin(a2)
    p = np.arange(P)
    for a in range(4):
        c[:, C_AMASK + a] = (p // 8) % 4 == a
        c[:, C_GMASK + a] = p // 32 == a
    rights = [sum(r for _, r in _tree(n)) for n in range(31)]
    c[:120, C_CNT] = [rights[q // 8] for q in range(120)]
    c[:, C_CNT + 1] = [rights[15 + q // 8] for q in range(P)]
    c[:, C_EPS] = LN_EPS
    c[:, C_HALF] = -0.5
    c[:, C_ONES:C_ONES + P] = 1.0
    c[:, C_IOTA:C_IOTA + 8] = np.arange(8)
    c[:, C_DUMP:C_DUMP + NTILE] = NSLOT + np.arange(NTILE)[None, :] * P + p[:, None]
    c[:, C_EMPTY:] = TOK + np.arange(NSLOT // P)[None, :] * P + p[:, None]
    b = np.zeros((P, NCONSTB), np.float32)
    for q in range(120):
        for anc, right in _tree(q // 8):
            b[anc * 8 + q % 8, B_ANC0 + q] = 1 if right else -1
    for q in range(P):
        for anc, right in _tree(15 + q // 8):
            b[anc * 8 + q % 8, B_ANC1 + q] = 1 if right else -1
    b[:, B_TRI:B_TRI + P] = p[:, None] <= p[None, :]
    b[:, B_ONES:B_ONES + P] = 1.0
    b[:, B_IDENT:B_IDENT + P] = np.eye(P)
    key, query = (p % 32)[:, None], np.arange(32)[None, :]
    b[:, B_CAUSAL:B_CAUSAL + 32] = np.where((key < NPATCH) & (key <= query), 0.0, FAR)
    return c, b


def _ffn_rows():
    rows = -np.ones((NCH, P), np.int64)
    q = np.arange(120)
    rows[0, :120] = (q % 8) * NODES + q // 8
    q = np.arange(P)
    for c in range(1, NCH):
        r = c.bit_length() - 1
        node = 2 ** (4 + r) - 1 + (q // 8) * 2 ** r + (c - 2 ** r)
        rows[c] = (q % 8) * NODES + node
    return rows.reshape(-1)


class Chain:

    def __init__(self, eng, sem):
        self.eng, self.sem, self.base, self.n = eng, sem, 0, 0

    def turn(self, i, per):
        self.base, self.start, self.n, self.per = self.floor() + i * per, self.floor(), 0, per

    def floor(self):
        return self.base + self.n if isinstance(self.base, int) else self.start

    def end(self, times):
        assert self.n == self.per, (self.n, self.per)
        self.base, self.n = self.start + times * self.per, 0

    def link(self, ins):
        self.n += 1
        ins.then_inc(self.sem, 1)
        self.eng.wait_ge(self.sem, self.base + self.n)


def order(pairs):
    first = [("rope", 0), ("sum", 0), ("weigh", 0), ("sum", 1), ("weigh", 1), ("rope", 1)]
    second = [("sum", 2), ("weigh", 2), ("sum", 3), ("weigh", 3)]
    if pairs <= 2:
        return [s for s in first if s[0] != "rope" or s[1] < pairs] + [("turn", 0), ("turn", 1)] + second + [("turn", 2), ("turn", 3)]
    return first + second + [("rope", 2), ("turn", 0), ("turn", 1), ("rope", 3), ("turn", 2), ("turn", 3), ("rope", 4)]


def pair_bank(pairs, p):
    return 2 * ((pairs - 1 - p) % 2)


def at_least(eng, sem, value):
    if not isinstance(value, int) or value > 0:
        eng.wait_ge(sem, value)


def bc(ap, axis, count):
    new = ap.unsqueeze(axis)
    shape = list(new.shape)
    shape[axis] = count
    return new.to_broadcast(shape)


def by_batch(ap):
    return ap.rearrange("p (b n) -> p b n", n=NPATCH)


def tower(nc, io, out):
    ctx = ExitStack()
    with ctx:
        def sb(name, shape, dt=F32):
            return ctx.enter_context(nc.sbuf_tensor(name, shape, dt))

        def sem(name):
            return ctx.enter_context(nc.semaphore(name))

        const = sb("const", [P, NCONST])
        constb = sb("constb", [P, NCONSTB], BF16)
        vecs = sb("vecs", [P, 22])
        negb = sb("negb", [P, NCH])
        rbias = sb("rbias", [1, EXPERTS])
        rows = sb("rows", [P, NTILE, ROW])
        xf, res = rows[:, :, 0:DIM], rows[:, :, REST:ROW]
        logit = sb("logit", [P, NTILE, EXPERTS])
        wr = sb("wr", [P, KC, EXPERTS])
        empties = sb("empties", [P, NSLOT // P, 2])
        idle, idleP = sb("idle", [P, 1]), sb("idle_pool", [P, 1])

        until_moe, after_a = ExitStack(), ExitStack()
        hT = until_moe.enter_context(nc.sbuf_tensor("hT", [P, KC, TOK], F32))
        dT, rstd, nrm, w1q, w1o = (after_a.enter_context(nc.sbuf_tensor(name, shape, F32)) for name, shape in (
            ("dT", [P, KC, TOK]),
            ("rstd", [P, TOK]),
            ("nrm", [P, 5, BLK]),
            ("w1q", [P, KC, 768]),
            ("w1o", [P, KC, DIM])))

        def here(*specs):
            with ExitStack() as place:
                return [place.enter_context(nc.sbuf_tensor(name, shape, dt)) for name, shape, dt in specs]

        WFF = 2 * NCH * DIM
        XT = XROWS * BATCH
        wff_hi, wff_lo, wkA, xhA, xlA = here(
            ("wff_hi", [P, WFF], F32R), ("wff_lo", [P, WFF], F32R), ("work_a", [P, 6840], F32),
            ("xa_hi", [P, 2, XT], F32R), ("xa_lo", [P, 2, XT], F32R))
        _, _, wkB, xh, xl, ah, al = here(
            ("wff_hi_", [P, WFF], F32R), ("wff_lo_", [P, WFF], F32R), ("work_b", [P, 6912], F32),
            ("x_hi", [P, KC, BLK], F32R), ("x_lo", [P, KC, BLK], F32R), ("a_hi", [P, 4, BLK], F32R), ("a_lo", [P, 4, BLK], F32R))
        w2q, w2o, wbig, wk = here(
            ("w2q", [P, KC, 1536], F32),
            ("w2o", [P, 8, DIM], F32),
            ("wbig", [P, 8192], F32),
            ("work", [P, 16080], F32))
        after_a.close()
        wtok_hi, wtok_lo = here(("wtok_hi", [P, PATCH, DIM], F32R), ("wtok_lo", [P, PATCH, DIM], F32R))
        until_moe.close()
        UP, DOWN = 2048, 1024
        (gh, gl, ysM, _, stE, actM, wh1, wl1, xth, xtl, _, wkR, wh0, wl0, xsM, restM, stO) = here(
            ("g_hi", [P, 2, 4, SLOTS], F32R), ("g_lo", [P, 2, 4, SLOTS], F32R), ("ys_rows", [P, 2, 3, DIM], F32), ("nrm_w1_", [P, 3968], F32),
            ("w_even", [P, UP + DOWN], F32), ("act_moe", [P, 2048], F32),
            ("w_hi1", [P, UP + DOWN], F32R), ("w_lo1", [P, UP + DOWN], F32R),
            ("xt_hi", [P, KC, SLOTS], F32R), ("xt_lo", [P, KC, SLOTS], F32R), ("gap", [P, 512], F32),
            ("work_route", [P, 3500], F32), ("w_hi0", [P, UP + DOWN], F32R), ("w_lo0", [P, UP + DOWN], F32R),
            ("xs_rows", [P, 2, 3, DIM], F32), ("rest_rows", [P, 2, 3, ROW - DIM], F32), ("w_odd", [P, UP], F32))
        ps = ctx.enter_context(nc.psum_tensor("ps", [P, 8, 512], F32))
        win_parts = [w[:, 0:WFF // 2].rearrange("p (k n) -> p k n", k=KC) for w in (wff_hi, wff_lo)]
        wout_parts = [w[:, WFF // 2:].rearrange("p (c n) -> p c n", c=NCH) for w in (wff_hi, wff_lo)]
        staged = rows[:].rearrange("p t n -> p (t n)")[:, ROW:ROW + WFF // 2]

        def carve(wk, *shapes):
            at, views = 0, []
            for s in shapes:
                n = int(np.prod(s))
                v = wk[:, at:at + n]
                if len(s) > 1:
                    names = "abcd"[:len(s)]
                    v = v.rearrange(f"p ({' '.join(names)}) -> p {' '.join(names)}",
                                    **{k: d for k, d in zip(names, s)})
                views.append(v)
                at += n
            assert at <= wk.shape[1], (at, wk.shape)
            return views

        constb32 = hT[:, 1, 0:NCONSTB]
        ident = const[:, C_IDENT:C_IDENT + P]
        meanw = const[:, C_MEAN:C_MEAN + P]

        (xin, posb, brow, hA, xnA, xnTA, smA, eA, etA, h2A, statA, mvA, varA, rsA, nbA, sumA, rinvA, idleA) = carve(
            wkA, (2, XT // 2), (NTILE, DIM), (DIM,), (2, DIM), (2, DIM), (KC, P), (P,), (P,), (P,),
            (DIM,), (6,), (2,), (1,), (1,), (1,), (1,), (1,), (1,))
        sqL, stdL, riL, varL = nrm[:, 0:2], nrm[:, 2], nrm[:, 3], nrm[:, 4]
        (xB, actB, accB, maskBf) = carve(wkB, (KC, BLK), (4, BLK), (4, BLK), (NCH, BLK // 2))
        maskB = maskBf.bitcast(BF16)
        (xC, qC, kC, tC, rawC, yC, mxC, suC, riC) = carve(
            wk, (KC, BB, 32), (2, 4 * BLK), (2, 4 * BB * 32), (2, 4, BLK), (4, BLK), (2, 4, BLK), (4, 16), (4, 16), (4, 16))
        vC = wbig[:, 0:4096].rearrange("p (b f) -> p b f", b=BB)
        pC = wbig[:, 4096:6144].rearrange("p (n s k) -> p n s k", n=NQ, k=32)
        sC = wbig[:, 6144:8192].rearrange("p (n s k) -> p n s k", n=NQ, k=32)

        def q_of(half, g):
            return qC[:, half, :].rearrange("p (b a n) -> p b a n", b=BB, a=4)[:, :, g, :]

        def k_of(half, a):
            return kC[:, half, :].rearrange("p (b a n) -> p b a n", b=BB, a=4)[:, :, a, 0:NPATCH]

        xfF, rF = (w1q[:].rearrange("p k n -> p (k n)")[:, i * 768:(i + 1) * 768].rearrange("p (k t) -> p k t", k=KC) for i in range(2))
        (top8, idx8f, e12, oh, pq, em, cumS, t96, tm, asg, mG, actG, rankG, slotf, wy, wx, slotSf, ohm, kept) = carve(
            wkR, (NTILE, 8), (NTILE, 8), (2, NTILE), (2, NTILE, 8 // 2), (2, NTILE),
            (2, NTILE, 8), (2, NTILE, 8), (2, NTILE, 8), (2, NTILE), (2, NTILE), (NTILE,), (NTILE,), (NTILE,), (2, NTILE),
            (2, NTILE), (2, NTILE), (NTILE,), (NTILE, 8 // 2), (NTILE - 3, DIM))
        aH, prodH, gelH = carve(actM, (2, SLOTS), (2, SLOTS), (1, SLOTS))
        xsH, restH, ysH = xsM[:], restM[:], ysM[:]
        ohB = oh.rearrange("p k t e -> p (k t e)").bitcast(BF16).rearrange("p (k t e) -> p k t e", k=2, t=NTILE)
        ohmB = ohm.rearrange("p t e -> p (t e)").bitcast(BF16).rearrange("p (t e) -> p t e", t=NTILE)
        idx8 = idx8f.bitcast(U32)
        slotS = slotSf.bitcast(I32)
        xs_d = nc.dram_tensor("xs", [NSLOT + TOK, ROW], F32).ap()
        w_up, w_down = (stE[:, 0:UP], stO[:]), stE[:, UP:]
        w_parts = ((wh0, wl0), (wh1, wl1))
        w1e, w2e = ([[w[:, at:at + 1024].rearrange("p (k n) -> p k n", k=KC) for w in parts] for parts in w_parts] for at in (0, 1024))
        w3e = [[w[:, UP:].rearrange("p (k n) -> p k n", k=4) for w in parts] for parts in w_parts]

        vd, gd = sem("dve_step"), sem("pool_step")
        const_in, wff_in, w1_in, w2_in = (sem(n) for n in ("const_in", "wffn_in", "watt1_in", "watt2_in"))
        wff_hi_ready, wff_lo_ready = sem("wff_hi_ready"), sem("wff_lo_ready")
        pos_in, constb_ready = sem("pos_in"), sem("constb_ready")
        wtok_in = [sem(f"wtok_in{r}") for r in range(4)]
        wtok_hi_ready, wtok_lo_ready, x_hi_ready, x_lo_ready = (
            sem(n) for n in ("wtok_hi_ready", "wtok_lo_ready", "x_hi_ready", "x_lo_ready"))
        x_in = [sem("x_in0"), sem("x_in1")]
        posb_ready, tok_ps, hA_ready, var_ready, rstdA_ready, xn_ready = (
            sem(n) for n in ("posb_ready", "tok_ps", "hA_ready", "var_ready", "rstdA_ready", "xn_ready"))
        xnT_ps, xnT_ready, sA_ps, smA_ready, eA_ready, eA_ps, etA_ready, pvA_ps, h2_ready, h2_ps, hT_ready = (
            sem(n) for n in ("xnT_ps", "xnT_ready", "sA_ps", "smA_ready", "eA_ready", "eA_ps", "etA_ready", "pvA_ps",
                             "h2_ready", "h2_ps", "hT_ready"))

        LN = {k: {n: sem(f"ln{k}_{n}") for n in ("mean_ps", "d_ready", "sq_ready", "var_ps", "std_ready", "done")}
              for k in "BCE"}
        LN["E"].update({n: sem(f"lnE_{n}") for n in ("ri_ready", "ms_ready", "rms_ready")})
        FB = {n: sem(f"ffn_{n}") for n in ("xf_ready", "xhi_ready", "x_ready", "l_ps", "dec_ready", "v_ps", "a_ready", "act_ready",
                                          "hi_ready", "lo_ready", "down_ps", "h_ready")}
        AT = {k: {n: sem(f"att{k}_{n}") for n in ("x_ready", "proj_ps", "t_ready", "qk_pool", "kx_ready", "qx_ready", "v_ps",
                                                 "v_ready", "s_ps", "st_ready", "sub_ready", "e_ready", "ri_ready",
                                                 "p_ready", "pt_ready", "y_ps", "y_ready", "o_ps", "h_ready", "zero_ready")}
              for k in "CE"}
        MO = {n: sem(f"moe_{n}") for n in ("r_ready", "std_ready", "xf_ready", "r_ps", "lg_ready", "diff_ready", "oh_ready",
                                          "cum_ps", "ohm_ready", "ex_ready", "rank_ps", "slot_ready", "a_ready",
                                          "prod_ready", "y_ps", "ys_ready", "rest_ready", "sq_ready", "ms_ps",
                                          "lg_ps", "xf_out", "wx_ready", "xt_ps", "xt_ready", "up_ps", "g_ready", "scattered")}
        MO["ys_out"] = [sem("moe_ys_out0"), sem("moe_ys_out1")]
        MO["xs_in"] = [sem("moe_xs_in0"), sem("moe_xs_in1")]
        MO.update({n: sem(f"moe_{n}") for n in ("down_in", "up_hi_ready", "up_lo_ready", "down_hi_ready", "down_lo_ready",
                                                "xhi_ready", "g_hi_ready")})
        for n in ("up_in", "rest_in"):
            MO[n] = [sem(f"moe_{n}{q}") for q in range(2)]
        idled, empty_ready, empty_out, rest_out = sem("pool_idled"), sem("empty_ready"), sem("empty_out"), sem("rest_out")

        block = ctx.enter_context(nc.Block())

        def y_ps(s):
            return ps[:, 6 + (s + 1) // 2, (s // 2) * DIM:(s // 2 + 1) * DIM]

        SPLITS, PIECE = (2, 8), 1024
        PARTS = ((0, NTILE - 3), (NTILE - 3, NTILE))

        @block.sync
        def _(sp):
            def load_x(t, half):
                cols = slice(half * XT // 2, (half + 1) * XT // 2)
                sp.dma_start(xin[:, half, :], io["x"][bass.ds(t, 1), :, cols].rearrange("t p n -> (t p) n")).then_inc(x_in[half], 16)

            for r in range(4):
                sp.dma_start(staged[:, r * 1024:(r + 1) * 1024], io["wtok"][:, 4 * r:4 * r + 4, :].rearrange("p r f -> p (r f)")).then_inc(wtok_in[r], 16)
                if r < 2:
                    load_x(0, r)
            sp.dma_start(const[:], io["const"]).then_inc(const_in, 16)
            sp.dma_start(constb32, io["constb"]).then_inc(const_in, 16)
            sp.dma_start(vecs[:], io["vecs"]).then_inc(const_in, 16)
            sp.dma_start(rbias[:], io["rb"]).then_inc(const_in, 16)
            with sp.Fori(1, NTILE) as t:
                for half in range(2):
                    sp.wait_ge(x_lo_ready, 2 * t + half - 1)
                    load_x(t, half)
            sp.wait_ge(empty_ready, 1)
            slots = xs_d[0:NSLOT, :].rearrange("(r p) f -> p r f", p=P)
            sp.dma_start(slots[:, :, 0:ID], bc(rows[:, 0, 0:ID], 1, NSLOT // P)).then_inc(empty_out, 16)
            sp.dma_start(slots[:, :, REST:ROW], bc(rows[:, 0, REST:ROW], 1, NSLOT // P)).then_inc(empty_out, 16)
            sp.dma_start(slots[:, :, ID:REST], empties[:]).then_inc(empty_out, 16)

            def load_up(e, q):
                sp.dma_start(w_up[q], io["wexp"][bass.ds(e, 1), :, 0:UP].rearrange("e p n -> (e p) n")).then_inc(MO["up_in"][q], 16)

            def load_down(e):
                sp.dma_start(w_down, io["wexp"][bass.ds(e, 1), :, UP:].rearrange("e p n -> (e p) n")).then_inc(MO["down_in"], 16)

            def load_slots(e, q):
                sp.dma_start(xsH[:, q], xs_d[bass.ds(e * SLOTS, SLOTS), 0:DIM].rearrange("(s p) f -> p s f", p=P)).then_inc(MO["xs_in"][q], 16)

            def load_rest(e, q):
                sp.dma_start(restH[:, q], xs_d[bass.ds(e * SLOTS, SLOTS), DIM:ROW].rearrange("(s p) f -> p s f", p=P)).then_inc(MO["rest_in"][q], 16)

            sp.wait_ge(AT["E"]["v_ps"], NBLK)
            load_up(0, 0)
            load_down(0)
            sp.wait_ge(AT["E"]["h_ready"], NBLK)
            load_up(1, 1)
            sp.wait_ge(MO["scattered"], 16 * NTILE)
            for q in range(2):
                load_slots(q, q)
            for q in range(2):
                load_rest(q, q)
            sp.wait_ge(MO["rest_ready"], 2)
            sp.dma_start(out[0:TOK, :].rearrange("(t p) f -> p t f", p=P), res).then_inc(rest_out, 16)

            def load_next(e, g, q, more=True):
                if more:
                    sp.wait_ge(MO["xt_ps"], e)
                    load_slots(e + 1, 1 - q)
                    sp.wait_ge(MO["up_lo_ready"], e)
                    load_up(e + 1, 1 - q)
                sp.wait_ge(MO["down_lo_ready"], e)
                load_down(e)
                if not isinstance(e, int) or e > 1:
                    sp.wait_ge(MO["ys_out"][q], 48 * g)
                    load_rest(e, q)

            load_next(1, 0, 1)
            with sp.Fori(1, EXPERTS // 2 - 1) as g:
                for q in range(2):
                    load_next(2 * g + q, g, q)
            load_next(EXPERTS - 2, EXPERTS // 2 - 1, 0)
            load_next(EXPERTS - 1, EXPERTS // 2 - 1, 1, more=False)

        @block.gpsimd
        def _(pool):
            pool.dma_start(posb[0:64, :, :], io["pos"][0:NPATCH:2, :].unsqueeze(0).to_broadcast([64, NTILE, DIM])).then_inc(pos_in, 16)
            pool.dma_start(posb[64:128, :, :], io["pos"][1:NPATCH:2, :].unsqueeze(0).to_broadcast([64, NTILE, DIM])).then_inc(pos_in, 16)
            pool.dma_start(brow, io["btok"].to_broadcast([P, DIM])).then_inc(pos_in, 16)
            pool.wait_ge(const_in, 64)
            ch = Chain(pool, gd)

            def rstd_a(i):
                pool.wait_ge(var_ready, i + 1)
                ch.link(nc.gpsimd.tensor_tensor(varA, mvA[:, 1:2], const[:, C_EPS:C_EPS + 1], ALU.add))
                nc.gpsimd.tensor_tensor(rsA, varA, const[:, C_HALF:C_HALF + 1], ALU.pow).then_inc(rstdA_ready, 1)

            pool.wait_ge(pos_in, 48)
            nc.gpsimd.tensor_tensor(posb, posb, bc(brow, 1, NTILE), ALU.add).then_inc(posb_ready, 1)

            pool.wait_ge(wtok_lo_ready, 4)
            pool.dma_start(staged, io["win"].rearrange("p k n -> p (k n)")).then_inc(wff_in, 16)

            def split_low(first, piece):
                pool.wait_ge(wff_hi_ready, first + piece + 1)
                cols = bass.ds((first + piece) * PIECE, PIECE)
                nc.gpsimd.tensor_tensor(wff_lo[:, cols], staged[:, bass.ds(piece * PIECE, PIECE)], wff_hi[:, cols].bitcast(F32),
                                        ALU.subtract).then_inc(wff_lo_ready, 1)

            for half, tiles in enumerate(((0, 1, 2), (7, 8))):
                for i in tiles:
                    rstd_a(i)
                first, last = tiles[-1] + 1, min(tiles[-1] + 5, NTILE)
                with pool.Fori(first, last) as i:
                    ch.turn(i - first, 1)
                    rstd_a(i)
                    split_low(4 * half, i - first)
                ch.end(last - first)
                if half == 0:
                    pool.wait_ge(wff_lo_ready, 4)
                    pool.dma_start(staged, io["wout"].rearrange("p c n -> p (c n)")).then_inc(wff_in, 16)
            split_low(4, 3)
            pool.wait_ge(tok_ps, NTILE)
            for dst, name in ((w1q, "w1q"), (w1o, "w1o")):
                pool.dma_start(dst[:], io[name]).then_inc(w1_in, 16)

            with pool.Fori(0, NBLK) as i:
                for c in range(NCH):
                    pool.wait_ge(FB["hi_ready"], i * NCH + c + 1)
                    nc.gpsimd.tensor_tensor(al[:, c % 4, :], accB[:, c % 4, :], ah[:, c % 4, :].bitcast(F32),
                                            ALU.subtract).then_inc(FB["lo_ready"], 1)
            pool.wait_ge(FB["h_ready"], NBLK)
            for dst, name in ((w2q, "w2q"), (w2o, "w2o"), (wr, "wr")):
                pool.dma_start(dst[:], io[name]).then_inc(w2_in, 16)


            def attention(kind, nk):
                S = AT[kind]
                pairs = 2 if kind == "C" else 5

                def rope(i, p):
                    pool.wait_ge(S["t_ready"], i * pairs + p + 1)
                    for half, (op, a, b) in enumerate(((ALU.subtract, 0, 1), (ALU.add, 2, 3))):
                        if kind == "C":
                            dst = by_batch(rawC[:, 2 * p + half, :])
                        else:
                            dst = by_batch(rawC[:, 2 + half, :]) if p == pairs - 1 else q_of(half, p)
                        ins = nc.gpsimd.tensor_tensor(dst, by_batch(tC[:, p % 2, a, :]), by_batch(tC[:, p % 2, b, :]), op)
                    ins.then_inc(S["qk_pool"], 1)

                def weigh(i, n):
                    pool.wait_ge(S["ri_ready"], 4 * i + n + 1)
                    nc.gpsimd.tensor_tensor(pC[:, n, :, 0:NPATCH], pC[:, n, :, 0:NPATCH], bc(riC[:, n, :], 2, NPATCH),
                                            ALU.mult).then_inc(S["p_ready"], 1)

                def body(i, nxt):
                    for step in order(pairs if nxt else 0):
                        if step[0] == "rope" and nxt:
                            rope(i + 1, step[1])
                        if step[0] == "weigh":
                            weigh(i, step[1])
                    if nk == "E":
                        scale_rms(i - 1)

                def scale_rms(m):
                    if isinstance(m, int) and m < 0:
                        return
                    S = LN["E"]
                    pool.wait_ge(S["ri_ready"], m + 1)
                    ch.link(nc.gpsimd.tensor_tensor(varL, varL, riL, ALU.mult))
                    nc.gpsimd.tensor_tensor(varL, varL, riL, ALU.mult).then_inc(S["ms_ready"], 1)

                if kind == "C":
                    pool.wait_ge(FB["h_ready"], NBLK)
                    nc.gpsimd.memset(kC, 0.0)
                    nc.gpsimd.memset(pC, 0.0)
                else:
                    pool.wait_ge(AT["C"]["h_ready"], NBLK)
                    pool.wait_ge(empty_out, 48)
                nc.gpsimd.memset(vC, 0.0).then_inc(S["zero_ready"], 1)
                for p in range(pairs):
                    rope(0, p)
                    if p == 0 and kind == "E":
                        scale_rms(3)
                body(0, True)
                with pool.Fori(1, NBLK - 1) as i:
                    ch.turn(i - 1, 1 if nk == "E" else 0)
                    body(i, True)
                ch.end(NBLK - 2)
                body(NBLK - 1, False)

            attention("C", "E")
            attention("E", None)
            for part, (first, last) in enumerate(PARTS):
                some = slice(first, last)
                if part == 0:
                    pool.wait_ge(MO["wx_ready"], 1)
                    pool.wait_ge(MO["xf_out"], last // 3)
                    ch.link(nc.gpsimd.tensor_tensor(kept, xf[:, some, :], bc(wx[:, 0, some], 2, DIM), ALU.mult))
                    nc.gpsimd.tensor_tensor(res[:, some, :], res[:, some, :], kept, ALU.add).then_inc(MO["rest_ready"], 1)
                pool.wait_ge(MO["rest_ready"], part + 1)
                pool.wait_ge(MO["slot_ready"], part + 1)
                for t in range(first, last):
                    pool.indirect_dma_start(xs_d, bass.IndirectOffsetOnAxis(ap=slotS[:, t:t + 1], axis=0), rows[:, t, :], None).then_inc(MO["scattered"], 16)
            pool.wait_ge(rest_out, 16)

            def idle_step():
                nc.gpsimd.tensor_tensor(idleP[:], const[:, 0:1], const[:, 0:1], ALU.add).then_inc(idled, 1)

            def split_down(e, q):
                pool.wait_ge(MO["down_hi_ready"], e + 1)
                nc.gpsimd.tensor_tensor(w_parts[q][1][:, UP:], w_down, w_parts[q][0][:, UP:].bitcast(F32),
                                        ALU.subtract).then_inc(MO["down_lo_ready"], 1)

            def store(e, q):
                for s in range(3):
                    pool.wait_ge(MO["ys_ready"], 3 * e + s + 1)
                    pool.wait_ge(idled, 3 * e + s + 1)
                    idle_step()
                    pool.indirect_dma_start(out, bass.IndirectOffsetOnAxis(ap=restH[:, q, s, 0:1].bitcast(I32), axis=0),
                                            ysH[:, q, s, :], None).then_inc(MO["ys_out"][q], 16)

            idle_step()
            with pool.Fori(0, EXPERTS // 2 - 1) as g:
                for q in range(2):
                    split_down(2 * g + q + 1, 1 - q)
                    store(2 * g + q, q)
            split_down(EXPERTS - 1, 1)
            store(EXPERTS - 2, 0)
            store(EXPERTS - 1, 1)
            for q in range(2):
                pool.wait_ge(MO["ys_out"][q], 48 * (EXPERTS // 2))

        @block.vector
        def _(dve):
            v = nc.vector
            ch = Chain(dve, vd)

            def wtok_low(r):
                dve.wait_ge(wtok_hi_ready, r + 1)
                rows4 = slice(4 * r, 4 * r + 4)
                v.tensor_tensor(wtok_lo[:, rows4].rearrange("p r f -> p (r f)"), staged[:, r * 1024:(r + 1) * 1024],
                                wtok_hi[:, rows4].rearrange("p r f -> p (r f)").bitcast(F32), ALU.subtract).then_inc(wtok_lo_ready, 1)

            def xa_low(t, q):
                for half in range(2):
                    cols = slice(half * XT // 2, (half + 1) * XT // 2)
                    dve.wait_ge(x_hi_ready, 2 * t + half + 1)
                    v.tensor_tensor(xlA[:, q, cols], xin[:, half, :], xhA[:, q, cols].bitcast(F32), ALU.subtract).then_inc(x_lo_ready, 1)

            wtok_low(0)
            xa_low(0, 0)
            for r in range(1, 4):
                wtok_low(r)
            xa_low(1, 1)
            dve.wait_ge(const_in, 64)
            ch.link(v.tensor_scalar(negb[:], vecs[:, 0:NCH], -1.0, None, ALU.mult))
            v.tensor_copy(constb[:], constb32).then_inc(constb_ready, 1)
            v.memset(rows[:, 0, :], 0.0)
            ch.link(v.memset(empties[:], 0.0))
            v.tensor_copy(empties[:, :, 0].bitcast(I32), const[:, C_EMPTY:]).then_inc(empty_ready, 1)
            dve.wait_ge(posb_ready, 1)

            def embed(i, q):
                dve.wait_ge(tok_ps, i + 1)
                v.tensor_tensor(hA[:, q, :], ps[:, q, 0:DIM], posb[:, bass.ds(i, 1), :].rearrange("p t f -> p (t f)"),
                                ALU.add).then_inc(hA_ready, 1)
                dve.wait_ge(hA_ready, i + 1)
                ch.link(v.bn_stats(statA, hA[:, q, :]))
                v.memset(idleA, 0.0)
                v.bn_aggr(mvA, statA).then_inc(var_ready, 1)
                dve.wait_ge(rstdA_ready, i + 1)
                v.tensor_scalar(xnA[:, q, :], hA[:, q, :], mvA[:, 0:1], rsA, ALU.subtract, ALU.mult).then_inc(xn_ready, 1)

            def soft_a(i):
                dve.wait_ge(sA_ps, i + 1)
                ch.link(v.scalar_tensor_tensor(smA, ps[:, 3, 0:P], 1.0 / 16, const[:, C_BLOCKMASK:C_BLOCKMASK + P],
                                               ALU.mult, ALU.add))
                v.tensor_reduce(nbA, smA, AX.X, ALU.max, negate=True).then_inc(smA_ready, 1)

            def out_a(i, q):
                dve.wait_ge(pvA_ps, i + 1)
                ch.link(v.reciprocal(rinvA, sumA))
                v.scalar_tensor_tensor(h2A, ps[:, 5, 0:DIM], rinvA, hA[:, q, :], ALU.mult, ALU.add).then_inc(h2_ready, 1)

            embed(0, 0)
            PER_A = 3

            def tile_a(i, q, last=False):
                soft_a(i)
                if not isinstance(i, int) or i < NTILE - 2:
                    xa_low(i + 2, q)
                if not last:
                    embed(i + 1, 1 - q)
                out_a(i, q)

            for i in (0, 1):
                tile_a(i, i)
            with dve.Fori(1, NTILE // 2 - 1) as j:
                ch.turn(j - 1, 2 * PER_A)
                for q in range(2):
                    tile_a(2 * j + q, q)
            ch.end(NTILE // 2 - 2)
            for i in (NTILE - 2, NTILE - 1):
                tile_a(i, i % 2, last=i == NTILE - 1)

            def center(kind, m, bank):
                S, cols = LN[kind], bass.ds(m * BLK, BLK)
                dve.wait_ge(S["mean_ps"], m + 1)
                v.tensor_tensor(dT[:, :, cols], hT[:, :, cols], bc(ps[:, bank, 0:BLK], 1, KC),
                                ALU.subtract).then_inc(S["d_ready"], 1)

            def invert(kind, m):
                dve.wait_ge(LN[kind]["std_ready"], m + 1)
                v.memset(idle[:], 0.0)
                v.reciprocal(rstd[:, bass.ds(m * BLK, BLK)], stdL).then_inc(LN[kind]["done"], 1)

            def standardise(m):
                S, cols = LN["E"], bass.ds(m * BLK, BLK)
                dve.wait_ge(S["std_ready"], m + 1)
                v.reciprocal(riL, stdL).then_inc(S["ri_ready"], 1)
                dve.wait_ge(S["ri_ready"], m + 1)
                v.tensor_tensor(dT[:, :, cols], dT[:, :, cols], bc(riL, 1, KC), ALU.mult)

            def invert_rms(m):
                S = LN["E"]
                dve.wait_ge(S["rms_ready"], m + 1)
                v.memset(idle[:], 0.0)
                v.reciprocal(rstd[:, bass.ds(m * BLK, BLK)], stdL).then_inc(S["done"], 1)

            dve.wait_ge(hT_ready, NTILE)
            def x_full(i):
                cols = bass.ds(i * BLK, BLK)
                dve.wait_ge(LN["B"]["done"], i + 1)
                v.tensor_tensor(xB, dT[:, :, cols], bc(rstd[:, cols], 1, KC), ALU.mult).then_inc(FB["xf_ready"], 1)

            def x_low(i):
                dve.wait_ge(FB["xhi_ready"], i + 1)
                v.tensor_tensor(xl[:], xB, xh[:].bitcast(F32), ALU.subtract).then_inc(FB["x_ready"], 1)

            center("B", 0, 6)
            invert("B", 0)
            x_full(0)
            x_low(0)

            def feed(i):
                cols = bass.ds(i * BLK, BLK)
                static = isinstance(i, int)
                for c in range(NCH):
                    l_ps = ps[:, c % 4, 0:BLK]
                    if c < 8:
                        dve.wait_ge(FB["l_ps"], i * NCH + c + 1)
                    if c == 0:
                        v.tensor_scalar(maskB[:, 0, :], l_ps, negb[:, 0:1], None, ALU.is_gt).then_inc(FB["dec_ready"], 1)
                        dve.wait_ge(FB["v_ps"], i + 1)
                        ch.link(v.tensor_scalar(maskB[:, 1, :], ps[:, 7, 0:BLK], const[:, C_CNT + 1:C_CNT + 2], None,
                                                ALU.is_equal))
                        dve.wait_ge(FB["a_ready"], i * NCH + c + 1)
                        at_least(dve, FB["lo_ready"], i * NCH + c - 3)
                        v.scalar_tensor_tensor(accB[:, 0, :], ps[:, 6, 0:BLK], const[:, C_CNT:C_CNT + 1], actB[:, 0, :],
                                               ALU.is_equal, ALU.mult).then_inc(FB["act_ready"], 1)
                        continue
                    if c < 8:
                        v.scalar_tensor_tensor(maskB[:, 2 * c + 1, :], l_ps, negb[:, c:c + 1], maskB[:, c, :],
                                               ALU.is_gt, ALU.mult).then_inc(FB["dec_ready"], 1)
                        dve.wait_ge(FB["dec_ready"], 8 * i + c + 1)
                        ch.link(v.tensor_tensor(maskB[:, 2 * c, :], maskB[:, c, :], maskB[:, 2 * c + 1, :], ALU.subtract))
                    dve.wait_ge(FB["a_ready"], i * NCH + c + 1)
                    at_least(dve, FB["lo_ready"], i * NCH + c - 3)
                    v.tensor_tensor(accB[:, c % 4, :], actB[:, c % 4, :], maskB[:, c, :], ALU.mult).then_inc(FB["act_ready"], 1)
                    if not static or i < NBLK - 1:
                        if c == 5:
                            center("B", i + 1, 6)
                        if c == 9:
                            invert("B", i + 1)
                        if c == 12:
                            x_full(i + 1)
                    if not static or i > 0:
                        if c == 10:
                            center("C", i - 1, 6)
                        if c == 14:
                            invert("C", i - 1)
                if not static or i < NBLK - 1:
                    x_low(i + 1)
                dve.wait_ge(FB["down_ps"], (i + 1) * NCH)
                v.tensor_tensor(hT[:, :, cols], hT[:, :, cols], ps[:, 4:6, 0:BLK], ALU.add).then_inc(FB["h_ready"], 1)

            feed(0)
            with dve.Fori(1, NBLK - 1) as i:
                ch.turn(i - 1, 8)
                feed(i)
            ch.end(NBLK - 2)
            feed(NBLK - 1)

            def attention(kind, nk):
                S = AT[kind]
                pairs = 2 if kind == "C" else 5
                cos0, sin0 = (C_COS1, C_SIN1) if kind == "C" else (C_COS2, C_SIN2)
                cos = bc(const[:, cos0:cos0 + NPATCH], 1, BB)
                sin = bc(const[:, sin0:sin0 + NPATCH], 1, BB)

                def scaled_x(i):
                    cols = bass.ds(i * BLK, BLK)
                    dve.wait_ge(LN[kind]["done"], i + 1)
                    at_least(dve, S["v_ps"], i)
                    for c in range(KC):
                        dst = xC[:, c, :, 0:NPATCH]
                        if kind == "C":
                            ins = v.tensor_tensor(dst, by_batch(dT[:, c, cols]), by_batch(rstd[:, cols]), ALU.mult)
                        else:
                            ins = v.scalar_tensor_tensor(dst, by_batch(dT[:, c, cols]), vecs[:, 16 + c:17 + c],
                                                         by_batch(rstd[:, cols]), ALU.mult, ALU.mult)
                    ins.then_inc(S["x_ready"], 1)

                def rope(i, p):
                    dve.wait_ge(S["proj_ps"], i * pairs + p + 1)
                    at_least(dve, S["qk_pool"], i * pairs + p - 1)
                    bank = pair_bank(pairs, p)
                    first, second = (by_batch(ps[:, bank + h, 0:BLK]) for h in range(2))
                    for k, (src, tab) in enumerate(((first, cos), (second, sin), (second, cos), (first, sin))):
                        ins = v.tensor_tensor(by_batch(tC[:, p % 2, k, :]), src, tab, ALU.mult)
                    ins.then_inc(S["t_ready"], 1)

                def spread_k(i):
                    dve.wait_ge(S["qk_pool"], (i + 1) * pairs)
                    col = C_AMASK if kind == "C" else C_GMASK
                    for half in range(2):
                        for a in range(4):
                            ins = v.tensor_scalar(k_of(half, a), by_batch(rawC[:, 2 + half, :]), const[:, col + a:col + a + 1],
                                                  None, ALU.mult)
                    ins.then_inc(S["kx_ready"], 1)

                def scores(i, n):
                    dve.wait_ge(S["s_ps"], 4 * i + n + 1)
                    v.transpose(sC[:, n].rearrange("p s k -> p (s k)"), ps[:, 4 + n, :]).then_inc(S["st_ready"], 1)
                    dve.wait_ge(S["st_ready"], 4 * i + n + 1)
                    s_n = sC[:, n, :, 0:NPATCH]
                    ch.link(v.tensor_reduce(mxC[:, n, :], s_n, AX.X, ALU.max))
                    v.tensor_tensor(s_n, s_n, bc(mxC[:, n, :], 2, NPATCH), ALU.subtract).then_inc(S["sub_ready"], 1)

                def total(i, n):
                    dve.wait_ge(S["e_ready"], 4 * i + n + 1)
                    ch.link(v.tensor_reduce(suC[:, n, :], pC[:, n, :, 0:NPATCH], AX.X, ALU.add))
                    v.reciprocal(riC[:, n, :], suC[:, n, :]).then_inc(S["ri_ready"], 1)

                def turn_back(i, n):
                    dve.wait_ge(S["p_ready"], 4 * i + n + 1)
                    v.transpose(sC[:, n].rearrange("p s k -> p (s k)"), pC[:, n].rearrange("p s k -> p (s k)")).then_inc(S["pt_ready"], 1)

                def body(i, nxt):
                    static = isinstance(i, int)
                    cols = bass.ds(i * BLK, BLK)
                    if nxt:
                        scaled_x(i + 1)
                    for n in range(NQ):
                        scores(i, n)
                    more = nk == "E" and (not static or i > 0)
                    if more and nxt:
                        center("E", i - 1, pair_bank(pairs, 1))
                    if kind == "E" and nxt and (not static or i > 0):
                        moe_input(i - 1)
                    for what, n in order(pairs if nxt else 0):
                        if not nxt and (what, n) == ("sum", 2):
                            if kind == "E":
                                moe_input(i - 1)
                            else:
                                center("E", i - 1, pair_bank(pairs, 1))
                        if what == "rope" and nxt:
                            rope(i + 1, n)
                        elif what == "sum":
                            total(i, n)
                        elif what == "turn":
                            turn_back(i, n)
                    if nxt:
                        spread_k(i + 1)
                    if more:
                        standardise(i - 1)
                    if kind == "E" and (not static or i > 0):
                        moe_logits(i - 1)
                    if kind == "E" and not nxt:
                        pick(0)
                        cap(0)
                    dve.wait_ge(S["o_ps"], i + 1)
                    if kind == "C":
                        for c in range(KC):
                            ins = v.scalar_tensor_tensor(hT[:, c, cols], ps[:, c, 0:BLK], vecs[:, 20 + c:21 + c], hT[:, c, cols],
                                                         ALU.add, ALU.add)
                        ins.then_inc(S["h_ready"], 1)
                    else:
                        v.tensor_tensor(dT[:, :, cols], dT[:, :, cols], ps[:, 0:2, 0:BLK], ALU.add).then_inc(S["h_ready"], 1)
                    if more:
                        invert_rms(i - 1)

                if kind == "C":
                    ch.link(v.memset(xC, 0.0))
                scaled_x(0)
                center(kind, 3, pair_bank(pairs, 1))
                rope(0, 0)
                for p in range(1, pairs):
                    if p == 1 and kind == "E":
                        standardise(3)
                    if p == 1 and kind == "C":
                        invert("C", 3)
                    rope(0, p)
                    if p == 2:
                        invert_rms(3)
                dve.wait_ge(S["zero_ready"], 1)
                if kind == "E":
                    v.tensor_scalar(rows[:, :, ID].bitcast(I32), const[:, C_DUMP:C_DUMP + NTILE], float(-NSLOT), None, ALU.add)
                spread_k(0)
                body(0, True)
                with dve.Fori(1, NBLK - 1) as i:
                    ch.turn(i - 1, 8 + (1 if kind == "E" else 0))
                    body(i, True)
                ch.end(NBLK - 2)
                body(NBLK - 1, False)

            def moe_input(m):
                cols = bass.ds(m * BLK, BLK)
                dve.wait_ge(AT["E"]["h_ready"], m + 1)
                v.tensor_tensor(rF, hT[:, :, cols], dT[:, :, cols], ALU.add)
                dve.wait_ge(MO["std_ready"], m + 1)
                ch.link(v.reciprocal(riL, stdL))
                for c in range(KC):
                    ins = v.scalar_tensor_tensor(xfF[:, c, :], dT[:, c, cols], vecs[:, 18 + c:19 + c], riL, ALU.mult, ALU.mult)
                ins.then_inc(MO["xf_ready"], 1)

            def moe_logits(m):
                dve.wait_ge(MO["lg_ps"], m + 1)
                v.tensor_copy(logit[:, bass.ds(3 * m, 3), :], ps[:, 1, DIM:DIM + 24].rearrange("p (t e) -> p t e", e=8)).then_inc(MO["lg_ready"], 1)
                dve.wait_ge(MO["r_ps"], m + 1)
                v.tensor_copy(res[:, bass.ds(3 * m, 2), :], ps[:, 0, :].rearrange("p (t f) -> p t f", f=DIM))
                v.tensor_copy(res[:, bass.ds(3 * m + 2, 1), :], ps[:, 1, 0:DIM].rearrange("p (t f) -> p t f", f=DIM)).then_inc(MO["r_ready"], 1)

            iota = const[:, C_IOTA:C_IOTA + 8]

            def pick(part):
                first, last = PARTS[part]
                some = slice(first, last)
                dve.wait_ge(MO["lg_ready"], last // 3)
                for t in range(first, last):
                    ins = v.max(top8[:, t, :], logit[:, t, :])
                ch.link(ins)
                for t in range(first, last):
                    ins = v.max_index(idx8[:, t, :], top8[:, t, :], logit[:, t, :])
                v.tensor_tensor(pq[:, 1, some], top8[:, some, 1], top8[:, some, 0], ALU.subtract).then_inc(MO["diff_ready"], 1)
                dve.wait_ge(MO["diff_ready"], part + 1)
                ch.link(v.tensor_copy(e12[:, :, some], idx8[:, some, 0:2].rearrange("p t k -> p k t")))
                for k in range(2):
                    ins = v.tensor_tensor(ohB[:, k, some], bc(iota, 1, last - first), bc(e12[:, k, some], 2, 8), ALU.is_equal)
                ins.then_inc(MO["oh_ready"], 1)

            def cap(part):
                first, last = PARTS[part]
                some = slice(first, last)
                iota_t = bc(iota, 1, last - first)
                dve.wait_ge(MO["cum_ps"], part + 1)
                cum = ps[:, 3, 0:192].rearrange("p (k t e) -> p k t e", k=2, t=NTILE)
                ch.link(v.tensor_copy(cumS[:, 0, some], cum[:, 0, some]))
                ch.link(v.tensor_tensor(cumS[:, 1, some], cum[:, 1, some], cumS[:, 0, some], ALU.add))
                ch.link(v.scalar_tensor_tensor(em[:, :, some], cumS[:, :, some], float(CAP), ohB[:, :, some], ALU.is_lt, ALU.mult))
                v.tensor_reduce(tm[:, :, some], em[:, :, some], AX.X, ALU.add)
                ch.link(v.tensor_tensor(t96[:, :, some], em[:, :, some], bc(iota_t, 1, 2), ALU.mult))
                ch.link(v.tensor_reduce(asg[:, :, some], t96[:, :, some], AX.X, ALU.add))
                v.tensor_tensor(actG[:, some], tm[:, 0, some], tm[:, 1, some], ALU.max)
                ch.link(v.tensor_tensor(mG[:, some], asg[:, 0, some], asg[:, 1, some], ALU.max))
                ch.link(v.tensor_tensor(t96[:, 0, some], iota_t, bc(mG[:, some], 2, 8), ALU.is_equal))
                v.tensor_tensor(ohmB[:, some], t96[:, 0, some], bc(actG[:, some], 2, 8), ALU.mult).then_inc(MO["ohm_ready"], 1)

            def place(part):
                first, last = PARTS[part]
                some = slice(first, last)
                dve.wait_ge(MO["ex_ready"], part + 1)
                ch.link(v.tensor_scalar(rankG[:, some], pq[:, 1, some], 1.0, None, ALU.add))
                ch.link(v.reciprocal(pq[:, 0, some], rankG[:, some]))
                ch.link(v.tensor_tensor(pq[:, 1, some], pq[:, 1, some], pq[:, 0, some], ALU.mult))
                ch.link(v.tensor_tensor(wy[:, :, some], tm[:, :, some], pq[:, :, some], ALU.mult))
                ch.link(v.tensor_tensor(wx[:, :, some], pq[:, :, some], wy[:, :, some], ALU.subtract))
                v.tensor_tensor(rows[:, some, WEIGHT], wy[:, 0, some], wy[:, 1, some], ALU.add)
                v.tensor_tensor(wx[:, 0, some], wx[:, 0, some], wx[:, 1, some], ALU.add).then_inc(MO["wx_ready"], 1)
                dump = const[:, C_DUMP + first:C_DUMP + last]
                dve.wait_ge(MO["rank_ps"], part + 1)
                ch.link(v.tensor_tensor(t96[:, 1, some], ps[:, 3, 192:288].rearrange("p (t e) -> p t e", e=8)[:, some], ohmB[:, some], ALU.mult))
                ch.link(v.tensor_reduce(rankG[:, some], t96[:, 1, some], AX.X, ALU.add))
                ch.link(v.scalar_tensor_tensor(slotf[:, 0, some], mG[:, some], float(SLOTS), rankG[:, some], ALU.mult, ALU.add))
                ch.link(v.scalar_tensor_tensor(slotf[:, 1, some], slotf[:, 0, some], -1.0, dump, ALU.add, ALU.subtract))
                ch.link(v.tensor_tensor(slotf[:, 0, some], slotf[:, 1, some], actG[:, some], ALU.mult))
                v.tensor_tensor(slotS[:, some], slotf[:, 0, some], dump, ALU.add).then_inc(MO["slot_ready"], 1)

            attention("C", "E")
            attention("E", None)
            place(0)
            moe_input(3)
            moe_logits(3)
            pick(1)
            cap(1)
            place(1)
            first, last = PARTS[1]
            dve.wait_ge(MO["wx_ready"], 2)
            dve.wait_ge(MO["rest_ready"], 1)
            dve.wait_ge(MO["xf_out"], NBLK)
            dve.wait_ge(MO["r_ready"], NBLK)
            for t in range(first, last):
                ins = v.scalar_tensor_tensor(res[:, t, :], xf[:, t, :], wx[:, 0, t:t + 1], res[:, t, :], ALU.mult, ALU.add)
            ins.then_inc(MO["rest_ready"], 1)

            def split_up(e, q):
                dve.wait_ge(MO["up_hi_ready"], e + 1)
                v.tensor_tensor(w_parts[q][1][:, 0:UP], w_up[q], w_parts[q][0][:, 0:UP].bitcast(F32), ALU.subtract).then_inc(MO["up_lo_ready"], 1)

            def x_low(e):
                dve.wait_ge(MO["xhi_ready"], e + 1)
                low, high = (x[:].rearrange("p c (s t) -> p s c t", t=P) for x in (xtl, xth))
                v.tensor_tensor(low[:, 0:2], ps[:, 0, :].rearrange("p (s c t) -> p s c t", c=KC, t=P), high[:, 0:2].bitcast(F32), ALU.subtract)
                v.tensor_tensor(low[:, 2], ps[:, 1, 0:DIM].rearrange("p (c t) -> p c t", t=P), high[:, 2].bitcast(F32),
                                ALU.subtract).then_inc(MO["xt_ready"], 1)

            def product(e, q, more=True):
                def low(j):
                    dve.wait_ge(MO["g_hi_ready"], e * 4 + j + 1)
                    v.tensor_tensor(gl[:, q, j, :], gelH[:, 0, :], gh[:, q, j, :].bitcast(F32), ALU.subtract).then_inc(MO["g_ready"], 1)

                for j in range(4):
                    dve.wait_ge(MO["a_ready"], e * 4 + j + 1)
                    v.tensor_tensor(prodH[:, j % 2, :], aH[:, j % 2, :], ps[:, 3 + 2 * (j % 2), 0:SLOTS], ALU.mult).then_inc(MO["prod_ready"], 1)
                    if j == 3 and more:
                        x_low(e + 1)
                    if j > 0:
                        low(j - 1)
                    if j == 1 and more:
                        split_up(e + 1, 1 - q)
                low(3)

            def combine(e, g, q):
                dve.wait_ge(MO["rest_in"][q], 16 * g + 16)
                at_least(dve, MO["ys_out"][q], 48 * g)
                for s in range(3):
                    dve.wait_ge(MO["y_ps"], e * 3 + (3 if s else 1))
                    v.scalar_tensor_tensor(ysH[:, q, s, :], y_ps(s), restH[:, q, s, 1:2],
                                           restH[:, q, s, REST - DIM:ROW - DIM], ALU.mult, ALU.add).then_inc(MO["ys_ready"], 1)

            split_up(0, 0)
            dve.wait_ge(MO["down_hi_ready"], 1)
            v.tensor_tensor(w_parts[0][1][:, UP:], w_down, w_parts[0][0][:, UP:].bitcast(F32), ALU.subtract).then_inc(MO["down_lo_ready"], 1)
            x_low(0)
            product(0, 0)
            product(1, 1)
            combine(0, 0, 0)
            product(2, 0)
            combine(1, 0, 1)
            with dve.Fori(1, EXPERTS // 2 - 1) as g:
                for q in range(2):
                    product(2 * g + q + 1, 1 - q)
                    combine(2 * g + q, g, q)
            product(EXPERTS - 1, 1, more=False)
            combine(EXPERTS - 2, EXPERTS // 2 - 1, 0)
            combine(EXPERTS - 1, EXPERTS // 2 - 1, 1)

        @block.scalar
        def _(act):
            a_ = nc.scalar

            def place_h(i):
                act.wait_ge(h2_ps, i + 1)
                dst = hT[:].rearrange("p c (b n) -> p c n b", n=NPATCH)[:, :, bass.ds(2 * i, 2), :]
                a_.activation(dst, ps[:, 6, 0:DIM].rearrange("p (c n b) -> p c n b", c=KC, n=2), ACT.Copy).then_inc(hT_ready, 1)

            def wtok_high(r):
                act.wait_ge(wtok_in[r], 16)
                a_.activation(wtok_hi[:, 4 * r:4 * r + 4].rearrange("p r f -> p (r f)"), staged[:, r * 1024:(r + 1) * 1024],
                              ACT.Copy).then_inc(wtok_hi_ready, 1)

            def xa_high(t, q):
                for half in range(2):
                    act.wait_ge(x_in[half], 16 * t + 16)
                    a_.activation(xhA[:, q, half * XT // 2:(half + 1) * XT // 2], xin[:, half, :], ACT.Copy).then_inc(x_hi_ready, 1)

            def tile_a(i, q, first=False, more=True):
                act.wait_ge(xnT_ps, i + 1)
                a_.activation(xnTA, ps[:, 2, 0:DIM].rearrange("p (c t) -> p c t", c=KC), ACT.Copy).then_inc(xnT_ready, 1)
                if more:
                    xa_high(i + 2, q)
                if not first:
                    place_h(i - 1)
                act.wait_ge(smA_ready, i + 1)
                a_.activation(eA, smA, ACT.Exp, bias=nbA, accum_out=sumA).then_inc(eA_ready, 1)
                act.wait_ge(eA_ps, i + 1)
                a_.activation(etA, ps[:, 4, 0:P], ACT.Copy).then_inc(etA_ready, 1)

            def split_high(first, piece):
                act.wait_ge(wff_in, 4 * first + 16)
                a_.activation(wff_hi[:, bass.ds((first + piece) * PIECE, PIECE)], staged[:, bass.ds(piece * PIECE, PIECE)],
                              ACT.Copy).then_inc(wff_hi_ready, 1)

            def pair_a(j, piece=None, more=True):
                for q in range(2):
                    tile_a(2 * j + q, q, first=isinstance(j, int) and 2 * j + q == 0, more=more)
                    if piece is not None:
                        split_high(*piece(2 * j + q))

            wtok_high(0)
            xa_high(0, 0)
            for r in range(1, 4):
                wtok_high(r)
            xa_high(1, 1)
            pair_a(0)
            with act.Fori(1, 3) as j:
                pair_a(j, lambda i: (0, i - SPLITS[0]))
            pair_a(3)
            for j in (4, 5):
                pair_a(j, lambda i: (4, i - SPLITS[1]), more=j == 4)
            place_h(NTILE - 1)

            def square(kind, m):
                act.wait_ge(LN[kind]["d_ready"], m + 1)
                a_.activation(sqL, dT[:, :, bass.ds(m * BLK, BLK)], ACT.Square).then_inc(LN[kind]["sq_ready"], 1)

            def root(kind, m, bank):
                S = LN[kind]
                act.wait_ge(S["var_ps"], m + 1)
                if kind == "E":
                    a_.activation(varL, ps[:, bank, 0:BLK], ACT.Copy)
                a_.activation(stdL, ps[:, bank, 0:BLK], ACT.Sqrt, bias=LN_EPS).then_inc(S["std_ready"], 1)

            def root_rms(m):
                act.wait_ge(LN["E"]["ms_ready"], m + 1)
                a_.activation(stdL, varL, ACT.Sqrt, bias=RMS_EPS).then_inc(LN["E"]["rms_ready"], 1)

            def x_high(i):
                act.wait_ge(FB["xf_ready"], i + 1)
                a_.activation(xh[:], xB, ACT.Copy).then_inc(FB["xhi_ready"], 1)

            def high(i, c):
                act.wait_ge(FB["act_ready"], i * NCH + c + 1)
                at_least(act, FB["down_ps"], i * NCH + c - 3)
                a_.activation(ah[:, c % 4, :], accB[:, c % 4, :], ACT.Copy).then_inc(FB["hi_ready"], 1)

            square("B", 0)
            root("B", 0, 7)
            x_high(0)

            def feed(i):
                static = isinstance(i, int)
                for c in range(NCH):
                    act.wait_ge(FB["l_ps"], i * NCH + c + 1)
                    if c < 8:
                        act.wait_ge(FB["dec_ready"], 8 * i + c + 1)
                    a_.activation(actB[:, c % 4, :], ps[:, c % 4, 0:BLK], ACT.Silu, bias=vecs[:, c:c + 1]).then_inc(FB["a_ready"], 1)
                    if c > 0:
                        high(i, c - 1)
                    if not static or i < NBLK - 1:
                        if c == 6:
                            square("B", i + 1)
                        if c == 8:
                            root("B", i + 1, 7)
                    if not static or i > 0:
                        if c == 11:
                            square("C", i - 1)
                        if c == 13:
                            root("C", i - 1, 7)
                high(i, NCH - 1)
                if not static or i < NBLK - 1:
                    x_high(i + 1)

            feed(0)
            with act.Fori(1, NBLK - 1) as i:
                feed(i)
            feed(NBLK - 1)

            def attention(kind, nk):
                S = AT[kind]
                pairs = 2 if kind == "C" else 5
                scale = 0.25 if kind == "C" else 0.125

                def values(i):
                    act.wait_ge(S["v_ps"], i + 1)
                    for b in range(4):
                        src = ps[32 * b:32 * b + 32, 2:4, :].rearrange("p k (n f) -> p (k n) f", f=DIM)
                        for h in range(4):
                            dst = vC[32 * h:32 * h + 32].rearrange("p (n b) f -> p n b f", b=4)[:, :, b, :]
                            if kind == "C":
                                ins = a_.activation(dst.rearrange("p n (g a d) -> p n g a d", g=4, a=4)[:, :, :, h, :],
                                                    src.rearrange("p n (g a d) -> p n g a d", g=4, a=4)[:, :, :, h, :], ACT.Copy)
                            else:
                                ins = a_.activation(dst[:, :, 64 * h:64 * h + 64], src[:, :, 64 * h:64 * h + 64], ACT.Copy)
                    ins.then_inc(S["v_ready"], 1)

                def spread_q(i):
                    act.wait_ge(S["qk_pool"], i * pairs + 1)
                    for half in range(2):
                        for g in range(4):
                            ins = a_.activation(q_of(half, g), by_batch(rawC[:, half, :]), ACT.Copy, scale=const[:, C_GMASK + g:C_GMASK + g + 1])
                    ins.then_inc(S["qx_ready"], 1)

                def output(i, np_):
                    for n in range(2):
                        act.wait_ge(S["y_ps"], 4 * i + 2 * np_ + n + 1)
                        t0 = (2 * np_ + n) * 96
                        for hp in range(2):
                            y = ps[:, 4 + 2 * n + hp, 0:BLK].rearrange("p (b g q) -> p b g q", b=4, g=4)
                            if kind == "C":
                                for u in range(2):
                                    half = slice(64 * u, 64 * u + 64)
                                    ins = a_.activation(by_batch(yC[half, hp, 0, t0:t0 + 96]), y[half, :, 2 * hp + u, :], ACT.Copy)
                            else:
                                ins = a_.activation(yC[:, hp, :, t0:t0 + 96].rearrange("p g (b q) -> p b g q", b=4), y, ACT.Copy)
                        ins.then_inc(S["y_ready"], 1)

                def body(i, nxt):
                    static = isinstance(i, int)
                    for n in range(NQ):
                        act.wait_ge(S["sub_ready"], 4 * i + n + 1)
                        a_.activation(pC[:, n, :, 0:NPATCH], sC[:, n, :, 0:NPATCH], ACT.Exp, scale=scale).then_inc(S["e_ready"], 1)
                        if kind == "E" and n == 0 and (not static or i > 0):
                            moe_square(i - 1)
                    if kind == "E" and (not static or i > 0):
                        moe_root(i - 1)
                    if nk == "E" and (not static or i > 0):
                        square("E", i - 1)
                    if nxt and kind == "C":
                        spread_q(i + 1)
                    output(i, 0)
                    if kind == "E" and (not static or i > 0):
                        moe_rows(i - 1)
                    if nk == "E" and (not static or i > 0):
                        root("E", i - 1, 1)
                    output(i, 1)
                    if nk == "E" and (not static or i > 0):
                        root_rms(i - 1)
                    if nxt:
                        values(i + 1)
                    elif kind == "E":
                        exp_route(0)

                square(kind, 3)
                root(kind, 3, pair_bank(pairs, 1) + 1)
                if kind == "E":
                    root_rms(3)
                if kind == "C":
                    spread_q(0)
                act.wait_ge(S["zero_ready"], 1)
                values(0)
                body(0, True)
                with act.Fori(1, NBLK - 1) as i:
                    body(i, True)
                body(NBLK - 1, False)

            def moe_square(m):
                act.wait_ge(AT["E"]["h_ready"], m + 1)
                a_.activation(sqL, dT[:, :, bass.ds(m * BLK, BLK)], ACT.Square).then_inc(MO["sq_ready"], 1)

            def moe_root(m):
                act.wait_ge(MO["ms_ps"], m + 1)
                a_.activation(stdL, ps[:, 2, 0:BLK], ACT.Sqrt, bias=RMS_EPS).then_inc(MO["std_ready"], 1)

            def moe_rows(m):
                act.wait_ge(MO["lg_ps"], m + 1)
                a_.activation(xf[:, bass.ds(3 * m, 2), :], ps[:, 0, :].rearrange("p (t f) -> p t f", f=DIM), ACT.Copy)
                act.wait_ge(MO["lg_ready"], m + 1)
                a_.activation(xf[:, bass.ds(3 * m + 2, 1), :], ps[:, 1, 0:DIM].rearrange("p (t f) -> p t f", f=DIM),
                              ACT.Copy).then_inc(MO["xf_out"], 1)

            def split_up(e, g, q):
                act.wait_ge(MO["up_in"][q], 16 * g + 16)
                a_.activation(w_parts[q][0][:, 0:UP], w_up[q], ACT.Copy).then_inc(MO["up_hi_ready"], 1)

            def split_down(e, q):
                act.wait_ge(MO["down_in"], 16 * e + 16)
                a_.activation(w_parts[q][0][:, UP:], w_down, ACT.Copy).then_inc(MO["down_hi_ready"], 1)

            def exp_route(part):
                some = slice(*PARTS[part])
                act.wait_ge(MO["diff_ready"], part + 1)
                a_.activation(pq[:, 1, some], pq[:, 1, some], ACT.Exp).then_inc(MO["ex_ready"], 1)

            attention("C", "E")
            attention("E", None)
            moe_square(3)
            moe_root(3)
            split_up(0, 0, 0)
            split_down(0, 0)
            moe_rows(3)
            exp_route(1)

            def x_high(e):
                act.wait_ge(MO["xt_ps"], e + 1)
                xt = xth[:].rearrange("p c (s t) -> p s c t", t=P)
                a_.activation(xt[:, 0:2], ps[:, 0, :].rearrange("p (s c t) -> p s c t", c=KC, t=P), ACT.Copy)
                a_.activation(xt[:, 2], ps[:, 1, 0:DIM].rearrange("p (c t) -> p c t", t=P), ACT.Copy).then_inc(MO["xhi_ready"], 1)

            def expert(e, g, q, more=True):
                def gelu(j):
                    act.wait_ge(MO["prod_ready"], e * 4 + j + 1)
                    at_least(act, MO["g_ready"], e * 4 + j)
                    a_.activation(gelH[:, 0, :], prodH[:, j % 2, :], ACT.Gelu)
                    a_.activation(gh[:, q, j, :], prodH[:, j % 2, :], ACT.Gelu).then_inc(MO["g_hi_ready"], 1)

                for j in range(4):
                    act.wait_ge(MO["up_ps"], e * 4 + j + 1)
                    a_.activation(aH[:, j % 2, :], ps[:, 2 + 2 * (j % 2), 0:SLOTS], ACT.Copy).then_inc(MO["a_ready"], 1)
                    if j == 3 and more:
                        x_high(e + 1)
                    if j:
                        gelu(j - 1)
                    if j == 0 and more:
                        split_up(e + 1, g + q, 1 - q)
                    if j == 2 and not (isinstance(e, int) and e == 0):
                        split_down(e, q)
                gelu(3)

            x_high(0)
            expert(0, 0, 0)
            expert(1, 0, 1)
            with act.Fori(1, EXPERTS // 2 - 1) as g:
                for q in range(2):
                    expert(2 * g + q, g, q)
            expert(EXPERTS - 2, EXPERTS // 2 - 1, 0)
            expert(EXPERTS - 1, EXPERTS // 2 - 1, 1, more=False)

        @block.tensor
        def _(pe):
            mm, tr = nc.tensor.matmul, nc.tensor.transpose

            def three(dst, w, x, first, last):
                mm(dst, w[0], x[0], start=first, stop=False)
                mm(dst, w[0], x[1], start=False, stop=False)
                return mm(dst, w[1], x[0], start=False, stop=last)

            def embed(q, first, last):
                parts = [x[:, q, :].rearrange("p (r l) -> p r l", r=STRIDE) for x in (xhA, xlA)]
                for r in range(first, last):
                    at = r // STRIDE * BATCH
                    ins = three(ps[:, q, 0:DIM], [x[:, r % STRIDE, at:at + P] for x in parts],
                                [w[:, r, :] for w in (wtok_hi, wtok_lo)], r == 0, r == PATCH - 1)
                if last == PATCH:
                    ins.then_inc(tok_ps, 1)

            def transpose_h():
                for c in range(KC):
                    ins = tr(ps[:, 6, c * P:(c + 1) * P], h2A[:, c * P:(c + 1) * P], ident)
                ins.then_inc(h2_ps, 1)

            def tile_a(i, q, j=0, first=False, last=False):
                if not last:
                    pe.wait_ge(x_lo_ready, 2 * i + 4)
                    at_least(pe, hA_ready, i)
                    embed(1 - q, 0, 8)
                pe.wait_ge(xn_ready, i + 1)
                for c in range(KC):
                    ins = tr(ps[:, 2, c * P:(c + 1) * P], xnA[:, q, c * P:(c + 1) * P], ident)
                ins.then_inc(xnT_ps, 1)
                if not last:
                    embed(1 - q, 8, 10)
                if not first:
                    pe.wait_ge(h2_ready, i)
                    transpose_h()
                pe.wait_ge(xnT_ready, i + 1)
                for c in range(KC):
                    ins = mm(ps[:, 3, 0:P], xnTA[:, c, :], xnTA[:, c, :], start=c == 0, stop=c == KC - 1)
                ins.then_inc(sA_ps, 1)
                if not last:
                    embed(1 - q, 10, 14)
                pe.wait_ge(eA_ready, i + 1)
                tr(ps[:, 4, 0:P], eA, ident).then_inc(eA_ps, 1)
                if not last:
                    embed(1 - q, 14, 16)
                pe.wait_ge(etA_ready, i + 1)
                mm(ps[:, 5, 0:DIM], etA, xnA[:, q, :], start=True, stop=True).then_inc(pvA_ps, 1)

            for r in range(0, PATCH, 4):
                pe.wait_ge(wtok_lo_ready, r // 4 + 1)
                if r < STRIDE:
                    pe.wait_ge(x_lo_ready, r // 4 + 1)
                embed(0, r, r + 4)
            pe.wait_ge(const_in, 64)
            tile_a(0, 0, j=0, first=True)
            tile_a(1, 1, j=0)
            with pe.Fori(1, NTILE // 2 - 1) as j:
                for q in range(2):
                    tile_a(2 * j + q, q, j=j)
            tile_a(NTILE - 2, 0, j=NTILE // 2 - 1)
            tile_a(NTILE - 1, 1, j=NTILE // 2 - 1, last=True)
            pe.wait_ge(h2_ready, NTILE)
            transpose_h()

            def mean(kind, m, bank):
                for c in range(KC):
                    ins = mm(ps[:, bank, 0:BLK], meanw, hT[:, c, bass.ds(m * BLK, BLK)], start=c == 0, stop=c == KC - 1)
                ins.then_inc(LN[kind]["mean_ps"], 1)

            def variance(kind, m, bank):
                pe.wait_ge(LN[kind]["sq_ready"], m + 1)
                for c in range(KC):
                    ins = mm(ps[:, bank, 0:BLK], meanw, sqL[:, c, :], start=c == 0, stop=c == KC - 1)
                ins.then_inc(LN[kind]["var_ps"], 1)

            pe.wait_ge(constb_ready, 1)
            pe.wait_ge(hT_ready, NTILE)
            mean("B", 0, 6)
            variance("B", 0, 7)
            pe.wait_ge(wff_lo_ready, 8)

            def feed(i):
                static = isinstance(i, int)
                LAG = 4
                pe.wait_ge(FB["x_ready"], i + 1)

                def down(c):
                    pe.wait_ge(FB["lo_ready"], i * NCH + c + 1)
                    for o in range(KC):
                        ins = three(ps[:, 4 + o, 0:BLK], [w[:, c, o * P:(o + 1) * P] for w in wout_parts],
                                    [a[:, c % 4, :] for a in (ah, al)], c == 0, c == NCH - 1)
                    ins.then_inc(FB["down_ps"], 1)

                for c in range(NCH):
                    if c >= 4:
                        pe.wait_ge(FB["act_ready"], i * NCH + c - 3)
                    for k in range(KC):
                        ins = three(ps[:, c % 4, 0:BLK], [w[:, k, c * P:(c + 1) * P] for w in win_parts],
                                    [x[:, k, :] for x in (xh, xl)], k == 0, k == KC - 1)
                    ins.then_inc(FB["l_ps"], 1)
                    if c == 1:
                        pe.wait_ge(FB["dec_ready"], 8 * i + 1)
                        mm(ps[:, 6, 0:BLK], constb[:, B_ANC0:B_ANC0 + P], maskB[:, 0, :], start=True, stop=True)
                        mm(ps[:, 7, 0:BLK], constb[:, B_ANC1:B_ANC1 + P], maskB[:, 0, :], start=True, stop=True).then_inc(FB["v_ps"], 1)
                    if c >= LAG:
                        down(c - LAG)
                    if not static or i < NBLK - 1:
                        if c == 5:
                            mean("B", i + 1, 6)
                        if c == 8:
                            variance("B", i + 1, 7)
                    if not static or i > 0:
                        if c == 10:
                            pe.wait_ge(FB["h_ready"], i)
                            mean("C", i - 1, 6)
                        if c == 13:
                            variance("C", i - 1, 7)
                for c in range(NCH - LAG, NCH):
                    down(c)

            feed(0)
            with pe.Fori(1, NBLK - 1) as i:
                feed(i)
            feed(NBLK - 1)

            def attention(kind, nk):
                S = AT[kind]
                pairs = 2 if kind == "C" else 5
                w, voff = (w1q, 512) if kind == "C" else (w2q, 1280)
                wo, nout = (w1o, 1) if kind == "C" else (w2o, 4)
                pe.wait_ge(w1_in if kind == "C" else w2_in, 32 if kind == "C" else 48)

                def project(i, p):
                    if p == 0:
                        pe.wait_ge(S["x_ready"], i + 1)
                        at_least(pe, S["h_ready"], i - 1)
                    at_least(pe, S["v_ready"], i)
                    at_least(pe, S["t_ready"], i * pairs + p - 1)
                    for half in range(2):
                        col = (2 * p + half) * P
                        for k in range(KC):
                            ins = mm(ps[:, pair_bank(pairs, p) + half, 0:BLK], w[:, k, col:col + P], xC[:, k, :, 0:NPATCH],
                                     start=k == 0, stop=k == KC - 1)
                    ins.then_inc(S["proj_ps"], 1)

                def values(i):
                    pe.wait_ge(S["t_ready"], (i + 1) * pairs - 1)
                    for n in range(NQ):
                        for k in range(KC):
                            ins = mm(ps[:, 2 + n // 2, (n % 2) * DIM:(n % 2 + 1) * DIM], xC[:, k, 4 * n:4 * n + 4, :].rearrange("p b n -> p (b n)"),
                                     w[:, k, voff:voff + DIM], start=k == 0, stop=k == KC - 1)
                    ins.then_inc(S["v_ps"], 1)

                def scores(i):
                    pe.wait_ge(S["kx_ready"], i + 1)
                    if kind == "C":
                        pe.wait_ge(S["qx_ready"], i + 1)
                    for n in range(NQ):
                        mm(ps[:, 4 + n, :], constb[:, B_IDENT:B_IDENT + P], bc(constb[:, B_CAUSAL:B_CAUSAL + 32], 1, 16),
                           start=True, stop=False, skip_group_check=True)
                        for b in range(4 * n, 4 * n + 4):
                            dst = ps[:, 4 + n, (b % 4) * P:(b % 4 + 1) * P].rearrange("p (g q) -> p g q", g=4)[:, :, 0:NPATCH]
                            for half in range(2):
                                ins = mm(dst, kC[:, half, b * P:(b + 1) * P], qC[:, half, b * 96:(b + 1) * 96],
                                         start=False, stop=b % 4 == 3 and half == 1, skip_group_check=True)
                        ins.then_inc(S["s_ps"], 1)

                def output(i, np_):
                    if np_ == 0:
                        pe.wait_ge(S["v_ready"], i + 1)
                        pe.wait_ge(S["st_ready"], 4 * i + 4)
                    for n in range(2):
                        if np_ == 1:
                            pe.wait_ge(S["y_ready"], 4 * i + n + 1)
                        q = 2 * np_ + n
                        pe.wait_ge(S["pt_ready"], 4 * i + q + 1)
                        for hp in range(2):
                            for b in range(4):
                                src = sC[:, q].rearrange("p (b g) q -> p b g q", b=4)[:, b, :, 0:NPATCH]
                                ins = mm(ps[:, 4 + 2 * n + hp, b * 96:(b + 1) * 96], vC[:, 4 * q + b, hp * P:(hp + 1) * P], src,
                                         start=True, stop=True)
                        ins.then_inc(S["y_ps"], 1)

                def body(i, nxt):
                    static = isinstance(i, int)
                    more = nk == "E" and (not static or i > 0)
                    moe = kind == "E" and (not static or i > 0)
                    scores(i)
                    if more or moe:
                        at_least(pe, S["v_ready"], i + 1)
                        pe.wait_ge(S["h_ready"], i)
                    if more:
                        mean("E", i - 1, pair_bank(pairs, 1))
                    if moe:
                        moe_square(i - 1)
                    if nxt:
                        for p in range(pairs):
                            if p == 1 and more:
                                pe.wait_ge(LN["E"]["d_ready"], i)
                            if p == 1 and moe:
                                pe.wait_ge(MO["std_ready"], i)
                            project(i + 1, p)
                        values(i + 1)
                    output(i, 0)
                    if nxt:
                        pe.wait_ge(S["t_ready"], (i + 2) * pairs)
                    if more:
                        at_least(pe, S["h_ready"], i)
                        variance("E", i - 1, 1)
                    if moe:
                        moe_rows(i - 1)
                    output(i, 1)
                    if moe:
                        moe_rest(i - 1)
                    pe.wait_ge(S["y_ready"], 4 * i + 4)
                    for o in range(KC):
                        if more and o == 1:
                            pe.wait_ge(LN["E"]["std_ready"], i)
                        for m in range(2 * nout):
                            ins = mm(ps[:, o, 0:BLK], wo[:, m, o * P:(o + 1) * P], yC[:, m // nout, m % nout, :],
                                     start=m == 0, stop=m == 2 * nout - 1)
                        if o == KC - 1:
                            ins.then_inc(S["o_ps"], 1)
                        if kind == "E" and not nxt:
                            (count_picks if o == 0 else count_kept)(0)

                source = FB if kind == "C" else AT["C"]
                pe.wait_ge(source["h_ready"], NBLK)
                mean(kind, 3, pair_bank(pairs, 1))
                project(0, 0)
                variance(kind, 3, pair_bank(pairs, 1) + 1)
                for p in range(1, pairs):
                    pe.wait_ge(LN[kind]["std_ready"], 4)
                    project(0, p)
                values(0)
                body(0, True)
                with pe.Fori(1, NBLK - 1) as i:
                    body(i, True)
                body(NBLK - 1, False)

            def moe_square(m):
                pe.wait_ge(MO["sq_ready"], m + 1)
                for c in range(KC):
                    ins = mm(ps[:, 2, 0:BLK], meanw, sqL[:, c, :], start=c == 0, stop=c == KC - 1)
                ins.then_inc(MO["ms_ps"], 1)

            def moe_rows(m):
                pe.wait_ge(MO["xf_ready"], m + 1)
                for t in range(3):
                    for c in range(KC):
                        tr(ps[:, t // 2, (t % 2) * DIM + c * P:(t % 2) * DIM + (c + 1) * P], xfF[:, c, t * P:(t + 1) * P], ident)
                for t in range(3):
                    dst = ps[:, 1, DIM + t * 8:DIM + t * 8 + 8]
                    for c in range(KC):
                        mm(dst, xfF[:, c, t * P:(t + 1) * P], wr[:, c, :], start=c == 0, stop=False)
                    ins = mm(dst, const[0:1, C_ONES:C_ONES + P], rbias[:], start=False, stop=True)
                ins.then_inc(MO["lg_ps"], 1)

            def moe_rest(m):
                pe.wait_ge(MO["xf_out"], m + 1)
                for t in range(3):
                    for c in range(KC):
                        ins = tr(ps[:, t // 2, (t % 2) * DIM + c * P:(t % 2) * DIM + (c + 1) * P], rF[:, c, t * P:(t + 1) * P], ident)
                ins.then_inc(MO["r_ps"], 1)
                pe.wait_ge(MO["r_ready"], m + 1)

            def count(dst, pick, part):
                first, last = PARTS[part]
                for k in range(pick.shape[1]):
                    mm(dst[:, k, first:last], constb[:, B_TRI:B_TRI + P], pick[:, k, first:last], start=True, stop=False,
                       skip_group_check=True)
                    for t in range(last - 1):
                        after = max(first, t + 1)
                        ins = mm(dst[:, k, after:last], constb[:, B_ONES:B_ONES + P], bc(pick[:, k, t, :], 1, last - after),
                                 start=False, stop=t == last - 2, skip_group_check=True)
                return ins

            def count_picks(part):
                pe.wait_ge(MO["oh_ready"], part + 1)
                count(ps[:, 3, 0:192].rearrange("p (k t e) -> p k t e", k=2, t=NTILE), ohB, part).then_inc(MO["cum_ps"], 1)

            def count_kept(part):
                pe.wait_ge(MO["ohm_ready"], part + 1)
                count(ps[:, 3, 192:288].rearrange("p (k t e) -> p k t e", k=1, t=NTILE), ohmB.unsqueeze(1), part).then_inc(MO["rank_ps"], 1)

            attention("C", "E")
            attention("E", None)
            moe_square(3)
            moe_rows(3)
            moe_rest(3)
            count_picks(1)
            count_kept(1)

            def turn_x(e, g, q):
                pe.wait_ge(MO["xs_in"][q], 16 * g + 16)
                for s in range(3):
                    for c in range(KC):
                        ins = tr(ps[:, s // 2, (s % 2) * DIM + c * P:(s % 2) * DIM + (c + 1) * P], xsH[:, q, s, c * P:(c + 1) * P], ident)
                ins.then_inc(MO["xt_ps"], 1)

            def up(e, g, q):
                pe.wait_ge(MO["up_lo_ready"], e + 1)
                pe.wait_ge(MO["xt_ready"], e + 1)
                for j in range(4):
                    at_least(pe, MO["prod_ready"], e * 4 + j - 1)
                    for m, w in enumerate((w2e[q], w1e[q])):
                        for k in range(KC):
                            ins = three(ps[:, 2 + 2 * (j % 2) + m, 0:SLOTS], [x[:, k, j * P:(j + 1) * P] for x in w],
                                        [x[:, k, :] for x in (xth, xtl)], k == 0, k == KC - 1)
                    ins.then_inc(MO["up_ps"], 1)

            def down(e, g, q):
                pe.wait_ge(MO["down_lo_ready"], e + 1)
                pe.wait_ge(MO["g_ready"], e * 4 + 4)
                for s in range(3):
                    at_least(pe, MO["ys_ready"], e * 3 if s else e * 3 - 2)
                    for j in range(4):
                        ins = three(y_ps(s), [x[:, q, j, s * P:(s + 1) * P] for x in (gh, gl)],
                                    [x[:, j, :] for x in w3e[q]], j == 0, j == 3)
                    ins.then_inc(MO["y_ps"], 1)

            turn_x(0, 0, 0)
            up(0, 0, 0)
            turn_x(1, 0, 1)

            def pair(g):
                up(2 * g + 1, g, 1)
                turn_x(2 * g + 2, g + 1, 0)
                down(2 * g, g, 0)
                up(2 * g + 2, g + 1, 0)
                turn_x(2 * g + 3, g + 1, 1)
                down(2 * g + 1, g, 1)

            pair(0)
            with pe.Fori(1, EXPERTS // 2 - 1) as g:
                pair(g)
            last = EXPERTS // 2 - 1
            up(EXPERTS - 1, last, 1)
            down(EXPERTS - 2, last, 0)
            down(EXPERTS - 1, last, 1)


def kernel(**inputs):
    import concourse.bacc as bacc
    from concourse.bass_utils import run_bass_kernel_spmd

    arrays = _layout(inputs)
    nc = bacc.Bacc("TRN2", target_bir_lowering=False, num_devices=1)
    io = {n: nc.dram_tensor(f"in_{n}", a.shape, mybir.dt.from_np(a.dtype), kind="ExternalInput").ap() for n, a in arrays.items()}
    out = nc.dram_tensor("out", [OUT_ROWS, DIM], F32, kind="ExternalOutput").ap()
    tower(nc, io, out)
    r = run_bass_kernel_spmd(nc, [{f"in_{n}": a for n, a in arrays.items()}], core_ids=[0])
    return r.results[0]["out"][:TOK].reshape(BATCH, NPATCH, DIM)


def _layout(inputs):
    g = {k: np.asarray(a) for k, a in inputs.items()}
    cols = lambda w: np.ascontiguousarray(w.reshape(-1, P, w.shape[1]).transpose(1, 0, 2))
    c, cb = _constants()
    rows = _ffn_rows()
    pad = lambda a: np.concatenate([a, np.zeros((1,) + a.shape[1:], a.dtype)])
    win = pad(g["L0_ffn_W_in"])[rows]
    wout = pad(np.ascontiguousarray(g["L0_ffn_W_out"].T))[rows]
    bin_ = pad(g["L0_ffn_b_in"])[rows].reshape(NCH, P).T
    two = lambda a: a.reshape(KC, P).T
    vecs = np.ascontiguousarray(np.concatenate([bin_, two(g["L1_ffn_g1"]), two(g["L1_ffn_g2"]), two(g["L1_attn_bproj"])], 1))
    r1 = np.arange(HEADS)[:, None] * HD1 + 2 * np.arange(8)[None, :]
    even, odd = r1.reshape(-1), r1.reshape(-1) + 1
    wqkv = g["L1_attn_Wqkv"].T
    w1q = np.concatenate([wqkv[:, even], wqkv[:, odd], wqkv[:, DIM + even], wqkv[:, DIM + odd], wqkv[:, 2 * DIM:]], 1)
    half = lambda h, s: (np.asarray(h)[:, None] * HD2 + 32 * s + np.arange(32)[None, :]).reshape(-1)
    wq, wk_, wv = g["L1_ffn_wq"], g["L1_ffn_wk"], g["L1_ffn_wv"]
    parts = []
    for q in range(4):
        heads = [4 * q + h for h in range(HKV)]
        parts += [wq[:, half(heads, 0)], wq[:, half(heads, 1)]]
    parts += [wk_[:, half(range(HKV), 0)], wk_[:, half(range(HKV), 1)], wv]
    wo = g["L1_ffn_wo"].reshape(4, 2, 2, HD2, DIM).transpose(1, 0, 2, 3, 4).reshape(8, P, DIM)
    ex = lambda w: w.reshape(EXPERTS, -1, P, w.shape[2]).transpose(0, 2, 1, 3).reshape(EXPERTS, P, -1)
    wexp = np.concatenate([ex(g["L1_ffn_w1"]), ex(g["L1_ffn_w2"]), ex(g["L1_ffn_w3"])], 2)
    xt = g["x"].transpose(2, 1, 0)[:, :8 * (NPATCH + 1)].reshape(IN_DIM, NPATCH + 1, 8, BATCH)
    return {
        "const": c, "constb": cb, "vecs": vecs, "rb": g["L1_ffn_router_b"].reshape(1, EXPERTS),
        "x": np.stack([xt[:, 2 * t:2 * t + 3].transpose(0, 2, 1, 3).reshape(IN_DIM, -1) for t in range(NTILE)]),
        "wtok": cols(g["L0_tok_W"]), "btok": g["L0_tok_b"].reshape(1, DIM),
        "pos": np.ascontiguousarray(g["L0_tok_pos_embed"][0, :NPATCH]),
        "win": cols(np.ascontiguousarray(win.T)), "wout": cols(wout),
        "w1q": cols(w1q), "w1o": cols(np.ascontiguousarray(g["L1_attn_Wproj"].T)),
        "w2q": cols(np.concatenate(parts, 1)), "w2o": np.ascontiguousarray(wo.transpose(1, 0, 2)),
        "wr": cols(g["L1_ffn_router_w"]), "wexp": np.ascontiguousarray(wexp),
    }
```
